# Optimizing a Trainium2 kernel written in Bass

```python
import numpy as np
import jax
import jax.numpy as jnp

def _softmax(x, axis=-1):
    return jax.nn.softmax(x, axis=axis)

def _gelu(x):
    return jax.nn.gelu(x, approximate=True)

def _silu(x):
    return jax.nn.silu(x)

def _sigmoid(x):
    return jax.nn.sigmoid(x)

def _layernorm(x, axis=-1, eps=1e-05):
    m = jnp.mean(x, axis=axis, keepdims=True)
    v = jnp.var(x, axis=axis, keepdims=True)
    return (x - m) / jnp.sqrt(v + eps)

def _scatter_add(tgt, idx, src, axis=0):
    return tgt.at[idx].add(src)

def _segment_sum(src, seg, n):
    return jax.ops.segment_sum(src, seg, n)
kernel_name = 'mk_perceiver_d2_seqx_r8_52611a'

def setup_inputs(seed: int=0):
    np.random.seed(seed)
    _w = jnp.asarray

    def _rec_inputs():
        import jax
        import jax.numpy as jnp
        _rk = jax.random.key(seed)
        x = -0.0002928 + 1 * jax.random.normal(jax.random.fold_in(_rk, 1), (128, 32, 128), jnp.float32)
        _lenS = 32 - jax.random.randint(jax.random.fold_in(_rk, 7), (128,), 0, max(1, 32 // 4) + 1, jnp.int32)
        _lenS2 = 257 - jax.random.randint(jax.random.fold_in(_rk, 8), (128,), 0, max(1, 257 // 4) + 1, jnp.int32)
        _ctx_1024P = jax.random.normal(jax.random.fold_in(_rk, 11), (128, 16, 128), jnp.float32)
        _ctx_1024c = jax.random.dirichlet(jax.random.fold_in(_rk, 511), 0.3 * jnp.ones((16,), jnp.float32), (128, 257))
        _ctx_1024t = jnp.einsum('bsk,bkd->bsd', _ctx_1024c, _ctx_1024P)
        _ctx_1024t = _ctx_1024t * jax.lax.rsqrt(jnp.mean(jnp.square(_ctx_1024t)) + 1e-12) * 0.953939
        ctx_1024 = -1.39393e-06 + 0.999914 * (_ctx_1024t + 0.3 * jax.random.normal(jax.random.fold_in(_rk, 611), (128, 257, 128), jnp.float32))
        _validS = jnp.arange(32)[None, :] < _lenS[:, None]
        _validS2 = jnp.arange(257)[None, :] < _lenS2[:, None]
        _causal = jnp.tril(jnp.ones((32, 32), dtype=bool))
        mask_1x1xSxS2_ik0 = jnp.where(jnp.broadcast_to(_validS2[0:1, None, None, :], (1, 1, 32, 257)), 0, 1).astype(jnp.int32)
        return (x, ctx_1024, mask_1x1xSxS2_ik0)
    x, ctx_1024, mask_1x1xSxS2_ik0 = _rec_inputs()

    def _L0_xattn_setup():
        import jax, jax.numpy as jnp
        import numpy as np
        D_MODEL = 128
        NUM_HEADS = 16
        HEAD_DIM = D_MODEL // NUM_HEADS
        B, S = (2, 256)
        key = jax.random.key(seed)
        ks = jax.random.split(key, 12)
        s = 0.02
        inp = {'Q': jax.random.normal(ks[0], (B, S, D_MODEL), jnp.float32), 'K': jax.random.normal(ks[1], (B, S, D_MODEL), jnp.float32), 'V': jax.random.normal(ks[2], (B, S, D_MODEL), jnp.float32), 'mask': jnp.tril(jnp.ones((S, S), jnp.int32))[None, None, :, :], 'Wq': jax.random.normal(ks[3], (D_MODEL, D_MODEL), jnp.float32) * s, 'bq': jnp.zeros((D_MODEL,), jnp.float32), 'Wk': jax.random.normal(ks[4], (D_MODEL, D_MODEL), jnp.float32) * s, 'bk': jnp.zeros((D_MODEL,), jnp.float32), 'Wv': jax.random.normal(ks[5], (D_MODEL, D_MODEL), jnp.float32) * s, 'bv': jnp.zeros((D_MODEL,), jnp.float32), 'Wo': jax.random.normal(ks[6], (D_MODEL, D_MODEL), jnp.float32) * s, 'bo': jnp.zeros((D_MODEL,), jnp.float32)}
        return inp
    _L0_xattn_all = _L0_xattn_setup()
    _L0_xattn_in = {k: v for k, v in _L0_xattn_all.items() if k in ('Wq', 'bq', 'Wk', 'bk', 'Wv', 'bv', 'Wo', 'bo')}
    del _L0_xattn_all

    def _L0_attn_setup():
        import jax, jax.numpy as jnp
        import numpy as np
        B, N, E = (4, 256, 128)
        H = 8
        D1 = 3 * E
        DH = D1 // H
        R = 64
        GAMMA = 0.99
        EPS = 1e-08

        def _srms(x):
            rms = jnp.linalg.norm(x, axis=-1, keepdims=True) * x.shape[-1] ** (-0.5)
            return x / (rms + EPS)
        key = jax.random.key(seed)
        ks = jax.random.split(key, 20)

        def lin(k, din, dout):
            kw, kb = jax.random.split(k)
            w = jax.random.normal(kw, (din, dout), jnp.float32) * din ** (-0.5)
            b = jax.random.normal(kb, (dout,), jnp.float32) * 0.02
            return (w, b)
        x = jax.random.normal(ks[0], (B, N, E), jnp.float32)
        u_w, u_b = lin(ks[1], E, D1)
        v_w, v_b = lin(ks[2], E, D1)
        o_w, o_b = lin(ks[3], D1, E)
        pos_w, pos_b = lin(ks[4], 1, R)
        lw0, lb0 = lin(ks[5], R, R)
        lw1, lb1 = lin(ks[6], R, R)
        lw2, lb2 = lin(ks[7], R, R)
        out_w, out_b = lin(ks[8], R, H * DH)
        return dict(x=x, u_w=u_w, u_b=u_b, v_w=v_w, v_b=v_b, o_w=o_w, o_b=o_b, pos_w=pos_w, pos_b=pos_b, lw0=lw0, lb0=lb0, lw1=lw1, lb1=lb1, lw2=lw2, lb2=lb2, out_w=out_w, out_b=out_b)
    _L0_attn_all = _L0_attn_setup()
    _L0_attn_in = {k: v for k, v in _L0_attn_all.items() if k in ('u_w', 'u_b', 'v_w', 'v_b', 'o_w', 'o_b', 'pos_w', 'pos_b', 'lw0', 'lb0', 'lw1', 'lb1', 'lw2', 'lb2', 'out_w', 'out_b')}
    del _L0_attn_all

    def _L0_ffn_setup():
        import jax, jax.numpy as jnp
        import numpy as np
        H = 128
        I = 64
        E = 8
        TOP_K = 2
        N_SHARED = 2
        SHARED_I = I * N_SHARED
        SCALE = 2.5
        NORM_TOPK = True
        B, S = (2, 128)

        def _swiglu(x, wg, wu, wd):
            g = x @ wg.T
            u = x @ wu.T
            return jax.nn.silu(g) * u @ wd.T
        key = jax.random.key(seed)
        ks = jax.random.split(key, 8)
        std = 0.02
        return {'hidden_states': jax.random.normal(ks[0], (B, S, H), jnp.float32), 'gate_weight': jax.random.normal(ks[1], (E, H), jnp.float32) * std, 'w_gate': jax.random.normal(ks[2], (E, I, H), jnp.float32) * std, 'w_up': jax.random.normal(ks[3], (E, I, H), jnp.float32) * std, 'w_down': jax.random.normal(ks[4], (E, H, I), jnp.float32) * std, 'ws_gate': jax.random.normal(ks[5], (SHARED_I, H), jnp.float32) * std, 'ws_up': jax.random.normal(ks[6], (SHARED_I, H), jnp.float32) * std, 'ws_down': jax.random.normal(ks[7], (H, SHARED_I), jnp.float32) * std}
    _L0_ffn_all = _L0_ffn_setup()
    _L0_ffn_in = {k: v for k, v in _L0_ffn_all.items() if k in ('gate_weight', 'w_gate', 'w_up', 'w_down', 'ws_gate', 'ws_up', 'ws_down')}
    del _L0_ffn_all

    def _L1_xattn_setup():
        import jax, jax.numpy as jnp
        import numpy as np
        B, LQ, LKV, D = (8, 256, 256, 128)
        key = jax.random.key(seed)
        k1, k2, k3, k4, k5, k6, k7 = jax.random.split(key, 7)
        s = 1.0 / np.sqrt(D)
        return {'query': jax.random.normal(k1, (B, LQ, D), jnp.float32), 'key': jax.random.normal(k2, (B, LKV, D), jnp.float32), 'value': jax.random.normal(k3, (B, LKV, D), jnp.float32), 'Wq': jax.random.uniform(k4, (D, D), jnp.float32, -s, s), 'bq': jax.random.uniform(k5, (D,), jnp.float32, -s, s), 'Wk': jax.random.uniform(k6, (D, D), jnp.float32, -s, s), 'bk': jax.random.uniform(k7, (D,), jnp.float32, -s, s), 'scale_factor': 32, 'dropout_p': 0}
    _L1_xattn_all = _L1_xattn_setup()
    _L1_xattn_in = {k: v for k, v in _L1_xattn_all.items() if k in ('Wq', 'bq', 'Wk', 'bk')}
    del _L1_xattn_all

    def _L1_attn_setup():
        import jax, jax.numpy as jnp
        import numpy as np
        D_MODEL, D_STATE, D_CONV, EXPAND = (128, 16, 4, 2)
        D_INNER = EXPAND * D_MODEL
        B_SZ, L_SEQ = (2, 256)
        LN_EPS = 1e-05

        def _selective_scan(u, dt, A, Bp, Cp):

            def step(h, inp):
                dt_t, B_t, C_t, u_t = inp
                dA = jnp.exp(jnp.clip(dt_t[:, :, None] * A, -20.0, 0.0))
                dB_u = jnp.clip(dt_t[:, :, None] * B_t[:, None, :] * u_t[:, :, None], -10.0, 10.0)
                h = jnp.clip(h * dA + dB_u, -100.0, 100.0)
                y = jnp.einsum('bdn,bn->bd', h, C_t)
                return (h, y)
            h0 = jnp.zeros((u.shape[0], u.shape[2], A.shape[0]), dtype=u.dtype)
            xs = (jnp.swapaxes(dt, 0, 1), jnp.swapaxes(Bp, 0, 1), jnp.swapaxes(Cp, 0, 1), jnp.swapaxes(u, 0, 1))
            _, ys = jax.lax.scan(step, h0, xs)
            return jnp.swapaxes(ys, 0, 1)
        key = jax.random.key(seed)
        ks = jax.random.split(key, 8)
        x = jax.random.normal(ks[0], (B_SZ, L_SEQ, D_MODEL), dtype=jnp.float32)
        W_in = jax.random.normal(ks[1], (2 * D_INNER, D_MODEL), dtype=jnp.float32) * (1.0 / np.sqrt(D_MODEL))
        conv_w = jax.random.normal(ks[2], (D_INNER, 1, D_CONV), dtype=jnp.float32) * (1.0 / np.sqrt(D_CONV))
        conv_b = jax.random.normal(ks[3], (D_INNER,), dtype=jnp.float32) * 0.01
        W_x = jax.random.normal(ks[4], (2 * D_STATE + 1, D_INNER), dtype=jnp.float32) * (1.0 / np.sqrt(D_INNER))
        W_dt = jax.random.uniform(ks[5], (D_INNER, 1), dtype=jnp.float32, minval=-0.01, maxval=0.01)
        b_dt = jnp.full((D_INNER,), 0.1, dtype=jnp.float32)
        A_log = jnp.log(jnp.arange(1, D_STATE + 1, dtype=jnp.float32) * 0.1)
        D_param = jnp.ones((D_INNER,), dtype=jnp.float32)
        W_out = jax.random.normal(ks[6], (D_MODEL, D_INNER), dtype=jnp.float32) * (1.0 / np.sqrt(D_INNER))
        ln_g = jnp.ones((D_INNER,), dtype=jnp.float32)
        ln_b = jnp.zeros((D_INNER,), dtype=jnp.float32)
        return {'x': x, 'W_in': W_in, 'conv_w': conv_w, 'conv_b': conv_b, 'W_x': W_x, 'W_dt': W_dt, 'b_dt': b_dt, 'A_log': A_log, 'D_param': D_param, 'W_out': W_out, 'ln_g': ln_g, 'ln_b': ln_b}
    _L1_attn_all = _L1_attn_setup()
    _L1_attn_in = {k: v for k, v in _L1_attn_all.items() if k in ('W_in', 'conv_w', 'conv_b', 'W_x', 'W_dt', 'b_dt', 'A_log', 'D_param', 'W_out', 'ln_g', 'ln_b')}
    del _L1_attn_all

    def _L1_ffn_setup():
        import jax, jax.numpy as jnp
        import numpy as np
        TAU = 1.0
        K_ROUTE = 3
        EPS = 1e-08

        def _route_combine_weights(x_addr, U, k, tau):
            z = x_addr @ U.T
            topv, topi = jax.lax.top_k(z, k)
            w = jax.nn.softmax(topv / (tau + EPS), axis=1)
            N, L = z.shape
            rows = jnp.arange(N)[:, None]
            return jnp.zeros((N, L), z.dtype).at[rows, topi].add(w)

        def _mixture(inp, C, W):
            L = W.shape[0]
            y = jnp.zeros((inp.shape[0], W.shape[1]), inp.dtype)
            for e in range(L):
                y = y + C[:, e:e + 1] * (inp @ W[e].T)
            return y
        key = jax.random.key(seed)
        ks = jax.random.split(key, 8)
        B, T, D_in, H, D_out, L, d_addr = (8, 1024, 128, 128, 128, 12, 64)

        def unit_rows(k, L_, d_):
            U = jax.random.normal(k, (L_, d_), dtype=jnp.float32)
            U = U - U.mean(axis=1, keepdims=True)
            return U / (jnp.linalg.norm(U, axis=1, keepdims=True) + EPS)

        def norm_tape(k, shape):
            W = jax.random.normal(k, shape, dtype=jnp.float32)
            n = jnp.sqrt(jnp.sum(W * W, axis=tuple(range(1, W.ndim)), keepdims=True)) + 1e-12
            return W / n
        x = jax.random.normal(ks[0], (B, T, D_in), dtype=jnp.float32)
        P_w = jax.random.normal(ks[1], (d_addr, D_in), dtype=jnp.float32) / np.sqrt(D_in)
        U1 = unit_rows(ks[2], L, d_addr)
        U2 = unit_rows(ks[3], L, d_addr)
        U3 = unit_rows(ks[4], L, d_addr)
        W1 = norm_tape(ks[5], (L, H, D_in))
        W2 = norm_tape(ks[6], (L, D_out, H))
        b2 = norm_tape(ks[7], (L, D_out))
        return {'x': x, 'P_w': P_w, 'U1': U1, 'U2': U2, 'U3': U3, 'W1': W1, 'W2': W2, 'b2': b2}
    _L1_ffn_all = _L1_ffn_setup()
    _L1_ffn_in = {k: v for k, v in _L1_ffn_all.items() if k in ('P_w', 'U1', 'U2', 'U3', 'W1', 'W2', 'b2')}
    del _L1_ffn_all
    return {'x': x, 'ctx_1024': ctx_1024, 'mask_1x1xSxS2_ik0': mask_1x1xSxS2_ik0, 'L0_xattn_Wq': _L0_xattn_in['Wq'], 'L0_xattn_bq': _L0_xattn_in['bq'], 'L0_xattn_Wk': _L0_xattn_in['Wk'], 'L0_xattn_bk': _L0_xattn_in['bk'], 'L0_xattn_Wv': _L0_xattn_in['Wv'], 'L0_xattn_bv': _L0_xattn_in['bv'], 'L0_xattn_Wo': _L0_xattn_in['Wo'], 'L0_xattn_bo': _L0_xattn_in['bo'], 'L0_attn_u_w': _L0_attn_in['u_w'], 'L0_attn_u_b': _L0_attn_in['u_b'], 'L0_attn_v_w': _L0_attn_in['v_w'], 'L0_attn_v_b': _L0_attn_in['v_b'], 'L0_attn_o_w': _L0_attn_in['o_w'], 'L0_attn_o_b': _L0_attn_in['o_b'], 'L0_attn_pos_w': _L0_attn_in['pos_w'], 'L0_attn_pos_b': _L0_attn_in['pos_b'], 'L0_attn_lw0': _L0_attn_in['lw0'], 'L0_attn_lb0': _L0_attn_in['lb0'], 'L0_attn_lw1': _L0_attn_in['lw1'], 'L0_attn_lb1': _L0_attn_in['lb1'], 'L0_attn_lw2': _L0_attn_in['lw2'], 'L0_attn_lb2': _L0_attn_in['lb2'], 'L0_attn_out_w': _L0_attn_in['out_w'], 'L0_attn_out_b': _L0_attn_in['out_b'], 'L0_ffn_gate_weight': _L0_ffn_in['gate_weight'], 'L0_ffn_w_gate': _L0_ffn_in['w_gate'], 'L0_ffn_w_up': _L0_ffn_in['w_up'], 'L0_ffn_w_down': _L0_ffn_in['w_down'], 'L0_ffn_ws_gate': _L0_ffn_in['ws_gate'], 'L0_ffn_ws_up': _L0_ffn_in['ws_up'], 'L0_ffn_ws_down': _L0_ffn_in['ws_down'], 'L1_xattn_Wq': _L1_xattn_in['Wq'], 'L1_xattn_bq': _L1_xattn_in['bq'], 'L1_xattn_Wk': _L1_xattn_in['Wk'], 'L1_xattn_bk': _L1_xattn_in['bk'], 'L1_attn_W_in': _L1_attn_in['W_in'], 'L1_attn_conv_w': _L1_attn_in['conv_w'], 'L1_attn_conv_b': _L1_attn_in['conv_b'], 'L1_attn_W_x': _L1_attn_in['W_x'], 'L1_attn_W_dt': _L1_attn_in['W_dt'], 'L1_attn_b_dt': _L1_attn_in['b_dt'], 'L1_attn_A_log': _L1_attn_in['A_log'], 'L1_attn_D_param': _L1_attn_in['D_param'], 'L1_attn_W_out': _L1_attn_in['W_out'], 'L1_attn_ln_g': _L1_attn_in['ln_g'], 'L1_attn_ln_b': _L1_attn_in['ln_b'], 'L1_ffn_P_w': _L1_ffn_in['P_w'], 'L1_ffn_U1': _L1_ffn_in['U1'], 'L1_ffn_U2': _L1_ffn_in['U2'], 'L1_ffn_U3': _L1_ffn_in['U3'], 'L1_ffn_W1': _L1_ffn_in['W1'], 'L1_ffn_W2': _L1_ffn_in['W2'], 'L1_ffn_b2': _L1_ffn_in['b2']}

def reference(x, ctx_1024, mask_1x1xSxS2_ik0, L0_xattn_Wq, L0_xattn_bq, L0_xattn_Wk, L0_xattn_bk, L0_xattn_Wv, L0_xattn_bv, L0_xattn_Wo, L0_xattn_bo, L0_attn_u_w, L0_attn_u_b, L0_attn_v_w, L0_attn_v_b, L0_attn_o_w, L0_attn_o_b, L0_attn_pos_w, L0_attn_pos_b, L0_attn_lw0, L0_attn_lb0, L0_attn_lw1, L0_attn_lb1, L0_attn_lw2, L0_attn_lb2, L0_attn_out_w, L0_attn_out_b, L0_ffn_gate_weight, L0_ffn_w_gate, L0_ffn_w_up, L0_ffn_w_down, L0_ffn_ws_gate, L0_ffn_ws_up, L0_ffn_ws_down, L1_xattn_Wq, L1_xattn_bq, L1_xattn_Wk, L1_xattn_bk, L1_attn_W_in, L1_attn_conv_w, L1_attn_conv_b, L1_attn_W_x, L1_attn_W_dt, L1_attn_b_dt, L1_attn_A_log, L1_attn_D_param, L1_attn_W_out, L1_attn_ln_g, L1_attn_ln_b, L1_ffn_P_w, L1_ffn_U1, L1_ffn_U2, L1_ffn_U3, L1_ffn_W1, L1_ffn_W2, L1_ffn_b2):
    import jax
    import jax.numpy as jnp

    def _L0_xattn_ref(Q, K, V, mask, Wq, bq, Wk, bk, Wv, bv, Wo, bo):
        import jax, jax.numpy as jnp
        import numpy as np
        D_MODEL = 128
        NUM_HEADS = 16
        HEAD_DIM = D_MODEL // NUM_HEADS
        B, S = (2, 256)
        b, sq, _ = Q.shape
        sk = K.shape[1]
        q = Q @ Wq.T + bq
        k = K @ Wk.T + bk
        v = V @ Wv.T + bv
        q = q.reshape(b, sq, NUM_HEADS, HEAD_DIM).transpose(0, 2, 1, 3)
        k = k.reshape(b, sk, NUM_HEADS, HEAD_DIM).transpose(0, 2, 1, 3)
        v = v.reshape(b, sk, NUM_HEADS, HEAD_DIM).transpose(0, 2, 1, 3)
        scores = jnp.einsum('bhqd,bhkd->bhqk', q, k) / jnp.sqrt(jnp.asarray(HEAD_DIM, q.dtype))
        scores = jnp.where(mask == 0, jnp.asarray(-jnp.inf, scores.dtype), scores)
        attn = jax.nn.softmax(scores, axis=-1)
        out = jnp.einsum('bhqk,bhkd->bhqd', attn, v)
        out = out.transpose(0, 2, 1, 3).reshape(b, sq, D_MODEL)
        return out @ Wo.T + bo

    def _L0_attn_ref(x, u_w, u_b, v_w, v_b, o_w, o_b, pos_w, pos_b, lw0, lb0, lw1, lb1, lw2, lb2, out_w, out_b):
        import jax, jax.numpy as jnp
        import numpy as np
        B, N, E = (4, 256, 128)
        H = 8
        D1 = 3 * E
        DH = D1 // H
        R = 64
        GAMMA = 0.99
        EPS = 1e-08

        def _srms(x):
            rms = jnp.linalg.norm(x, axis=-1, keepdims=True) * x.shape[-1] ** (-0.5)
            return x / (rms + EPS)
        b, n, _ = x.shape
        u = jax.nn.silu(x @ u_w + u_b)
        v = jax.nn.silu(x @ v_w + v_b)
        v = v.reshape(b, n, H, DH).transpose(0, 2, 1, 3)
        pos_idx = jnp.arange(n, dtype=x.dtype)[:, None]
        h_ = pos_idx @ pos_w + pos_b
        for w, bb in ((lw0, lb0), (lw1, lb1), (lw2, lb2)):
            h_ = jax.nn.relu(_srms(h_)) @ w + bb
        coefs = jax.nn.relu(_srms(h_)) @ out_w + out_b
        coefs = coefs.reshape(n, H, DH).transpose(1, 0, 2)
        zero = coefs[:, :1]
        pos = coefs[:, 1:]
        decay = GAMMA ** jnp.arange(1, n, dtype=x.dtype)[None, :, None]
        pos = pos * decay
        a = jnp.concatenate([zero, pos, zero], axis=1)
        m = 2 * n
        av = jnp.fft.rfft(a, m, axis=1)
        xv = jnp.fft.rfft(v, m, axis=2)
        tv = jnp.fft.irfft(av[None] * xv, m, axis=2)[:, :, :n, :]
        out = tv.transpose(0, 2, 1, 3).reshape(b, n, H * DH)
        out = u * out
        return out @ o_w + o_b

    def _L0_ffn_ref(hidden_states, gate_weight, w_gate, w_up, w_down, ws_gate, ws_up, ws_down):
        import jax, jax.numpy as jnp
        import numpy as np
        H = 128
        I = 64
        E = 8
        TOP_K = 2
        N_SHARED = 2
        SHARED_I = I * N_SHARED
        SCALE = 2.5
        NORM_TOPK = True
        B, S = (2, 128)

        def _swiglu(x, wg, wu, wd):
            g = x @ wg.T
            u = x @ wu.T
            return jax.nn.silu(g) * u @ wd.T
        b, s, h = hidden_states.shape
        x = hidden_states.reshape(-1, h)
        shared_out = _swiglu(x, ws_gate, ws_up, ws_down)
        logits = x.astype(jnp.float32) @ gate_weight.astype(jnp.float32).T
        scores = jax.nn.sigmoid(logits)
        topk_w, topk_idx = jax.lax.top_k(scores, TOP_K)
        if TOP_K > 1 and NORM_TOPK:
            topk_w = topk_w / (topk_w.sum(-1, keepdims=True) + 1e-20)
        topk_w = topk_w * SCALE
        onehot = jax.nn.one_hot(topk_idx, E, dtype=topk_w.dtype)
        combine = jnp.einsum('tk,tke->te', topk_w, onehot)
        g = jnp.einsum('th,eih->tei', x, w_gate)
        u = jnp.einsum('th,eih->tei', x, w_up)
        hmid = jax.nn.silu(g) * u
        y = jnp.einsum('tei,ehi->teh', hmid, w_down)
        routed_out = jnp.einsum('te,teh->th', combine, y)
        out = (routed_out + shared_out).reshape(b, s, h)
        return out

    def _L1_xattn_ref(query, key, value, Wq, bq, Wk, bk, scale_factor, dropout_p):
        import jax, jax.numpy as jnp
        import numpy as np
        B, LQ, LKV, D = (8, 256, 256, 128)
        q = jnp.einsum('bld,ed->ble', query, Wq) + bq
        k = jnp.einsum('bld,ed->ble', key, Wk) + bk
        scores = jnp.einsum('bqd,bkd->bqk', q, k) / jnp.float32(scale_factor)
        attn = jax.nn.softmax(scores, axis=-1)
        return jnp.einsum('bqk,bkd->bqd', attn, value)

    def _L1_attn_ref(x, W_in, conv_w, conv_b, W_x, W_dt, b_dt, A_log, D_param, W_out, ln_g, ln_b):
        import jax, jax.numpy as jnp
        import numpy as np
        D_MODEL, D_STATE, D_CONV, EXPAND = (128, 16, 4, 2)
        D_INNER = EXPAND * D_MODEL
        B_SZ, L_SEQ = (2, 256)
        LN_EPS = 1e-05

        def _selective_scan(u, dt, A, Bp, Cp):

            def step(h, inp):
                dt_t, B_t, C_t, u_t = inp
                dA = jnp.exp(jnp.clip(dt_t[:, :, None] * A, -20.0, 0.0))
                dB_u = jnp.clip(dt_t[:, :, None] * B_t[:, None, :] * u_t[:, :, None], -10.0, 10.0)
                h = jnp.clip(h * dA + dB_u, -100.0, 100.0)
                y = jnp.einsum('bdn,bn->bd', h, C_t)
                return (h, y)
            h0 = jnp.zeros((u.shape[0], u.shape[2], A.shape[0]), dtype=u.dtype)
            xs = (jnp.swapaxes(dt, 0, 1), jnp.swapaxes(Bp, 0, 1), jnp.swapaxes(Cp, 0, 1), jnp.swapaxes(u, 0, 1))
            _, ys = jax.lax.scan(step, h0, xs)
            return jnp.swapaxes(ys, 0, 1)
        B, L, _ = x.shape
        d_state = A_log.shape[0]
        d_inner = D_param.shape[0]
        xz = jnp.einsum('bld,ed->ble', x, W_in)
        xc, z = (xz[..., :d_inner], xz[..., d_inner:])
        xt = jnp.swapaxes(xc, 1, 2)
        conv = jax.lax.conv_general_dilated(xt, conv_w, window_strides=(1,), padding=[(conv_w.shape[-1] - 1, 0)], feature_group_count=d_inner, dimension_numbers=('NCH', 'OIH', 'NCH'))
        conv = conv + conv_b[None, :, None]
        u = jax.nn.silu(jnp.swapaxes(conv, 1, 2))
        x_dbl = jnp.einsum('bld,ed->ble', u, W_x)
        dt_raw = x_dbl[..., :1]
        Bp = x_dbl[..., 1:1 + d_state]
        Cp = x_dbl[..., 1 + d_state:]
        dt = jnp.clip(jax.nn.softplus(jnp.einsum('blo,eo->ble', dt_raw, W_dt) + b_dt), 0.0001, 10.0)
        A = -jnp.exp(jnp.minimum(A_log, 5.0))
        y = _selective_scan(u, dt, A, Bp, Cp)
        mu = jnp.mean(y, axis=-1, keepdims=True)
        var = jnp.mean(jnp.square(y - mu), axis=-1, keepdims=True)
        yn = (y - mu) * jax.lax.rsqrt(var + LN_EPS) * ln_g + ln_b
        y = yn + D_param * u
        y = y * jax.nn.silu(z)
        return jnp.einsum('ble,de->bld', y, W_out)

    def _L1_ffn_ref(x, P_w, U1, U2, U3, W1, W2, b2):
        import jax, jax.numpy as jnp
        import numpy as np
        TAU = 1.0
        K_ROUTE = 3
        EPS = 1e-08

        def _route_combine_weights(x_addr, U, k, tau):
            z = x_addr @ U.T
            topv, topi = jax.lax.top_k(z, k)
            w = jax.nn.softmax(topv / (tau + EPS), axis=1)
            N, L = z.shape
            rows = jnp.arange(N)[:, None]
            return jnp.zeros((N, L), z.dtype).at[rows, topi].add(w)

        def _mixture(inp, C, W):
            L = W.shape[0]
            y = jnp.zeros((inp.shape[0], W.shape[1]), inp.dtype)
            for e in range(L):
                y = y + C[:, e:e + 1] * (inp @ W[e].T)
            return y
        B, T, D = x.shape
        xf = x.reshape(B * T, D)
        xa = xf @ P_w.T
        C1 = _route_combine_weights(xa, U1, K_ROUTE, TAU)
        C2 = _route_combine_weights(xa, U2, K_ROUTE, TAU)
        C3 = _route_combine_weights(xa, U3, K_ROUTE, TAU)
        h = jax.nn.gelu(_mixture(xf, C1, W1), approximate=False)
        y = _mixture(h, C2, W2) + C3 @ b2
        return y.reshape(B, T, -1)
    x = x + _L0_xattn_ref(_layernorm(x, axis=-1), ctx_1024, ctx_1024, mask_1x1xSxS2_ik0, L0_xattn_Wq, L0_xattn_bq, L0_xattn_Wk, L0_xattn_bk, L0_xattn_Wv, L0_xattn_bv, L0_xattn_Wo, L0_xattn_bo)
    x = x + _L0_attn_ref(_layernorm(x, axis=-1), L0_attn_u_w, L0_attn_u_b, L0_attn_v_w, L0_attn_v_b, L0_attn_o_w, L0_attn_o_b, L0_attn_pos_w, L0_attn_pos_b, L0_attn_lw0, L0_attn_lb0, L0_attn_lw1, L0_attn_lb1, L0_attn_lw2, L0_attn_lb2, L0_attn_out_w, L0_attn_out_b)
    x = x + _L0_ffn_ref(_layernorm(x, axis=-1), L0_ffn_gate_weight, L0_ffn_w_gate, L0_ffn_w_up, L0_ffn_w_down, L0_ffn_ws_gate, L0_ffn_ws_up, L0_ffn_ws_down)
    x = x + _L1_xattn_ref(_layernorm(x, axis=-1), ctx_1024, ctx_1024, L1_xattn_Wq, L1_xattn_bq, L1_xattn_Wk, L1_xattn_bk, 32, 0)
    x = x + _L1_attn_ref(_layernorm(x, axis=-1), L1_attn_W_in, L1_attn_conv_w, L1_attn_conv_b, L1_attn_W_x, L1_attn_W_dt, L1_attn_b_dt, L1_attn_A_log, L1_attn_D_param, L1_attn_W_out, L1_attn_ln_g, L1_attn_ln_b)
    x = x + _L1_ffn_ref(_layernorm(x, axis=-1), L1_ffn_P_w, L1_ffn_U1, L1_ffn_U2, L1_ffn_U3, L1_ffn_W1, L1_ffn_W2, L1_ffn_b2)
    return x

_drawn_inputs = setup_inputs


def setup_inputs(seed=0):
    import zlib

    import numpy as np

    out = dict(_drawn_inputs(seed))
    spreads = {'L0_xattn_bq': (0.0, 0.8),
     'L0_xattn_bk': (0.0, 2.0),
     'L0_xattn_bv': (0.0, 0.1),
     'L0_xattn_bo': (0.0, 0.1),
     'L1_attn_b_dt': (0.10000000149011612, 0.6),
     'L1_attn_D_param': (1.0, 0.6),
     'L1_attn_ln_g': (1.0, 0.6),
     'L1_attn_ln_b': (0.0, 0.897)}
    factors = {'L0_xattn_Wq': 8.0,
     'L0_xattn_Wk': 8.0,
     'L0_attn_u_b': 3.196,
     'L0_attn_o_b': 3.241,
     'L0_attn_lb1': 2.76,
     'L0_ffn_gate_weight': 8.0,
     'L0_ffn_w_gate': 8.0,
     'L0_ffn_w_up': 8.0,
     'L0_ffn_w_down': 8.0,
     'L0_ffn_ws_gate': 8.0,
     'L0_ffn_ws_up': 8.0,
     'L0_ffn_ws_down': 8.0,
     'L1_xattn_Wq': 3.291,
     'L1_xattn_bq': 36.365,
     'L1_xattn_Wk': 3.565,
     'L1_xattn_bk': 200.0,
     'L1_attn_conv_b': 25.555,
     'L1_attn_W_dt': 193.419,
     'L1_ffn_U1': 8.0,
     'L1_ffn_U2': 8.0,
     'L1_ffn_W1': 8.0,
     'L1_ffn_W2': 8.0,
     'L1_ffn_U3': 7.65,
     'L1_ffn_b2': 6.915}
    for name, (base, spread) in spreads.items():
        noise = np.random.default_rng([zlib.crc32(name.encode()), seed]).standard_normal(out[name].shape)
        drawn = base * np.exp(spread * noise) if base else spread * noise
        out[name] = jnp.asarray(drawn.astype(out[name].dtype))
    for name, factor in factors.items():
        out[name] = (out[name] * factor).astype(out[name].dtype)
    return out
```

```python
import numpy as np
from contextlib import ExitStack

import concourse.bass as bass
import concourse.mybir as mybir

F32 = mybir.dt.float32
BF16 = mybir.dt.bfloat16
I32 = mybir.dt.int32
ALU = mybir.AluOpType
ACT = mybir.ActivationFunctionType
AX = mybir.AxisListType

P = 128
NB, S, D = 128, 32, 128
S2 = 257
BT = P // S
T = NB // BT
BANK = 512
EPS = 1e-5

XH, XD = 16, 8
CH = 4
UN = 2 * BT
MASKED = -3.0e38


class Ctx:
    pass


def sem_maker(nc, g, prefix):
    def sem(name):
        g.sems.append(nc.alloc_semaphore(f"{prefix}_{name}"))
        return g.sems[-1]
    return sem


def clear_semaphores(nc, g):
    nc.clear_and_free_semaphores(g.sems)
    nc.all_engine_barrier()
    g.sems = []


def tensor_makers(nc, ctx, prefix):
    def sb(name, shape, dt=F32):
        return ctx.enter_context(nc.sbuf_tensor(f"{prefix}_{name}", shape, dt))

    def ps(name, shape, dt=F32):
        return ctx.enter_context(nc.psum_tensor(f"{prefix}_{name}", shape, dt))
    return sb, ps


def stage_load(nc, g):
    with ExitStack() as ctx:
        sem = sem_maker(nc, g, "ld")
        x_in, stats_done = sem("x_in"), sem("stats_done")
        block = ctx.enter_context(nc.Block())

        @block.sync
        def _(sp):
            sp.dma_start(g.x[:, :, :], g.dram["x"].rearrange("(t b) s d -> (b s) t d", b=BT)).then_inc(x_in, 16)
            sp.dma_start(g.ident[:, :], g.dram["c_ident"]).then_inc(x_in, 16)
            sp.wait_ge(x_in, 32)

        @block.vector
        def _(dve):
            dve.wait_ge(x_in, 32)
            with dve.Fori(0, T) as t:
                nc.vector.bn_stats(g.bn[:, t, :], g.x[:, t, :]).then_inc(stats_done, 1)
            dve.wait_ge(stats_done, T)


def norm_coefficients(nc, g, act, dve, step, w, width=D):
    if act is not None:
        act.wait_ge(step, 6)
        nc.scalar.activation(w[:, 1, :], w[:, 0, :], ACT.Sqrt).then_inc(step, 1)
        return
    m0, v0, m1, v1 = (g.bn[:, :, k] for k in (1, 2, 4, 5))
    nc.vector.tensor_tensor(w[:, 0, :], m0, m1, ALU.subtract).then_inc(step, 1)
    nc.vector.tensor_tensor(w[:, 1, :], v0, v1, ALU.add).then_inc(step, 1)
    nc.vector.tensor_tensor(w[:, 2, :], m0, m1, ALU.add).then_inc(step, 1)
    dve.wait_ge(step, 3)
    nc.vector.scalar_tensor_tensor(w[:, 3, :], w[:, 0, :], 0.25, w[:, 0, :], ALU.mult, ALU.mult).then_inc(step, 1)
    nc.vector.tensor_scalar(w[:, 1, :], w[:, 1, :], 1.0 / width, EPS, ALU.mult, ALU.add).then_inc(step, 1)
    dve.wait_ge(step, 5)
    nc.vector.tensor_tensor(w[:, 0, :], w[:, 1, :], w[:, 3, :], ALU.add).then_inc(step, 1)
    dve.wait_ge(step, 7)
    nc.vector.reciprocal(g.rstd[:, :], w[:, 1, :]).then_inc(step, 1)
    dve.wait_ge(step, 8)
    nc.vector.scalar_tensor_tensor(g.shift[:, :], w[:, 2, :], -0.5, g.rstd[:, :], ALU.mult, ALU.mult).then_inc(step, 1)
    dve.wait_ge(step, 9)


def stage_cross0(nc, g):
    scale = 1.0 / float(np.sqrt(XD))
    with ExitStack() as ctx:
        sem = sem_maker(nc, g, "x0")
        sb, ps = tensor_makers(nc, ctx, "x0")
        w_qkv = sb("w_qkv", [P, 3, D])
        w_o = sb("w_o", [P, D])
        w_om = sb("w_om", [P, CH, D])
        cols = sb("cols", [P, 3])
        bo_row = sb("bo_row", [1, D])
        out_bias = sb("out_bias", [1, D])
        ones = sb("ones", [1, P])
        one_col = sb("one_col", [P, 1])
        headmask = sb("headmask", [P, CH])
        headmask_s = sb("headmask_s", [P, CH])
        tailmask = sb("tailmask", [BT * CH, 2, CH])
        onehot = sb("onehot", [P, P], BF16)
        mask_i = sb("mask_i", [P, S2], I32)
        mask_b = sb("mask_b", [P, S2], BF16)
        ctx_t = [sb(f"ctx_t{p}", [P, BT * S2]) for p in range(2)]
        xn = sb("xn", [P, D])
        xnT = sb("xnT", [P, P])
        qT = sb("qT", [P, P])
        qblk = [sb(f"qblk{p}", [P, BT * P]) for p in range(2)]
        kT = [sb(f"kT{p}", [P, BT * S2]) for p in range(2)]
        v = [sb(f"v{p}", [P, BT * 2 * D]) for p in range(2)]
        v_tail = [sb(f"v_tail{p}", [BT * CH, D]) for p in range(2)]
        neg_max = [sb(f"neg_max{p}", [P, BT * CH]) for p in range(2)]
        sums = [sb(f"sums{p}", [P, BT * CH]) for p in range(2)]
        probs = [sb(f"probs{p}", [P, BT * CH, S2]) for p in range(2)]
        rsum = sb("rsum", [P, BT * CH])
        pT = [sb(f"pT{p}", [P, BANK]) for p in range(2)]
        p_tail = sb("p_tail", [BT * CH, BT, P])
        o_raw = sb("o_raw", [P, BANK])
        o_norm = sb("o_norm", [P, CH, BT, S])
        ctx_last = sb("ctx_last", [P, BT, CH])
        rsum_b = sb("rsum_b", [P, BT * CH, S])
        lnw = sb("lnw", [P, 4, T])

        s_ps = [ps(f"s_ps{p}", [P, 2, BANK]) for p in range(2)]
        pT_ps = [ps(f"pT_ps{p}", [P, BANK]) for p in range(2)]
        o_ps = ps("o_ps", [P, BANK])
        m_ps = ps("m_ps", [P, BANK])

        w_in, mask_in = sem("w_in"), sem("mask_in")
        ctx_in = [sem(f"ctx_in{p}") for p in range(2)]
        one_ready = sem("one_ready")
        prep_dve, prep_pe, ln_step = sem("prep_dve"), sem("prep_pe"), sem("ln_step")
        xn_ready, xnT_psum, xnT_sb = sem("xn_ready"), sem("xnT_psum"), sem("xnT_sb")
        qT_psum, q_sb, qblk_sb = sem("qT_psum"), sem("q_sb"), sem("qblk_sb")
        k_psum, k_sb = sem("k_psum"), sem("k_sb")
        tails_psum, tails_sb = sem("tails_psum"), sem("tails_sb")
        v_psum, v_sb = sem("v_psum"), sem("v_sb")
        scores_psum, max_sb, exp_sb = sem("scores_psum"), sem("max_sb"), sem("exp_sb")
        pT_psum, pT_sb, av_done = sem("pT_psum"), sem("pT_sb"), sem("av_done")
        ptail_psum, ptail_sb = sem("ptail_psum"), sem("ptail_sb")
        rsum_sb, r_psum = sem("rsum_sb"), sem("r_psum")
        ctx_last_sb, rsum_b_sb = sem("ctx_last_sb"), sem("rsum_b_sb")
        o_done, o_sb, on_sb = sem("o_done"), sem("o_sb"), sem("on_sb")
        out_psum, x_sb, stats_sb = sem("out_psum"), sem("x_sb"), sem("stats_sb")
        block = ctx.enter_context(nc.Block())

        @block.sync
        def _(sp):
            for n, name in enumerate(("Wq", "Wk", "Wv")):
                sp.dma_start(w_qkv[:, n, :], g.dram[f"L0_xattn_{name}_T"]).then_inc(w_in, 16)
            sp.dma_start(w_o[:, :], g.dram["L0_xattn_Wo_T"]).then_inc(w_in, 16)
            for n, name in enumerate(("bq", "bk", "bv")):
                sp.dma_start(cols[:, n:n + 1], g.dram[f"L0_xattn_{name}"].rearrange("(p a) -> p a", a=1)).then_inc(w_in, 16)
            sp.dma_start(bo_row[:, :], g.dram["L0_xattn_bo"].rearrange("(a n) -> a n", a=1)).then_inc(w_in, 16)
            sp.dma_start(headmask[:, :], g.dram["c_headmask"]).then_inc(w_in, 16)
            sp.dma_start(tailmask[:, :, :], g.dram["c_tailmask"]).then_inc(w_in, 16)
            sp.dma_start(onehot[:, :], g.dram["c_onehot"]).then_inc(w_in, 16)
            for c in range(CH):
                sp.dma_start(mask_i[S * c:S * c + S, :], g.dram["mask"]).then_inc(mask_in, 16)

            def load(t, p):
                sp.dma_start(ctx_t[p][:, :].rearrange("d (b k) -> d b k", b=BT),
                             g.dram["ctxT"][bass.ds(t * BT, BT)].rearrange("b d k -> d b k")).then_inc(ctx_in[p], 16)

            load(0, 0)
            load(1, 1)
            with sp.Fori(0, T // 2 - 1) as i:
                for p in range(2):
                    sp.wait_ge(v_psum, i * 4 + 2 * p + 2)
                    load(i * 2 + (2 + p), p)

        @block.gpsimd
        def _(pool):
            def one(a, b):
                return one_col[:, :].unsqueeze(2).to_broadcast([P, a, b])

            def last_rows(t, p):
                pool.wait_ge(ctx_in[p], (t - p) * 8 + 16)
                if not (isinstance(t, int) and t == 0):
                    pool.wait_ge(tails_psum, t)
                rows = ctx_t[p][:, :].rearrange("d (b k) -> d b k", b=BT)[:, :, S2 - 1:S2]
                nc.gpsimd.tensor_tensor(ctx_last[:, :, :], rows.to_broadcast([P, BT, CH]), one(BT, CH), ALU.mult).then_inc(ctx_last_sb, 1)

            def spread_sums(t):
                pool.wait_ge(rsum_sb, t + 1)
                nc.gpsimd.tensor_tensor(rsum_b[:, :, :], rsum[:, :].unsqueeze(2).to_broadcast([P, BT * CH, S]),
                                        one(BT * CH, S), ALU.mult)\
                  .then_inc(rsum_b_sb, 1)

            nc.gpsimd.memset(one_col[:, :], 1.0).then_inc(one_ready, 1)
            pool.wait_ge(one_ready, 1)
            last_rows(0, 0)
            last_rows(1, 1)
            with pool.Fori(0, T // 2 - 1) as i:
                for p in range(2):
                    spread_sums(i * 2 + p)
                    last_rows(i * 2 + (p + 2), p)
            spread_sums(T - 2)
            spread_sums(T - 1)

        @block.tensor
        def _(pe):
            mm, tr = nc.tensor.matmul, nc.tensor.transpose

            def fill_xnT(t):
                pe.wait_ge(xn_ready, t + 1)
                tr(m_ps[:, 0:P], xn[:, :], g.ident[:, :]).then_inc(xnT_psum, 1)

            def fill_qT(t):
                pe.wait_ge(xnT_sb, t + 1)
                mm(m_ps[:, P:2 * P], w_qkv[:, 0, :], xnT[:, :], start=True, stop=True).then_inc(qT_psum, 1)

            def fill_k(t, p, n):
                if n == 0:
                    pe.wait_ge(ctx_in[p], (t - p) * 8 + 16)
                else:
                    pe.wait_ge(k_sb, t * 2 + n)
                mm(m_ps[:, :], w_qkv[:, 1, :], ctx_t[p][:, n * BANK:(n + 1) * BANK], start=True, stop=True).then_inc(k_psum, 1)

            def fill_tails(t, p):
                pe.wait_ge(k_sb, t * 2 + 2)
                mm(m_ps[:, 0:BT], w_qkv[:, 1, :], ctx_t[p][:, 2 * BANK:BT * S2], start=True, stop=True)
                pe.wait_ge(ctx_last_sb, t + 1)
                mm(m_ps[0:BT * CH, P:2 * P], ctx_last[:, :, :], w_qkv[:, 2, :], start=True, stop=True).then_inc(tails_psum, 1)

            def fill_v(t, p, n):
                if n == 0:
                    pe.wait_ge(tails_sb, t * 2 + 2)
                else:
                    pe.wait_ge(v_sb, t * 2 + 1)
                for j in range(4):
                    b, k = 2 * n + j // 2, j % 2
                    ins = mm(m_ps[:, j * D:(j + 1) * D], ctx_t[p][:, b * S2 + k * P:b * S2 + k * P + P],
                             w_qkv[:, 2, :], start=True, stop=True)
                ins.then_inc(v_psum, 1)

            def scores(t, p, u):
                if u == 0:
                    pe.wait_ge(qblk_sb, t + 1)
                    pe.wait_ge(v_sb, t * 2 + 2)
                b = u // 2
                for j in range(2):
                    c = 2 * (u % 2) + j
                    r = slice(S * c, S * c + S)
                    mm(s_ps[u % 2][:, j, 0:S2], qblk[p][r, b * P:(b + 1) * P], kT[p][r, b * S2:(b + 1) * S2],
                       start=True, stop=False)
                for j in range(2):
                    c = 2 * (u % 2) + j
                    r = slice(S * c, S * c + S)
                    ins = mm(s_ps[u % 2][:, j, 0:S2], onehot[r, :], mask_b[r, :], start=False, stop=True)
                ins.then_inc(scores_psum, 1)

            def turn(t, p, u):
                pe.wait_ge(exp_sb, t * UN + u + 1)
                if not (isinstance(t, int) and t == 0 and u < 2):
                    pe.wait_ge(pT_sb, t * UN + u - 1)
                for j in range(2):
                    for k in range(2):
                        n = 2 * j + k
                        ins = tr(pT_ps[u % 2][:, n * P:(n + 1) * P], probs[p][:, 2 * u + j, k * P:(k + 1) * P],
                                 g.ident[:, :])
                ins.then_inc(pT_psum, 1)

            def attend(t, p, u):
                pe.wait_ge(pT_sb, t * UN + u + 1)
                b = u // 2
                if u == 0 and not (isinstance(t, int) and t == 0):
                    pe.wait_ge(o_sb, t)
                for k in range(2):
                    for j in range(2):
                        c = 2 * (u % 2) + j
                        q = slice(S * c, S * c + S)
                        n = 2 * j + k
                        ins = mm(o_ps[q, b * P:(b + 1) * P], v[p][:, (2 * b + k) * D + S * c:(2 * b + k) * D + S * c + S],
                                 pT[u % 2][:, n * P:(n + 1) * P], start=(b == 0 and k == 0), stop=False,
                                 skip_group_check=True)
                ins.then_inc(av_done, 1)

            def attend_tail(t, p):
                pe.wait_ge(ptail_sb, t + 1)
                mm(o_ps[:, :], v_tail[p][:, :], p_tail[:, :, :], start=False, stop=True,
                   skip_group_check=True).then_inc(o_done, 1)

            def fill_ptail(p):
                tr(m_ps[0:BT * CH, P:2 * P], probs[p][:, :, S2 - 1], g.ident[:, :]).then_inc(ptail_psum, 1)

            def fill_r(t):
                pe.wait_ge(rsum_b_sb, t + 1)
                for b in range(BT):
                    ins = tr(m_ps[:, b * P:(b + 1) * P], rsum_b[:, b * CH:(b + 1) * CH, :], g.ident[:, :])
                ins.then_inc(r_psum, 1)

            def fill_out(t):
                pe.wait_ge(on_sb, t + 1)
                for h in range(CH):
                    mm(m_ps[:, 0:D], o_norm[:, h, :, :], w_om[:, h, :], start=(h == 0), stop=False)
                mm(m_ps[:, 0:D], ones[:, :], out_bias[:, :], start=False, stop=True).then_inc(out_psum, 1)

            def tile(t, p, prev, nxt):
                for u in range(UN):
                    scores(t, p, u)
                    if u == 0 and prev:
                        turn(t - 1, 1 - p, UN - 1)
                        attend(t - 1, 1 - p, UN - 2)
                    if u == 1 and prev:
                        turn(t, p, 0)
                        attend(t - 1, 1 - p, UN - 1)
                    elif u >= 1:
                        turn(t, p, u - 1)
                    if u >= 2:
                        attend(t, p, u - 2)
                    if u == 0:
                        if nxt:
                            fill_xnT(t + 1)
                        if prev:
                            fill_ptail(1 - p)
                    if u == 1 and prev:
                        if nxt:
                            pe.wait_ge(xnT_sb, t + 2)
                        pe.wait_ge(ptail_sb, t)
                        fill_r(t - 1)
                        attend_tail(t - 1, 1 - p)
                    if u == 3:
                        if prev:
                            fill_out(t - 1)
                        if nxt:
                            fill_qT(t + 1)
                    if u == 4 and nxt:
                        if prev:
                            pe.wait_ge(x_sb, t)
                        pe.wait_ge(q_sb, t + 2)
                        fill_k(t + 1, 1 - p, 0)
                    if u == 5 and nxt:
                        fill_k(t + 1, 1 - p, 1)
                    if u == 6 and nxt:
                        fill_tails(t + 1, 1 - p)
                        fill_v(t + 1, 1 - p, 0)
                    if u == 7 and nxt:
                        fill_v(t + 1, 1 - p, 1)

            pe.wait_ge(prep_dve, 4)
            mm(m_ps[0:1, 0:D], cols[:, 2:3], w_o[:, :], start=True, stop=True).then_inc(prep_pe, 1)
            pe.wait_ge(prep_dve, 5)
            fill_xnT(0)
            fill_qT(0)
            pe.wait_ge(q_sb, 1)
            fill_k(0, 0, 0)
            fill_k(0, 0, 1)
            fill_tails(0, 0)
            fill_v(0, 0, 0)
            fill_v(0, 0, 1)
            tile(0, 0, False, True)
            with pe.Fori(0, T // 2 - 1) as i:
                tile(i * 2 + 1, 1, True, True)
                tile(i * 2 + 2, 0, True, True)
            tile(T - 1, 1, True, False)
            turn(T - 1, 1, UN - 1)
            attend(T - 1, 1, UN - 2)
            attend(T - 1, 1, UN - 1)
            pe.wait_ge(x_sb, T - 1)
            fill_ptail(1)
            pe.wait_ge(ptail_sb, T)
            fill_r(T - 1)
            attend_tail(T - 1, 1)
            fill_out(T - 1)

        @block.scalar
        def _(act):
            def copy_k(t, p, n):
                act.wait_ge(k_psum, t * 2 + n + 1)
                nc.scalar.activation(kT[p][:, n * BANK:(n + 1) * BANK], m_ps[:, :], ACT.Identity,
                                     bias=cols[:, 1:2]).then_inc(k_sb, 1)

            def copy_v(t, p, n):
                act.wait_ge(v_psum, t * 2 + n + 1)
                nc.scalar.activation(v[p][:, n * BANK:(n + 1) * BANK], m_ps[:, :], ACT.Copy).then_inc(v_sb, 1)

            def exps(t, p, u):
                act.wait_ge(max_sb, t * UN + u + 1)
                for j in range(2):
                    n = 2 * u + j
                    ins = nc.scalar.activation(probs[p][:, n, :], s_ps[u % 2][:, j, 0:S2], ACT.Exp,
                                               bias=neg_max[p][:, n:n + 1], accum_out=sums[p][:, n:n + 1])
                ins.then_inc(exp_sb, 1)

            def copy_o(t):
                act.wait_ge(o_done, t + 1)
                nc.scalar.activation(o_raw[:, :], o_ps[:, :], ACT.Copy).then_inc(o_sb, 1)

            def tile(t, p, prev, nxt):
                for u in range(UN):
                    exps(t, p, u)
                    if u == 1 and prev:
                        copy_o(t - 1)
                    if u in (4, 5) and nxt:
                        copy_k(t + 1, 1 - p, u - 4)
                    if u in (6, 7) and nxt:
                        copy_v(t + 1, 1 - p, u - 6)

            norm_coefficients(nc, g, act, None, ln_step, lnw)
            act.wait_ge(w_in, 16 * 11)
            copy_k(0, 0, 0)
            copy_k(0, 0, 1)
            copy_v(0, 0, 0)
            copy_v(0, 0, 1)
            tile(0, 0, False, True)
            with act.Fori(0, T // 2 - 1) as i:
                tile(i * 2 + 1, 1, True, True)
                tile(i * 2 + 2, 0, True, True)
            tile(T - 1, 1, True, False)
            copy_o(T - 1)

        @block.vector
        def _(dve):
            vec = nc.vector

            def norm(t):
                vec.tensor_scalar(xn[:, :], g.x[:, t, :], g.rstd[:, bass.ds(t, 1)], g.shift[:, bass.ds(t, 1)],
                                  ALU.mult, ALU.add).then_inc(xn_ready, 1)

            def copy_xnT(t):
                dve.wait_ge(xnT_psum, t + 1)
                vec.tensor_copy(xnT[:, :], m_ps[:, 0:P]).then_inc(xnT_sb, 1)

            def copy_q(t, p):
                dve.wait_ge(qT_psum, t + 1)
                vec.tensor_scalar(qT[:, :], m_ps[:, P:2 * P], cols[:, 0:1], None, ALU.add).then_inc(q_sb, 1)
                dve.wait_ge(q_sb, t + 1)
                vec.tensor_tensor(qblk[p][:, :].rearrange("p (b h s) -> p b h s", b=BT, h=CH),
                                  qT[:, :].rearrange("p (b s) -> p b s", b=BT).unsqueeze(2).to_broadcast([P, BT, CH, S]),
                                  headmask_s[:, :].unsqueeze(1).unsqueeze(3).to_broadcast([P, BT, CH, S]),
                                  ALU.mult).then_inc(qblk_sb, 1)

            def copy_tails(t, p):
                dve.wait_ge(tails_psum, t + 1)
                vec.tensor_scalar(kT[p][:, 2 * BANK:BT * S2], m_ps[:, 0:BT], cols[:, 1:2], None, ALU.add).then_inc(tails_sb, 1)
                vec.tensor_tensor(v_tail[p][:, :].rearrange("r (c e) -> r c e", c=CH),
                                  m_ps[0:BT * CH, P:2 * P].rearrange("r (c e) -> r c e", c=CH),
                                  tailmask[:, 1, :].unsqueeze(2).to_broadcast([BT * CH, CH, S]),
                                  ALU.mult).then_inc(tails_sb, 1)

            def maxes(t, p, u):
                dve.wait_ge(scores_psum, t * UN + u + 1)
                vec.tensor_reduce(neg_max[p][:, 2 * u:2 * u + 2], s_ps[u % 2][:, :, 0:S2], AX.X, ALU.max,
                                  negate=True).then_inc(max_sb, 1)

            def copy_pT(t, u):
                dve.wait_ge(pT_psum, t * UN + u + 1)
                if not (isinstance(t, int) and t == 0 and u < 2):
                    dve.wait_ge(av_done, t * UN + u - 1)
                vec.tensor_copy(pT[u % 2][:, :], pT_ps[u % 2][:, :]).then_inc(pT_sb, 1)

            def copy_ptail(t):
                dve.wait_ge(ptail_psum, t + 1)
                vec.tensor_tensor(p_tail[:, :, :], m_ps[0:BT * CH, P:2 * P].unsqueeze(1).to_broadcast([BT * CH, BT, P]),
                                  tailmask[:, 0, :].unsqueeze(2).to_broadcast([BT * CH, BT, P]),
                                  ALU.mult).then_inc(ptail_sb, 1)

            def recip(t, p):
                dve.wait_ge(exp_sb, t * UN + UN)
                vec.reciprocal(rsum[:, :], sums[p][:, :]).then_inc(rsum_sb, 1)

            def normalise(t):
                dve.wait_ge(r_psum, t + 1)
                dve.wait_ge(o_sb, t + 1)
                four = "p (b h s) -> p h b s"
                vec.tensor_tensor(o_norm[:, :, :, :], o_raw[:, :].rearrange(four, b=BT, h=CH),
                                  m_ps[:, :].rearrange(four, b=BT, h=CH), ALU.mult).then_inc(on_sb, 1)

            def add_out(t):
                dve.wait_ge(out_psum, t + 1)
                vec.tensor_tensor(g.x[:, t, :], g.x[:, t, :], m_ps[:, 0:D], ALU.add).then_inc(x_sb, 1)

            def moments(t):
                dve.wait_ge(x_sb, t + 1)
                vec.bn_stats(g.bn[:, t, :], g.x[:, t, :]).then_inc(stats_sb, 1)

            def tile(t, p, prev, nxt):
                if nxt:
                    norm(t + 1)
                for u in range(UN):
                    maxes(t, p, u)
                    if u == 0 and prev:
                        copy_pT(t - 1, UN - 1)
                    if u >= 1:
                        copy_pT(t, u - 1)
                    if u == 0:
                        if nxt and prev:
                            dve.wait_ge(ptail_psum, t)
                        if nxt:
                            copy_xnT(t + 1)
                        if prev:
                            copy_ptail(t - 1)
                            recip(t - 1, 1 - p)
                    if u == 2 and prev:
                        normalise(t - 1)
                    if u == 3:
                        if nxt and prev:
                            dve.wait_ge(qT_psum, t + 2)
                        if prev:
                            add_out(t - 1)
                        if nxt:
                            copy_q(t + 1, 1 - p)
                    if u == 5 and prev:
                        moments(t - 1)
                    if u == 6 and nxt:
                        copy_tails(t + 1, 1 - p)

            norm_coefficients(nc, g, None, dve, ln_step, lnw)
            dve.wait_ge(w_in, 16 * 11)
            dve.wait_ge(mask_in, 16 * CH)
            vec.memset(ones[:, :], 1.0).then_inc(prep_dve, 1)
            vec.tensor_scalar(headmask_s[:, :], headmask[:, :], scale, None, ALU.mult).then_inc(prep_dve, 1)
            vec.tensor_tensor(w_om[:, :, :], w_o[:, :].unsqueeze(1).to_broadcast([P, CH, D]),
                              headmask[:, :].unsqueeze(2).to_broadcast([P, CH, D]), ALU.mult).then_inc(prep_dve, 1)
            vec.tensor_scalar(mask_b[:, :], mask_i[:, :], 0, MASKED, ALU.is_equal, ALU.mult).then_inc(prep_dve, 1)
            norm(0)
            dve.wait_ge(prep_pe, 1)
            vec.tensor_tensor(out_bias[:, :], m_ps[0:1, 0:D], bo_row[:, :], ALU.add).then_inc(prep_dve, 1)
            copy_xnT(0)
            copy_q(0, 0)
            copy_tails(0, 0)
            tile(0, 0, False, True)
            with dve.Fori(0, T // 2 - 1) as i:
                tile(i * 2 + 1, 1, True, True)
                tile(i * 2 + 2, 0, True, True)
            tile(T - 1, 1, True, False)
            copy_pT(T - 1, UN - 1)
            copy_ptail(T - 1)
            recip(T - 1, 1)
            normalise(T - 1)
            add_out(T - 1)
            moments(T - 1)
            dve.wait_ge(stats_sb, T)


def split_row(vec, dve, done, base, src, masks, work, out):
    hi, rest, f = work
    n = [base]

    def run(ins):
        ins.then_inc(done, 1)
        n[0] += 1
        dve.wait_ge(done, n[0])

    run(vec.tensor_copy(hi, src))
    run(vec.tensor_tensor(rest, src, hi, ALU.subtract))
    run(vec.tensor_scalar(f, hi, masks[:, 0:1], None, ALU.mult))
    run(vec.tensor_copy(hi, rest))
    run(vec.tensor_tensor(rest, rest, hi, ALU.subtract))
    run(vec.scalar_tensor_tensor(f, hi, masks[:, 1:2], f, ALU.mult, ALU.add))
    run(vec.tensor_copy(hi, rest))
    run(vec.scalar_tensor_tensor(f, hi, masks[:, 2:3], f, ALU.mult, ALU.add))
    run(vec.tensor_copy(out, f))
    return n[0]


E1 = 3 * D
R0 = 64
CB = E1 // P
SRMS_EPS = 1e-8
GAMMA = 0.99


def stage_mixer0(nc, g):
    with ExitStack() as ctx:
        sem = sem_maker(nc, g, "m0")
        sb, ps = tensor_makers(nc, ctx, "m0")
        w_uv = sb("w_uv", [P, 2, E1])
        w_o = sb("w_o", [P, CB, D])
        uvb3 = sb("uvb3", [3, 2 * E1])
        b_hi, b_rest, b_f = sb("b_hi", [3, 2 * E1], BF16), sb("b_rest", [3, 2 * E1]), sb("b_f", [3, 2 * E1])
        uvb = sb("uvb", [3, 2 * E1], BF16)
        ob = sb("ob", [1, D])
        ones3, ones1 = sb("ones3", [3, P], BF16), sb("ones1", [1, P])
        rowmask = sb("rowmask", [3, 3])
        dft = sb("dft", [P, 3, P])
        idft = sb("idft", [P, 3, P])
        cdft = sb("cdft", [S, 3, P])
        pos = sb("pos", [1, S])
        pos_w = sb("pos_w", [1, 2, R0])
        lw = sb("lw", [R0, 3, R0])
        lb = sb("lb", [1, 3, R0])
        out_w, out_b = sb("out_w", [R0, E1]), sb("out_b", [1, E1])
        sq, ss, rr = sb("sq", [S, R0]), sb("ss", [S, 4]), sb("rr", [S, 4, 2])
        hn, hT = sb("hn", [S, R0]), sb("hT", [R0, S])
        coef = sb("coef", [S, E1])
        mult = sb("mult", [P, 3, E1])
        lnw = sb("lnw", [P, 4, T])
        xn, xnT = sb("xn", [P, D]), sb("xnT", [P, P])
        u = [sb(f"u{p}", [P, E1]) for p in range(2)]
        v = sb("v", [P, E1])
        prod = sb("prod", [P, 3, E1])
        gated, gT = sb("gated", [P, E1]), sb("gT", [P, E1])

        m_ps = ps("m_ps", [P, BANK])
        t_ps = ps("t_ps", [P, BANK])
        uv_ps = [ps(f"uv_ps{n}", [P, BANK]) for n in range(2)]
        f_ps = [ps(f"f_ps{n}", [P, BANK]) for n in range(3)]
        y_ps = ps("y_ps", [P, BANK])

        w_in, line, ln_step, ready, bias_step = sem("w_in"), sem("line"), sem("ln_step"), sem("ready"), sem("bias_step")
        xn_ready, xnT_psum, xnT_sb = sem("xn_ready"), sem("xnT_psum"), sem("xnT_sb")
        uv_psum, v_sb, u_sb = sem("uv_psum"), sem("v_sb"), sem("u_sb")
        sums_psum, prod_sb, y_psum, gated_sb = sem("sums_psum"), sem("prod_sb"), sem("y_psum"), sem("gated_sb")
        gT_psum, gT_sb, out_psum, x_sb, stats_sb = sem("gT_psum"), sem("gT_sb"), sem("out_psum"), sem("x_sb"), sem("stats_sb")
        N_LOADS = 19
        block = ctx.enter_context(nc.Block())

        def row(name):
            return g.dram[name].rearrange("(a n) -> a n", a=1)

        @block.sync
        def _(sp):
            def load(dst, src):
                sp.dma_start(dst, src).then_inc(w_in, 16)

            load(w_uv[:, 0, :], g.dram["L0_attn_u_w"])
            load(w_uv[:, 1, :], g.dram["L0_attn_v_w"])
            load(w_o[:, :, :], g.dram["L0_attn_o_w"].rearrange("(c p) n -> p c n", p=P))
            load(uvb3[:, 0:E1], row("L0_attn_u_b").to_broadcast([3, E1]))
            load(uvb3[:, E1:2 * E1], row("L0_attn_v_b").to_broadcast([3, E1]))
            load(ob[:, :], row("L0_attn_o_b"))
            load(rowmask[:, :], g.dram["c_rowmask"])
            load(dft[:, :, :], g.dram["c_dft"])
            load(idft[:, :, :], g.dram["c_idft"])
            load(cdft[:, :, :], g.dram["c_cdft"])
            load(pos[:, :], g.dram["c_pos"])
            load(pos_w[:, 0, :], g.dram["L0_attn_pos_w"])
            load(pos_w[:, 1, :], row("L0_attn_pos_b"))
            for n in range(3):
                load(lw[:, n, :], g.dram[f"L0_attn_lw{n}"])
            load(lb[:, :, :].rearrange("a n r -> a (n r)"), g.dram["c_lb"])
            load(out_w[:, :], g.dram["L0_attn_out_w"])
            load(out_b[:, :], row("L0_attn_out_b"))

        ROUND = 8

        @block.tensor
        def _(pe):
            mm, tr = nc.tensor.matmul, nc.tensor.transpose
            pe.wait_ge(w_in, 16 * N_LOADS)
            pe.wait_ge(ready, 2)
            for n in range(5):
                if n:
                    pe.wait_ge(line, n * ROUND)
                width = R0 if n < 4 else E1
                rhs = [pos_w[:, 0, :], lw[:, 0, :], lw[:, 1, :], lw[:, 2, :], out_w[:, :]][n]
                bias = [pos_w[:, 1, :], lb[:, 0, :], lb[:, 1, :], lb[:, 2, :], out_b[:, :]][n]
                mm(m_ps[0:S, 0:width], pos[:, :] if n == 0 else hT[:, :], rhs, start=True, stop=False)
                mm(m_ps[0:S, 0:width], ones1[:, 0:S], bias, start=False, stop=True).then_inc(line, 1)
                if n < 4:
                    pe.wait_ge(line, n * ROUND + 6)
                    tr(t_ps[0:R0, 0:S], hn[:, :], g.ident[0:S, 0:S]).then_inc(line, 1)
            pe.wait_ge(line, 4 * ROUND + 2)
            for n in range(3):
                ins = mm(f_ps[n][:, 0:E1], cdft[:, n, :], coef[:, :], start=True, stop=True)
            ins.then_inc(line, 1)
            pe.wait_ge(bias_step, 9)

            def turn_xn(t):
                pe.wait_ge(xn_ready, t + 1)
                tr(m_ps[:, 0:P], xn[:, :], g.ident[:, :]).then_inc(xnT_psum, 1)

            def uv(t):
                pe.wait_ge(xnT_sb, t + 1)
                for n in range(2):
                    mm(uv_ps[n][:, 0:E1], xnT[:, :], w_uv[:, n, :], start=True, stop=False)
                    ins = mm(uv_ps[n][:, 0:E1], ones3[:, :], uvb[:, n * E1:(n + 1) * E1], start=False, stop=True)
                ins.then_inc(uv_psum, 1)

            def transform(t):
                pe.wait_ge(v_sb, t + 1)
                for n in range(3):
                    ins = mm(f_ps[n][:, 0:E1], dft[:, n, :], v[:, :], start=True, stop=True)
                ins.then_inc(sums_psum, 1)

            def back(t):
                pe.wait_ge(prod_sb, t * 3 + 3)
                for n in range(3):
                    ins = mm(y_ps[:, 0:E1], idft[:, n, :], prod[:, n, :], start=(n == 0), stop=(n == 2))
                ins.then_inc(y_psum, 1)

            def turn_gated(t):
                pe.wait_ge(gated_sb, t + 1)
                for c in range(CB):
                    ins = tr(t_ps[:, c * P:(c + 1) * P], gated[:, c * P:(c + 1) * P], g.ident[:, :])
                ins.then_inc(gT_psum, 1)

            def project(t):
                pe.wait_ge(gT_sb, t + 1)
                for c in range(CB):
                    mm(m_ps[:, 0:D], gT[:, c * P:(c + 1) * P], w_o[:, c, :], start=(c == 0), stop=False)
                mm(m_ps[:, 0:D], ones1[:, :], ob[:, :], start=False, stop=True).then_inc(out_psum, 1)

            def tile(t, prev, nxt):
                if prev and not (isinstance(t, int) and t == 1):
                    pe.wait_ge(x_sb, t - 1)
                if nxt:
                    turn_xn(t + 1)
                transform(t)
                if nxt:
                    pe.wait_ge(u_sb, t + 1)
                    uv(t + 1)
                if prev:
                    if nxt:
                        pe.wait_ge(xnT_sb, t + 2)
                    project(t - 1)
                back(t)
                turn_gated(t)

            pe.wait_ge(line, 4 * ROUND + 4)
            turn_xn(0)
            uv(0)
            tile(0, False, True)
            tile(1, True, True)
            with pe.Fori(2, T - 1) as t:
                tile(t, True, True)
            tile(T - 1, True, False)
            pe.wait_ge(x_sb, T - 1)
            project(T - 1)

        @block.scalar
        def _(act):
            norm_coefficients(nc, g, act, None, ln_step, lnw)
            for n in range(4):
                act.wait_ge(line, n * ROUND + 1)
                nc.scalar.activation(sq[:, :], m_ps[0:S, 0:R0], ACT.Square, accum_out=ss[:, n:n + 1]).then_inc(line, 1)
                act.wait_ge(line, n * ROUND + 2)
                nc.scalar.activation(rr[:, n, 0:1], ss[:, n:n + 1], ACT.Sqrt, scale=1.0 / R0).then_inc(line, 1)

            def silus(t, p):
                act.wait_ge(uv_psum, t + 1)
                nc.scalar.activation(v[:, :], uv_ps[1][:, 0:E1], ACT.Silu).then_inc(v_sb, 1)
                nc.scalar.activation(u[p][:, :], uv_ps[0][:, 0:E1], ACT.Silu).then_inc(u_sb, 1)

            def copy_gT(t):
                act.wait_ge(gT_psum, t + 1)
                nc.scalar.activation(gT[:, :], t_ps[:, 0:E1], ACT.Copy).then_inc(gT_sb, 1)

            silus(0, 0)
            with act.Fori(0, T // 2 - 1) as i:
                for p in range(2):
                    act.wait_ge(sums_psum, i * 2 + (p + 1))
                    silus(i * 2 + (p + 1), 1 - p)
                    copy_gT(i * 2 + p)
            act.wait_ge(sums_psum, T - 1)
            silus(T - 1, 1)
            copy_gT(T - 2)
            copy_gT(T - 1)

        @block.vector
        def _(dve):
            vec = nc.vector
            vec.memset(ones1[:, :], 1.0).then_inc(ready, 1)
            vec.memset(ones3[:, :], 1.0).then_inc(ready, 1)
            norm_coefficients(nc, g, None, dve, ln_step, lnw)
            for n in range(4):
                k = n * ROUND
                dve.wait_ge(line, k + 3)
                vec.tensor_scalar(rr[:, n, 1:2], rr[:, n, 0:1], SRMS_EPS, None, ALU.add).then_inc(line, 1)
                dve.wait_ge(line, k + 4)
                vec.reciprocal(rr[:, n, 1:2], rr[:, n, 1:2]).then_inc(line, 1)
                dve.wait_ge(line, k + 5)
                vec.tensor_scalar(hn[:, :], m_ps[0:S, 0:R0], rr[:, n, 1:2], 0.0, ALU.mult, ALU.max).then_inc(line, 1)
                dve.wait_ge(line, k + 7)
                vec.tensor_copy(hT[:, :], t_ps[0:R0, 0:S]).then_inc(line, 1)
            dve.wait_ge(line, 4 * ROUND + 1)
            vec.tensor_copy(coef[:, :], m_ps[0:S, 0:E1]).then_inc(line, 1)
            dve.wait_ge(line, 4 * ROUND + 3)
            for n in range(3):
                ins = vec.tensor_copy(mult[:, n, :], f_ps[n][:, 0:E1])
            ins.then_inc(line, 1)
            dve.wait_ge(w_in, 16 * N_LOADS)
            split_row(vec, dve, bias_step, 0, uvb3[:, :], rowmask, (b_hi[:, :], b_rest[:, :], b_f[:, :]), uvb[:, :])

            def norm(t):
                vec.tensor_scalar(xn[:, :], g.x[:, t, :], g.rstd[:, bass.ds(t, 1)], g.shift[:, bass.ds(t, 1)],
                                  ALU.mult, ALU.add).then_inc(xn_ready, 1)

            def copy_xnT(t):
                dve.wait_ge(xnT_psum, t + 1)
                vec.tensor_copy(xnT[:, :], m_ps[:, 0:P]).then_inc(xnT_sb, 1)

            def products(t):
                dve.wait_ge(sums_psum, t + 1)
                for n in range(3):
                    vec.tensor_tensor(prod[:, n, :], f_ps[n][:, 0:E1], mult[:, n, :], ALU.mult).then_inc(prod_sb, 1)

            def gate(t, p):
                dve.wait_ge(y_psum, t + 1)
                vec.tensor_tensor(gated[:, :], u[p][:, :], y_ps[:, 0:E1], ALU.mult).then_inc(gated_sb, 1)

            def add_out(t):
                dve.wait_ge(out_psum, t + 1)
                vec.tensor_tensor(g.x[:, t, :], g.x[:, t, :], m_ps[:, 0:D], ALU.add).then_inc(x_sb, 1)
                dve.wait_ge(x_sb, t + 1)
                vec.bn_stats(g.bn[:, t, :], g.x[:, t, :]).then_inc(stats_sb, 1)

            def tile(t, p, prev, nxt):
                if nxt:
                    copy_xnT(t + 1)
                products(t)
                if nxt and not (isinstance(t, int) and t == T - 2):
                    norm(t + 2)
                if prev:
                    add_out(t - 1)
                gate(t, p)

            dve.wait_ge(line, 4 * ROUND + 4)
            norm(0)
            copy_xnT(0)
            norm(1)
            tile(0, 0, False, True)
            tile(1, 1, True, True)
            with dve.Fori(0, T // 2 - 2) as i:
                tile(i * 2 + 2, 0, True, True)
                tile(i * 2 + 3, 1, True, True)
            tile(T - 2, 0, True, True)
            tile(T - 1, 1, True, False)
            add_out(T - 1)
            dve.wait_ge(stats_sb, T)


GT = 4
NG = T // GT
TOK = GT * P
NE, EI = 8, 64
RC = NE * EI // P
HC = RC + 1
TOP0, ROUTE_SCALE = 2, 2.5
PAD = -3.0e38
TAKEN = 3.0e38


def wait(eng, sem, value):
    if not (isinstance(value, int) and value <= 0):
        eng.wait_ge(sem, value)


def take_top(vec, run, alone, scores, width, top, r):
    rows = scores.shape[1]
    alone()
    for j in range(rows):
        run(vec.max(r["sorted"][:, j, :], scores[:, j, 0:width]), last=(j == rows - 1))
    run(vec.tensor_copy(r["taken"][:, :, 0:top], r["sorted"][:, :, 0:top]))
    alone()
    for j in range(rows):
        run(vec.match_replace(r["marked"][:, j, :], r["taken"][:, j, :], scores[:, j, :], TAKEN), last=(j == rows - 1))
    run(vec.tensor_tensor(r["sel"], scores[:, :, 0:width], r["marked"][:, :, 0:width], ALU.not_equal))


def split_three(vec, run, value, parts, hi, rest):
    run(vec.tensor_copy(hi, value))
    run(vec.tensor_copy(parts[0], hi), last=False)
    run(vec.tensor_tensor(rest, value, hi, ALU.subtract))
    run(vec.tensor_copy(hi, rest))
    run(vec.tensor_copy(parts[1], hi), last=False)
    run(vec.tensor_tensor(parts[2], rest, hi, ALU.subtract))


def stage_experts0(nc, g):
    with ExitStack() as ctx:
        sem = sem_maker(nc, g, "e0")
        sb, ps = tensor_makers(nc, ctx, "e0")
        w_g, w_u, w_d = sb("w_g", [P, HC, P]), sb("w_u", [P, HC, P]), sb("w_d", [P, HC, D])
        w_r = sb("w_r", [P, NE])
        spread = sb("spread", [3 * NE, RC, P], BF16)
        lnw = sb("lnw", [P, 4, T])
        xn = sb("xn", [P, GT, D])
        xnT = [sb(f"xnT{p}", [P, TOK]) for p in range(2)]
        scores = sb("scores", [P, GT, NE + 8 - TOP0])
        r = {"sorted": sb("sorted", [P, GT, 8]), "taken": sb("taken", [P, GT, 8]),
             "marked": sb("marked", [P, GT, NE + 8 - TOP0]), "sel": sb("sel", [P, GT, NE])[:, :, :]}
        total, weight = sb("total", [P, GT]), sb("weight", [P, GT, NE])
        part_hi, part_rest = sb("part_hi", [P, GT, NE], BF16), sb("part_rest", [P, GT, NE])
        parts = sb("parts", [P, GT, 3 * NE])
        weightT = [sb(f"weightT{p}", [3 * NE, TOK], BF16) for p in range(2)]
        gate = [sb(f"gate{p}", [P, TOK]) for p in range(2)]
        hid = [sb(f"hid{p}", [P, TOK]) for p in range(2)]

        m_ps = ps("m_ps", [P, BANK])
        g_ps = [ps(f"g_ps{p}", [P, BANK]) for p in range(2)]
        u_ps = [ps(f"u_ps{p}", [P, BANK]) for p in range(2)]
        w_ps = [ps(f"w_ps{p}", [P, BANK]) for p in range(2)]
        o_ps = ps("o_ps", [P, BANK])

        w_in, ln_step, pads = sem("w_in"), sem("ln_step"), sem("pads")
        xn_ready, xT_psum, xT_sb = sem("xn_ready"), sem("xT_psum"), sem("xT_sb")
        logits_psum, scores_sb, route = sem("logits_psum"), sem("scores_sb"), sem("route")
        wT_psum, wT_sb = sem("wT_psum"), sem("wT_sb")
        up_psum, gate_sb, mid_sb, hid_sb, down = sem("up_psum"), sem("gate_sb"), sem("mid_sb"), sem("hid_sb"), sem("down")
        x_sb, stats_sb = sem("x_sb"), sem("stats_sb")
        waited = sem("waited")
        N_LOADS = 5
        ROUTE_STEPS = 2 * GT + 13
        block = ctx.enter_context(nc.Block())

        @block.sync
        def _(sp):
            sp.dma_start(w_g[:, :, :].rearrange("p h n -> p (h n)"), g.dram["L0_gate_T"]).then_inc(w_in, 16)
            sp.dma_start(w_u[:, :, :].rearrange("p h n -> p (h n)"), g.dram["L0_up_T"]).then_inc(w_in, 16)
            sp.dma_start(w_d[:, :, :], g.dram["L0_down_T"].rearrange("(h p) n -> p h n", p=P)).then_inc(w_in, 16)
            sp.dma_start(w_r[:, :], g.dram["L0_ffn_gate_weight_T"]).then_inc(w_in, 16)
            sp.dma_start(spread[:, :, :].rearrange("r h n -> r (h n)"), g.dram["c_spread0"]).then_inc(w_in, 16)

        @block.tensor
        def _(pe):
            mm, tr = nc.tensor.matmul, nc.tensor.transpose

            def turn_x(n):
                pe.wait_ge(xn_ready, n * GT + GT)
                for k in range(GT):
                    ins = tr(m_ps[:, k * P:(k + 1) * P], xn[:, k, :], g.ident[:, :])
                ins.then_inc(xT_psum, 1)

            def logits(n, p):
                pe.wait_ge(xT_sb, n + 1)
                for k in range(GT):
                    ins = mm(m_ps[:, k * NE:(k + 1) * NE], xnT[p][:, k * P:(k + 1) * P], w_r[:, :], start=True, stop=True)
                ins.then_inc(logits_psum, 1)

            def turn_weights(n):
                pe.wait_ge(route, n * ROUTE_STEPS + ROUTE_STEPS)
                for k in range(GT):
                    ins = tr(m_ps[0:3 * NE, k * P:(k + 1) * P], parts[:, k, :], g.ident[:, :])
                ins.then_inc(wT_psum, 1)

            def up(n, p, h):
                b = (p + h) % 2
                if h == 0:
                    pe.wait_ge(wT_sb, n + 1)
                wait(pe, hid_sb, n * HC + h - 1)
                mm(g_ps[b][:, :], w_g[:, h, :], xnT[p][:, :], start=True, stop=True)
                ins = mm(u_ps[b][:, :], w_u[:, h, :], xnT[p][:, :], start=True, stop=True)
                if h < RC:
                    ins = mm(w_ps[b][:, :], spread[:, h, :], weightT[p][:, :], start=True, stop=True)
                ins.then_inc(up_psum, 1)

            def project(n, p, h):
                pe.wait_ge(hid_sb, n * HC + h + 1)
                if h == 0:
                    wait(pe, x_sb, n)
                for k in range(GT):
                    ins = mm(o_ps[:, k * D:(k + 1) * D], hid[(p + h) % 2][:, k * P:(k + 1) * P], w_d[:, h, :],
                             start=(h == 0 and k == 0), stop=(h == HC - 1), skip_group_check=True)
                ins.then_inc(down, 1)

            def group(n, p, prev, nxt):
                for h in range(HC):
                    up(n, p, h)
                    if h:
                        project(n, p, h - 1)
                    elif prev:
                        project(n - 1, 1 - p, HC - 1)
                    if nxt and h == 1:
                        turn_x(n + 1)
                    if nxt and h == 2:
                        logits(n + 1, 1 - p)
                    if nxt and h == 4:
                        turn_weights(n + 1)

            pe.wait_ge(w_in, 16 * N_LOADS)
            turn_x(0)
            logits(0, 0)
            turn_weights(0)
            group(0, 0, False, True)
            with pe.Fori(0, NG // 2 - 1) as i:
                group(i * 2 + 1, 1, True, True)
                group(i * 2 + 2, 0, True, True)
            group(NG - 1, 1, True, False)
            project(NG - 1, 1, HC - 1)

        @block.scalar
        def _(act):
            def sigmoids(n):
                act.wait_ge(logits_psum, n + 1)
                nc.scalar.activation(scores[:, :, 0:NE], m_ps[:, 0:GT * NE].rearrange("p (k e) -> p k e", k=GT),
                                     ACT.Sigmoid).then_inc(scores_sb, 1)

            def silu(n, p, h):
                act.wait_ge(up_psum, n * HC + h + 1)
                nc.scalar.activation(gate[(p + h) % 2][:, :], g_ps[(p + h) % 2][:, :], ACT.Silu).then_inc(gate_sb, 1)

            def group(n, p, nxt):
                for h in range(HC):
                    silu(n, p, h)
                    if nxt and h == 2:
                        sigmoids(n + 1)

            norm_coefficients(nc, g, act, None, ln_step, lnw)
            sigmoids(0)
            with act.Fori(0, NG // 2 - 1) as i:
                group(i * 2, 0, True)
                group(i * 2 + 1, 1, True)
            group(NG - 2, 0, True)
            group(NG - 1, 1, False)

        @block.vector
        def _(dve):
            vec = nc.vector

            def norm(n):
                for k in range(GT):
                    t = n * GT + k
                    vec.tensor_scalar(xn[:, k, :], g.x[:, t, :], g.rstd[:, bass.ds(t, 1)], g.shift[:, bass.ds(t, 1)],
                                      ALU.mult, ALU.add).then_inc(xn_ready, 1)

            def copy_xT(n, p):
                dve.wait_ge(xT_psum, n + 1)
                vec.tensor_copy(xnT[p][:, :], m_ps[:, :]).then_inc(xT_sb, 1)

            def routing(n):
                dve.wait_ge(scores_sb, n + 1)
                done = [0]

                def run(ins, last=True):
                    ins.then_inc(route, 1)
                    done[0] += 1
                    if last:
                        dve.wait_ge(route, n * ROUTE_STEPS + done[0])

                take_top(vec, run, lambda: dve.sem_inc(waited, 1), scores[:, :, :], NE, TOP0, r)
                run(vec.tensor_tensor(weight[:, :, :], r["sel"], scores[:, :, 0:NE], ALU.mult))
                run(vec.tensor_reduce(total[:, :], weight[:, :, :], AX.X, ALU.add))
                run(vec.tensor_scalar(total[:, :], total[:, :], 1e-20, None, ALU.add))
                run(vec.reciprocal(total[:, :], total[:, :]))
                run(vec.scalar_tensor_tensor(weight[:, :, :], weight[:, :, :], ROUTE_SCALE,
                                             total[:, :].unsqueeze(2).to_broadcast([P, GT, NE]), ALU.mult, ALU.mult))
                split_three(vec, run, weight[:, :, :], [parts[:, :, j * NE:(j + 1) * NE] for j in range(3)],
                            part_hi[:, :, :], part_rest[:, :, :])
                assert done[0] == ROUTE_STEPS

            def copy_weights(n, p):
                dve.wait_ge(wT_psum, n + 1)
                vec.tensor_copy(weightT[p][:, :], m_ps[0:3 * NE, :]).then_inc(wT_sb, 1)

            def hidden(n, p, h):
                b = (p + h) % 2
                dve.wait_ge(gate_sb, n * HC + h + 1)
                wait(dve, down, n * HC + h - 1)
                first = vec.tensor_tensor(hid[b][:, :], gate[b][:, :], u_ps[b][:, :], ALU.mult)
                if h < RC:
                    first.then_inc(mid_sb, 1)
                    dve.wait_ge(mid_sb, n * RC + h + 1)
                    vec.tensor_tensor(hid[b][:, :], hid[b][:, :], w_ps[b][:, :], ALU.mult).then_inc(hid_sb, 1)
                else:
                    first.then_inc(hid_sb, 1)

            def add_out(n):
                dve.wait_ge(down, n * HC + HC)
                xs = g.x[:, bass.ds(n * GT, GT), :]
                vec.tensor_tensor(xs, xs, o_ps[:, :].rearrange("p (k d) -> p k d", k=GT), ALU.add).then_inc(x_sb, 1)
                dve.wait_ge(x_sb, n + 1)
                for k in range(GT):
                    vec.bn_stats(g.bn[:, n * GT + k, :], g.x[:, n * GT + k, :]).then_inc(stats_sb, 1)

            def group(n, p, prev, nxt):
                for h in range(HC):
                    hidden(n, p, h)
                    if h == 0:
                        if prev:
                            add_out(n - 1)
                        if nxt:
                            norm(n + 1)
                    if nxt and h == 1:
                        copy_xT(n + 1, 1 - p)
                    if nxt and h == 2:
                        routing(n + 1)
                    if nxt and h == 4:
                        copy_weights(n + 1, 1 - p)

            vec.memset(scores[:, :, NE:], PAD).then_inc(pads, 1)
            vec.memset(r["taken"][:, :, TOP0:], PAD).then_inc(pads, 1)
            norm_coefficients(nc, g, None, dve, ln_step, lnw)
            dve.wait_ge(pads, 2)
            norm(0)
            copy_xT(0, 0)
            routing(0)
            copy_weights(0, 0)
            group(0, 0, False, True)
            with dve.Fori(0, NG // 2 - 1) as i:
                group(i * 2 + 1, 1, True, True)
                group(i * 2 + 2, 0, True, True)
            group(NG - 1, 1, True, False)
            add_out(NG - 1)
            dve.wait_ge(stats_sb, T)


def pipeline(eng, step, ahead, behind, unroll=2):
    first = -(-behind // unroll) * unroll
    last = T - -(-ahead // unroll) * unroll
    for t in range(-ahead, first):
        step(t, t % unroll)
    with eng.Fori(0, (last - first) // unroll) as i:
        for p in range(unroll):
            step(i * unroll + (first + p), p)
    for t in range(last, T + behind):
        step(t, t % unroll)


def inside(t):
    return not isinstance(t, int) or 0 <= t < T


def stage_cross1(nc, g):
    inv = 1.0 / 32.0
    with ExitStack() as ctx:
        sem = sem_maker(nc, g, "x1")
        sb, ps = tensor_makers(nc, ctx, "x1")
        w_q, w_k = sb("w_q", [P, D]), sb("w_k", [P, D])
        cols = sb("cols", [P, 2])
        lnw = sb("lnw", [P, 4, T])
        ctx_t = [sb(f"ctx_t{p}", [P, BT, S2]) for p in range(2)]
        ctx_n = [sb(f"ctx_n{p}", [P, 2, BT, D]) for p in range(2)]
        ctx_l = [sb(f"ctx_l{p}", [1, BT, D]) for p in range(2)]
        xn = [sb(f"xn{p}", [P, D]) for p in range(2)]
        xnT, qT, qkT = ([sb(f"{n}{p}", [P, P]) for p in range(2)] for n in ("xnT", "qT", "qkT"))
        c = [sb(f"c{p}", [P, 1]) for p in range(2)]
        neg, bias = sb("neg", [P, 2, 2]), sb("bias", [P, 2])
        sums, rsum = sb("sums", [P, 2]), sb("rsum", [P, 2])
        probs = [sb(f"probs{p}", [P, S2]) for p in range(2)]
        pT = [sb(f"pT{p}", [P, 2, P]) for p in range(2)]
        pT_l = [sb(f"pT_l{p}", [1, P]) for p in range(2)]

        x_ps, q_ps, k_ps, p_ps, o_ps = (ps(n, [P, BANK]) for n in ("x_ps", "q_ps", "k_ps", "p_ps", "o_ps"))
        s_ps = [ps(f"s_ps{p}", [P, BANK]) for p in range(2)]

        w_in, ln_step = sem("w_in"), sem("ln_step")
        ctxT_in, ctx_in = ([sem(f"{n}{p}") for p in range(2)] for n in ("ctxT_in", "ctx_in"))
        xn_ready, xT_psum, xT_sb, q_psum, q_sb = (sem(n) for n in ("xn_ready", "xT_psum", "xT_sb", "q_psum", "q_sb"))
        qk_psum, qk_sb, scores_psum, max_sb = (sem(n) for n in ("qk_psum", "qk_sb", "scores_psum", "max_sb"))
        neg_sb, bias_sb, exp_sb, pT_psum, pT_sb = (sem(n) for n in ("neg_sb", "bias_sb", "exp_sb", "pT_psum", "pT_sb"))
        rsum_sb, o_psum, x_sb, x_out = (sem(n) for n in ("rsum_sb", "o_psum", "x_sb", "x_out"))
        block = ctx.enter_context(nc.Block())
        W_LOADS = 4

        @block.sync
        def _(sp):
            def load_T(t, p):
                sp.dma_start(ctx_t[p][:, :, :], g.dram["ctxT"][bass.ds(t * BT, BT)].rearrange("b d k -> d b k"))\
                  .then_inc(ctxT_in[p], 16)

            def load_n(t, p):
                src = g.dram["ctx"][bass.ds(t * BT, BT)]
                for k in range(2):
                    sp.dma_start(ctx_n[p][:, k, :, :], src[:, k * P:(k + 1) * P, :].rearrange("b p d -> p b d"))\
                      .then_inc(ctx_in[p], 16)
                sp.dma_start(ctx_l[p][:, :, :], src[:, 2 * P:S2, :].rearrange("b k d -> k b d")).then_inc(ctx_in[p], 16)

            sp.dma_start(w_q[:, :], g.dram["L1_xattn_Wq_T"]).then_inc(w_in, 16)
            sp.dma_start(w_k[:, :], g.dram["L1_xattn_Wk"]).then_inc(w_in, 16)
            sp.dma_start(cols[:, 0:1], g.dram["L1_xattn_bq"].rearrange("(p a) -> p a", a=1)).then_inc(w_in, 16)
            sp.dma_start(cols[:, 1:2], g.dram["L1_xattn_bk"].rearrange("(p a) -> p a", a=1)).then_inc(w_in, 16)
            load_T(0, 0)
            load_T(1, 1)

            def step(t, p):
                if inside(t):
                    wait(sp, o_psum, t - 1)
                    load_n(t, p)
                if inside(t + 2) and inside(t):
                    sp.wait_ge(scores_psum, t + 1)
                    load_T(t + 2, p)
                if inside(t - 3):
                    sp.wait_ge(x_sb, t - 2)
                    dst = g.x_mid[bass.ds((t - 3) * BT, BT)].rearrange("b s d -> (b s) d")
                    sp.dma_start(dst, g.x[:, t - 3, :]).then_inc(x_out, 16)

            pipeline(sp, step, 2, 3)
            sp.wait_ge(x_out, 16 * T)

        @block.tensor
        def _(pe):
            mm, tr = nc.tensor.matmul, nc.tensor.transpose

            def step(t, p):
                o = 1 - p
                if inside(t + 3):
                    pe.wait_ge(xn_ready, t + 4)
                    wait(pe, xT_sb, t + 3)
                    tr(x_ps[:, 0:P], xn[o][:, :], g.ident[:, :]).then_inc(xT_psum, 1)
                if inside(t + 2):
                    pe.wait_ge(xT_sb, t + 3)
                    wait(pe, q_sb, t + 2)
                    mm(q_ps[:, 0:P], w_q[:, :], xnT[p][:, :], start=True, stop=True).then_inc(q_psum, 1)
                if inside(t + 1):
                    pe.wait_ge(q_sb, t + 2)
                    wait(pe, qk_sb, (t + 1) * 2)
                    mm(k_ps[:, 0:P], w_k[:, :], qT[o][:, :], start=True, stop=True)
                    mm(k_ps[:, P:P + 1], qT[o][:, :], cols[:, 1:2], start=True, stop=True).then_inc(qk_psum, 1)
                if inside(t):
                    pe.wait_ge(qk_sb, (t + 1) * 2)
                    pe.wait_ge(ctxT_in[p], (t - p) * 8 + 16)
                    wait(pe, exp_sb, t - 1)
                    for b in range(BT):
                        q = slice(b * S, b * S + S)
                        ins = mm(s_ps[p][q, 0:S2], qkT[p][:, q], ctx_t[p][:, b, :], start=True, stop=True)
                    ins.then_inc(scores_psum, 1)
                if inside(t - 1):
                    pe.wait_ge(exp_sb, t)
                    wait(pe, pT_sb, (t - 1) * 2)
                    for k in range(2):
                        tr(p_ps[:, k * P:(k + 1) * P], probs[o][:, k * P:(k + 1) * P], g.ident[:, :])
                    tr(p_ps[0:1, 2 * P:3 * P], probs[o][:, 2 * P:S2], g.ident[:, :]).then_inc(pT_psum, 1)
                if inside(t - 2):
                    pe.wait_ge(pT_sb, (t - 1) * 2)
                    pe.wait_ge(ctx_in[p], (t - 2 - p) * 24 + 48)
                    wait(pe, x_sb, t - 2)
                    for k in range(3):
                        for b in range(BT):
                            q = slice(b * S, b * S + S)
                            lhs, rhs = (pT[p][:, k, q], ctx_n[p][:, k, b, :]) if k < 2 else (pT_l[p][:, q], ctx_l[p][:, b, :])
                            ins = mm(o_ps[q, 0:D], lhs, rhs, start=(k == 0), stop=(k == 2), skip_group_check=True)
                    ins.then_inc(o_psum, 1)

            pe.wait_ge(w_in, 16 * W_LOADS)
            pipeline(pe, step, 3, 2)

        @block.scalar
        def _(act):
            def step(t, p):
                o = 1 - p
                if inside(t + 2):
                    act.wait_ge(q_psum, t + 3)
                    nc.scalar.activation(qT[p][:, :], q_ps[:, 0:P], ACT.Identity, bias=cols[:, 0:1]).then_inc(q_sb, 1)
                if inside(t + 3):
                    act.wait_ge(xT_psum, t + 4)
                    nc.scalar.activation(xnT[o][:, :], x_ps[:, 0:P], ACT.Copy).then_inc(xT_sb, 1)
                if inside(t):
                    act.wait_ge(bias_sb, t + 1)
                    nc.scalar.activation(probs[p][:, :], s_ps[p][:, 0:S2], ACT.Exp, scale=inv, bias=bias[:, p:p + 1],
                                         accum_out=sums[:, p:p + 1]).then_inc(exp_sb, 1)

            norm_coefficients(nc, g, act, None, ln_step, lnw)
            act.wait_ge(w_in, 16 * W_LOADS)
            pipeline(act, step, 3, 0)

        @block.vector
        def _(dve):
            vec = nc.vector

            def norm(t, p):
                vec.tensor_scalar(xn[p][:, :], g.x[:, t, :], g.rstd[:, bass.ds(t, 1)], g.shift[:, bass.ds(t, 1)],
                                  ALU.mult, ALU.add).then_inc(xn_ready, 1)

            def step(t, p):
                o = 1 - p
                if inside(t + 4):
                    wait(dve, xT_psum, t + 3)
                    norm(t + 4, p)
                if inside(t + 1):
                    wait(dve, bias_sb, t)
                    dve.wait_ge(qk_psum, t + 2)
                    vec.tensor_copy(qkT[o][:, :], k_ps[:, 0:P]).then_inc(qk_sb, 1)
                    vec.tensor_copy(c[o][:, :], k_ps[:, P:P + 1]).then_inc(qk_sb, 1)
                if inside(t):
                    dve.wait_ge(scores_psum, t + 1)
                    vec.tensor_reduce(neg[:, p, 0:1], s_ps[p][:, 0:S2], AX.X, ALU.max, negate=True).then_inc(max_sb, 1)
                    dve.wait_ge(max_sb, t + 1)
                    vec.tensor_scalar(neg[:, p, 1:2], neg[:, p, 0:1], c[p][:, :], inv, ALU.subtract, ALU.mult).then_inc(neg_sb, 1)
                    dve.wait_ge(neg_sb, t + 1)
                    vec.scalar_tensor_tensor(bias[:, p:p + 1], c[p][:, :], inv, neg[:, p, 1:2], ALU.mult, ALU.add)\
                       .then_inc(bias_sb, 1)
                if inside(t - 1):
                    dve.wait_ge(pT_psum, t)
                    vec.tensor_copy(pT[o][:, :, :], p_ps[:, 0:2 * P].rearrange("p (k q) -> p k q", k=2)).then_inc(pT_sb, 1)
                    vec.tensor_copy(pT_l[o][:, :], p_ps[0:1, 2 * P:3 * P]).then_inc(pT_sb, 1)
                    wait(dve, x_sb, t - 2)
                    vec.reciprocal(rsum[:, o:o + 1], sums[:, o:o + 1]).then_inc(rsum_sb, 1)
                if inside(t - 2):
                    dve.wait_ge(o_psum, t - 1)
                    dve.wait_ge(rsum_sb, t - 1)
                    vec.scalar_tensor_tensor(g.x[:, t - 2, :], o_ps[:, 0:D], rsum[:, p:p + 1], g.x[:, t - 2, :],
                                             ALU.mult, ALU.add).then_inc(x_sb, 1)

            norm_coefficients(nc, g, None, dve, ln_step, lnw)
            pipeline(dve, step, 4, 2)
            dve.wait_ge(x_sb, T)


DI, NS, TAPS = 256, 16, 4
DB = DI // P
XW = 1 + 2 * NS
NH = NS // 2
TINY = float(np.exp(-20.0))
LN_Q = 4


def stage_scan1(nc, g):
    with ExitStack() as ctx:
        sb = tensor_makers(nc, ctx, "sc")[0]
        uz = sb("uz", [P, T, 2 * DI])
        dt = sb("dt", [P, T, DI])
        xd = sb("xd", [P, T, XW])
        scan_inputs(nc, g, uz, dt, xd)
        scan_states(nc, g, uz, dt, xd)
        scan_output(nc, g, uz, dt)


def scan_inputs(nc, g, uz, dt, xd):
    with ExitStack() as ctx:
        sem = sem_maker(nc, g, "si")
        sb, ps = tensor_makers(nc, ctx, "si")
        w_in_T = sb("w_in_T", [P, 2 * DI])
        taps = sb("taps", [P, TAPS, DI])
        w_c = sb("w_c", [P, TAPS, DI])
        w_x = sb("w_x", [P, DB, XW])
        w_dt, b_dt = sb("w_dt", [P, DI]), sb("b_dt", [P, DI])
        cb3, c_rest, c_f = sb("cb3", [3, DI]), sb("c_rest", [3, DI]), sb("c_f", [3, DI])
        c_hi, cb = sb("c_hi", [3, DI], BF16), sb("cb", [3, DI], BF16)
        ones3, rowmask = sb("ones3", [3, P], BF16), sb("rowmask", [3, 3])
        lnw = sb("lnw", [P, 4, T])
        xn = [sb(f"xn{p}", [P, D]) for p in range(2)]
        xnT = [sb(f"xnT{p}", [P, P]) for p in range(TAPS)]
        u = [sb(f"u{p}", [P, 2 * DI]) for p in range(2)]
        uT = [sb(f"uT{p}", [P, DI]) for p in range(2)]
        soft = sb("soft", [P, T, DI])

        x_ps, c_ps, u_ps, d_ps = (ps(n, [P, BANK]) for n in ("x_ps", "c_ps", "u_ps", "d_ps"))
        c_ps = [c_ps, ps("c_ps1", [P, BANK])]

        x_in, w_in, stats, ln_step, prep = (sem(n) for n in ("x_in", "w_in", "stats", "ln_step", "prep"))
        xn_ready, xT_psum, xT_sb, conv_psum, u_sb = (sem(n) for n in ("xn_ready", "xT_psum", "xT_sb", "conv_psum", "u_sb"))
        uz_sb, uT_psum, uT_sb, xd_psum, xd_sb, dt_sb = (sem(n) for n in ("uz_sb", "uT_psum", "uT_sb", "xd_psum", "xd_sb", "dt_sb"))
        waited, abs_sb, exp_sb, ln_sb, soft_sb, clip_sb = (sem(n) for n in ("waited", "abs_sb", "exp_sb", "ln_sb", "soft_sb", "clip_sb"))
        block = ctx.enter_context(nc.Block())
        W_LOADS = 7
        QT = T // LN_Q

        @block.sync
        def _(sp):
            sp.dma_start(g.x[:, :, :], g.x_mid).then_inc(x_in, 16)
            sp.dma_start(w_in_T[:, :], g.dram["L1_attn_W_in_T"]).then_inc(w_in, 16)
            sp.dma_start(taps[:, :, :].rearrange("p k e -> p (k e)"),
                         g.dram["L1_conv_T"].to_broadcast([P, TAPS * DI])).then_inc(w_in, 16)
            sp.dma_start(w_x[:, :, :], g.dram["L1_attn_W_x_T"].rearrange("(c p) n -> p c n", p=P)).then_inc(w_in, 16)
            sp.dma_start(w_dt[:, :], g.dram["L1_attn_W_dt_T"].to_broadcast([P, DI])).then_inc(w_in, 16)
            sp.dma_start(b_dt[:, :], g.dram["L1_attn_b_dt"].rearrange("(a n) -> a n", a=1).to_broadcast([P, DI])).then_inc(w_in, 16)
            sp.dma_start(cb3[:, :], g.dram["L1_attn_conv_b"].rearrange("(a n) -> a n", a=1).to_broadcast([3, DI])).then_inc(w_in, 16)
            sp.dma_start(rowmask[:, :], g.dram["c_rowmask"]).then_inc(w_in, 16)

        @block.tensor
        def _(pe):
            mm, tr = nc.tensor.matmul, nc.tensor.transpose

            def step(t, p):
                if inside(t + 2):
                    pe.wait_ge(xn_ready, t + 3)
                    wait(pe, xT_sb, t + 2)
                    tr(x_ps[:, 0:P], xn[p % 2][:, :], g.ident[:, :]).then_inc(xT_psum, 1)
                if inside(t + 1):
                    pe.wait_ge(xT_sb, t + 2)
                    wait(pe, u_sb, t)
                    out = c_ps[(p + 1) % 2]
                    for j in range(TAPS):
                        if inside(t + 1 - j):
                            mm(out[:, 0:DI], xnT[(p + 1 - j) % TAPS][:, :], w_c[:, TAPS - 1 - j, :], start=(j == 0), stop=False)
                    mm(out[:, 0:DI], ones3[:, :], cb[:, :], start=False, stop=True)
                    mm(out[:, DI:2 * DI], xnT[(p + 1) % TAPS][:, :], w_in_T[:, DI:2 * DI], start=True, stop=True)\
                      .then_inc(conv_psum, 1)
                if inside(t):
                    pe.wait_ge(u_sb, t + 1)
                    wait(pe, uT_sb, t)
                    for c in range(DB):
                        ins = tr(u_ps[:, c * P:(c + 1) * P], u[p % 2][:, c * P:(c + 1) * P], g.ident[:, :])
                    ins.then_inc(uT_psum, 1)
                if inside(t - 1):
                    pe.wait_ge(uT_sb, t)
                    wait(pe, xd_sb, t - 1)
                    for c in range(DB):
                        ins = mm(d_ps[:, 0:XW], uT[(p + 1) % 2][:, c * P:(c + 1) * P], w_x[:, c, :], start=(c == 0), stop=(c == DB - 1))
                    ins.then_inc(xd_psum, 1)

            pe.wait_ge(prep, TAPS + 1 + 9)
            pipeline(pe, step, 2, 1, TAPS)

        @block.scalar
        def _(act):
            def step(t, p):
                if inside(t + 1):
                    act.wait_ge(conv_psum, t + 2)
                    wait(act, uz_sb, t)
                    nc.scalar.activation(u[(p + 1) % 2][:, :], c_ps[(p + 1) % 2][:, :], ACT.Silu).then_inc(u_sb, 1)
                if inside(t + 2):
                    act.wait_ge(xT_psum, t + 3)
                    nc.scalar.activation(xnT[(p + 2) % TAPS][:, :], x_ps[:, 0:P], ACT.Copy).then_inc(xT_sb, 1)

            norm_coefficients(nc, g, act, None, ln_step, lnw)
            pipeline(act, step, 2, 0, TAPS)
            act.wait_ge(dt_sb, T)
            for q in range(LN_Q):
                s = slice(q * QT, (q + 1) * QT)
                nc.scalar.activation(soft[:, s, :], dt[:, s, :], ACT.Abs).then_inc(abs_sb, 1)
            for q in range(LN_Q):
                s = slice(q * QT, (q + 1) * QT)
                act.wait_ge(abs_sb, q + 1)
                nc.scalar.activation(soft[:, s, :], soft[:, s, :], ACT.Exp, scale=-1.0).then_inc(exp_sb, 1)
            for q in range(LN_Q):
                s = slice(q * QT, (q + 1) * QT)
                act.wait_ge(exp_sb, q + 1)
                nc.scalar.activation(soft[:, s, :], soft[:, s, :], ACT.Ln, bias=1.0).then_inc(ln_sb, 1)

        @block.gpsimd
        def _(pool):
            def keep(t, p):
                pool.wait_ge(u_sb, t + 1)
                pool.sem_inc(waited, 1)
                nc.gpsimd.tensor_copy(uz[:, t, :], u[p][:, :]).then_inc(uz_sb, 1)

            with pool.Fori(0, T // 2) as i:
                keep(i * 2, 0)
                keep(i * 2 + 1, 1)
            pool.wait_ge(uz_sb, T)

        @block.vector
        def _(dve):
            vec = nc.vector

            def step(t, p):
                if inside(t + 3):
                    wait(dve, xT_psum, t + 2)
                    vec.tensor_scalar(xn[(p + 1) % 2][:, :], g.x[:, t + 3, :], g.rstd[:, bass.ds(t + 3, 1)],
                                      g.shift[:, bass.ds(t + 3, 1)], ALU.mult, ALU.add).then_inc(xn_ready, 1)
                if inside(t):
                    dve.wait_ge(uT_psum, t + 1)
                    vec.tensor_copy(uT[p % 2][:, :], u_ps[:, 0:DI]).then_inc(uT_sb, 1)
                if inside(t - 1):
                    dve.wait_ge(xd_psum, t)
                    vec.tensor_copy(xd[:, t - 1, :], d_ps[:, 0:XW]).then_inc(xd_sb, 1)
                    dve.wait_ge(xd_sb, t)
                    vec.scalar_tensor_tensor(dt[:, t - 1, :], w_dt[:, :], xd[:, t - 1, 0:1], b_dt[:, :],
                                             ALU.mult, ALU.add).then_inc(dt_sb, 1)

            dve.wait_ge(x_in, 16)
            with dve.Fori(0, T) as t:
                vec.bn_stats(g.bn[:, t, :], g.x[:, t, :]).then_inc(stats, 1)
            dve.wait_ge(stats, T)
            norm_coefficients(nc, g, None, dve, ln_step, lnw)
            dve.wait_ge(w_in, 16 * W_LOADS)
            for k in range(TAPS):
                vec.tensor_tensor(w_c[:, k, :], w_in_T[:, 0:DI], taps[:, k, :], ALU.mult).then_inc(prep, 1)
            vec.memset(ones3[:, :], 1.0).then_inc(prep, 1)
            split_row(vec, dve, prep, TAPS + 1, cb3[:, :], rowmask, (c_hi[:, :], c_rest[:, :], c_f[:, :]), cb[:, :])
            pipeline(dve, step, 3, 1, TAPS)
            for q in range(LN_Q):
                s = slice(q * QT, (q + 1) * QT)
                dve.wait_ge(ln_sb, q + 1)
                vec.scalar_tensor_tensor(dt[:, s, :], dt[:, s, :], 0.0, soft[:, s, :], ALU.max, ALU.add).then_inc(soft_sb, 1)
                dve.wait_ge(soft_sb, q + 1)
                vec.tensor_scalar(dt[:, s, :], dt[:, s, :], 1e-4, 10.0, ALU.max, ALU.min).then_inc(clip_sb, 1)
            dve.wait_ge(clip_sb, LN_Q)


def scan_states(nc, g, uz, dt, xd):
    with ExitStack() as ctx:
        sem = sem_maker(nc, g, "ss")
        sb, ps = tensor_makers(nc, ctx, "ss")
        a = sb("a", [P, NS])
        dtu = [sb(f"dtu{p}", [P, DI]) for p in range(2)]
        decay = [sb(f"decay{k}", [P, NH, DI]) for k in range(2)]
        come = [sb(f"come{k}", [P, NH, DI]) for k in range(2)]
        h = [[sb(f"h{k}{p}", [P, NH, DI]) for p in range(2)] for k in range(2)]
        diag = [sb(f"diag{k}", [P, NH, P]) for k in range(2)]
        y_ps = [ps(f"y_ps{p}", [P, BANK]) for p in range(2)]

        a_in, a_step = sem("a_in"), sem("a_step")
        dtu_sb, raw_sb, come_sb, diag_sb, waited = (sem(n) for n in ("dtu_sb", "raw_sb", "come_sb", "diag_sb", "waited"))
        decay_sb, kept_sb, sum_sb, h_sb, y_psum, y_sb = (sem(n) for n in ("decay_sb", "kept_sb", "sum_sb", "h_sb", "y_psum", "y_sb"))
        waited_act = sem("waited_act")
        block = ctx.enter_context(nc.Block())

        @block.sync
        def _(sp):
            sp.dma_start(a[:, :], g.dram["L1_attn_A_log"].rearrange("(a n) -> a n", a=1).to_broadcast([P, NS])).then_inc(a_in, 16)

        @block.gpsimd
        def _(pool):
            def unit(t, p, k):
                if k == 0:
                    nc.gpsimd.tensor_tensor(dtu[p][:, :], dt[:, t, :], uz[:, t, 0:DI], ALU.mult).then_inc(dtu_sb, 1)
                pool.wait_ge(dtu_sb, t + 1)
                wait(pool, sum_sb, t * 2 + k - 1)
                b = xd[:, t, 1 + k * NH:1 + (k + 1) * NH]
                nc.gpsimd.tensor_tensor(come[k][:, :, :], dtu[p][:, :].unsqueeze(1).to_broadcast([P, NH, DI]),
                                        b.unsqueeze(2).to_broadcast([P, NH, DI]), ALU.mult).then_inc(raw_sb, 1)
                pool.wait_ge(raw_sb, t * 2 + k + 1)
                pool.sem_inc(waited, 1)
                nc.gpsimd.tensor_scalar(come[k][:, :, :], come[k][:, :, :], 10.0, -10.0, ALU.min, ALU.max).then_inc(come_sb, 1)
                wait(pool, y_psum, t * 2 + k - 1)
                c = xd[:, t, 1 + NS + k * NH:1 + NS + (k + 1) * NH]
                nc.gpsimd.tensor_tensor(diag[k][:, :, :], g.ident[:, :].unsqueeze(1).to_broadcast([P, NH, P]),
                                        c.unsqueeze(2).to_broadcast([P, NH, P]), ALU.mult).then_inc(diag_sb, 1)

            def position(t, p):
                unit(t, p, 0)
                unit(t, p, 1)

            position(0, 0)
            position(1, 1)
            with pool.Fori(1, T // 2) as i:
                position(i * 2, 0)
                position(i * 2 + 1, 1)

        @block.scalar
        def _(act):
            def decays(t, k):
                wait(act, sum_sb, t * 2 + k - 1)
                act.sem_inc(waited_act, 1)
                for n in range(NH):
                    m = k * NH + n
                    ins = nc.scalar.activation(decay[k][:, n, :], dt[:, t, :], ACT.Exp, scale=a[:, m:m + 1])
                ins.then_inc(decay_sb, 1)

            def keep_y(t, p):
                act.wait_ge(y_psum, t * 2 + 2)
                act.wait_ge(dtu_sb, t + 1)
                act.sem_inc(waited_act, 1)
                nc.scalar.activation(dt[:, t, :], y_ps[p][:, 0:DI], ACT.Copy).then_inc(y_sb, 1)

            act.wait_ge(a_step, 1)
            nc.scalar.activation(a[:, :], a[:, :], ACT.Exp).then_inc(a_step, 1)
            act.wait_ge(a_step, 3)
            decays(1, 0)
            decays(1, 1)
            keep_y(0, 0)
            with act.Fori(1, T // 2) as i:
                decays(i * 2, 0)
                decays(i * 2, 1)
                keep_y(i * 2 - 1, 1)
                decays(i * 2 + 1, 0)
                decays(i * 2 + 1, 1)
                keep_y(i * 2, 0)
            keep_y(T - 1, 1)

        @block.vector
        def _(dve):
            vec = nc.vector

            def unit(t, p, k):
                n = t * 2 + k
                dve.wait_ge(decay_sb, n - 1)
                wait(dve, h_sb, n - 1)
                vec.scalar_tensor_tensor(decay[k][:, :, :], decay[k][:, :, :], TINY, h[k][1 - p][:, :, :],
                                         ALU.max, ALU.mult).then_inc(kept_sb, 1)
                dve.wait_ge(come_sb, n + 1)
                dve.wait_ge(kept_sb, n - 1)
                wait(dve, y_psum, n - 3)
                vec.tensor_tensor(h[k][p][:, :, :], decay[k][:, :, :], come[k][:, :, :], ALU.add).then_inc(sum_sb, 1)
                dve.wait_ge(sum_sb, n + 1)
                vec.tensor_scalar(h[k][p][:, :, :], h[k][p][:, :, :], 100.0, -100.0, ALU.min, ALU.max).then_inc(h_sb, 1)

            dve.wait_ge(a_in, 16)
            vec.tensor_scalar(a[:, :], a[:, :], 5.0, None, ALU.min).then_inc(a_step, 1)
            dve.wait_ge(a_step, 2)
            vec.tensor_scalar(a[:, :], a[:, :], -1.0, None, ALU.mult).then_inc(a_step, 1)
            for k in range(2):
                dve.wait_ge(come_sb, k + 1)
                vec.tensor_copy(h[k][0][:, :, :], come[k][:, :, :]).then_inc(sum_sb, 1)
                dve.wait_ge(sum_sb, k + 1)
                vec.tensor_scalar(h[k][0][:, :, :], h[k][0][:, :, :], 100.0, -100.0, ALU.min, ALU.max).then_inc(h_sb, 1)
            unit(1, 1, 0)
            unit(1, 1, 1)
            with dve.Fori(1, T // 2) as i:
                for p in range(2):
                    for k in range(2):
                        unit(i * 2 + p, p, k)

        @block.tensor
        def _(pe):
            def unit(t, p, k):
                pe.wait_ge(h_sb, t * 2 + k + 1)
                pe.wait_ge(diag_sb, t * 2 + k + 1)
                if k == 0:
                    wait(pe, y_sb, t - 1)
                for n in range(NH):
                    ins = nc.tensor.matmul(y_ps[p][:, 0:DI], diag[k][:, n, :], h[k][p][:, n, :],
                                           start=(k == 0 and n == 0), stop=(k == 1 and n == NH - 1))
                ins.then_inc(y_psum, 1)

            for t in range(2):
                unit(t, t, 0)
                unit(t, t, 1)
            with pe.Fori(1, T // 2) as i:
                for p in range(2):
                    for k in range(2):
                        unit(i * 2 + p, p, k)


def scan_output(nc, g, uz, y):
    NGS = T // LN_Q
    with ExitStack() as ctx:
        sem = sem_maker(nc, g, "so")
        sb, ps = tensor_makers(nc, ctx, "so")
        ln_g, ln_b, d_p = sb("ln_g", [P, DI]), sb("ln_b", [P, DI]), sb("d_p", [P, DI])
        w_o = sb("w_o", [P, DB, D])
        lnw = sb("lnw", [P, 4, T])
        skip = [sb(f"skip{p}", [P, LN_Q, DI]) for p in range(2)]
        v = [sb(f"v{p}", [P, LN_Q, DI]) for p in range(2)]
        vT = [sb(f"vT{p}", [P, 2, BANK]) for p in range(2)]
        t_ps = ps("t_ps", [P, 2, BANK])
        o_ps = ps("o_ps", [P, BANK])
        w_in, stats, ln_step = sem("w_in"), sem("stats"), sem("ln_step")
        du_sb, skip_sb, yn_sb, mul_sb, add_sb, v_sb = (sem(n) for n in ("du_sb", "skip_sb", "yn_sb", "mul_sb", "add_sb", "v_sb"))
        vT_psum, vT_sb, o_psum, x_sb, moments = (sem(n) for n in ("vT_psum", "vT_sb", "o_psum", "x_sb", "moments"))
        block = ctx.enter_context(nc.Block())
        W_LOADS = 4

        def every(row):
            return row[:, :].unsqueeze(1).to_broadcast([P, LN_Q, DI])

        @block.sync
        def _(sp):
            for dst, name in ((ln_g, "ln_g"), (ln_b, "ln_b"), (d_p, "D_param")):
                row = g.dram[f"L1_attn_{name}"].rearrange("(a n) -> a n", a=1)
                sp.dma_start(dst[:, :], row.to_broadcast([P, DI])).then_inc(w_in, 16)
            sp.dma_start(w_o[:, :, :], g.dram["L1_attn_W_out_T"].rearrange("(c p) n -> p c n", p=P)).then_inc(w_in, 16)

        @block.gpsimd
        def _(pool):
            def skips(n, p):
                wait(pool, add_sb, n - 1)
                nc.gpsimd.tensor_tensor(skip[p][:, :, :], uz[:, bass.ds(n * LN_Q, LN_Q), 0:DI], every(d_p), ALU.mult).then_inc(du_sb, 1)
                pool.wait_ge(du_sb, n + 1)
                nc.gpsimd.tensor_tensor(skip[p][:, :, :], skip[p][:, :, :], every(ln_b), ALU.add).then_inc(skip_sb, 1)

            pool.wait_ge(w_in, 16 * W_LOADS)
            skips(0, 0)
            skips(1, 1)
            with pool.Fori(1, NGS // 2) as i:
                skips(i * 2, 0)
                skips(i * 2 + 1, 1)

        @block.vector
        def _(dve):
            vec = nc.vector

            def gated(n, p):
                wait(dve, vT_psum, n - 1)
                for j in range(LN_Q):
                    t = n * LN_Q + j
                    vec.tensor_scalar(v[p][:, j, :], y[:, t, :], g.rstd[:, bass.ds(t, 1)], g.shift[:, bass.ds(t, 1)],
                                      ALU.mult, ALU.add).then_inc(yn_sb, 1)
                dve.wait_ge(yn_sb, n * LN_Q + LN_Q)
                vec.tensor_tensor(v[p][:, :, :], v[p][:, :, :], every(ln_g), ALU.mult).then_inc(mul_sb, 1)
                dve.wait_ge(mul_sb, n + 1)
                dve.wait_ge(skip_sb, n + 1)
                vec.tensor_tensor(v[p][:, :, :], v[p][:, :, :], skip[p][:, :, :], ALU.add).then_inc(add_sb, 1)
                dve.wait_ge(add_sb, n + 1)
                vec.tensor_tensor(v[p][:, :, :], v[p][:, :, :], uz[:, bass.ds(n * LN_Q, LN_Q), DI:2 * DI], ALU.mult)\
                   .then_inc(v_sb, 1)

            def add_out(n):
                dve.wait_ge(o_psum, n + 1)
                xs = g.x[:, bass.ds(n * LN_Q, LN_Q), :]
                vec.tensor_tensor(xs, xs, o_ps[:, :].rearrange("p (k d) -> p k d", k=LN_Q), ALU.add).then_inc(x_sb, 1)
                dve.wait_ge(x_sb, n + 1)
                for j in range(LN_Q):
                    vec.bn_stats(g.bn[:, n * LN_Q + j, :], g.x[:, n * LN_Q + j, :]).then_inc(moments, 1)

            with dve.Fori(0, T) as t:
                vec.bn_stats(g.bn[:, t, :], y[:, t, :]).then_inc(stats, 1)
            dve.wait_ge(stats, T)
            norm_coefficients(nc, g, None, dve, ln_step, lnw, DI)
            dve.wait_ge(w_in, 16 * W_LOADS)
            gated(0, 0)
            gated(1, 1)
            add_out(0)
            with dve.Fori(1, NGS // 2) as i:
                gated(i * 2, 0)
                add_out(i * 2 - 1)
                gated(i * 2 + 1, 1)
                add_out(i * 2)
            add_out(NGS - 1)
            dve.wait_ge(moments, T)

        @block.scalar
        def _(act):
            norm_coefficients(nc, g, act, None, ln_step, lnw, DI)

            def copy(n, p):
                act.wait_ge(vT_psum, n + 1)
                for b in range(2):
                    nc.scalar.activation(vT[p][:, b, :], t_ps[:, b, :], ACT.Copy).then_inc(vT_sb, 1)

            with act.Fori(0, NGS // 2) as i:
                copy(i * 2, 0)
                copy(i * 2 + 1, 1)

        @block.tensor
        def _(pe):
            mm, tr = nc.tensor.matmul, nc.tensor.transpose

            def turn(n, p):
                pe.wait_ge(v_sb, n + 1)
                wait(pe, vT_sb, n * 2)
                for j in range(LN_Q):
                    for c in range(DB):
                        ins = tr(t_ps[:, j // 2, (j % 2 * DB + c) * P:(j % 2 * DB + c + 1) * P],
                                 v[p][:, j, c * P:(c + 1) * P], g.ident[:, :])
                ins.then_inc(vT_psum, 1)

            def project(n, p):
                pe.wait_ge(vT_sb, n * 2 + 2)
                wait(pe, x_sb, n)
                for j in range(LN_Q):
                    for c in range(DB):
                        k = j % 2 * DB + c
                        ins = mm(o_ps[:, j * D:(j + 1) * D], vT[p][:, j // 2, k * P:(k + 1) * P], w_o[:, c, :],
                                 start=(c == 0), stop=(c == DB - 1))
                ins.then_inc(o_psum, 1)

            pe.wait_ge(w_in, 16 * W_LOADS)
            turn(0, 0)
            turn(1, 1)
            project(0, 0)
            with pe.Fori(1, NGS // 2) as i:
                turn(i * 2, 0)
                project(i * 2 - 1, 1)
                turn(i * 2 + 1, 1)
                project(i * 2, 0)
            project(NGS - 1, 1)


ME, MA = 12, 64
NR, TOP1 = 3, 3
MC = 2 * ME


def stage_experts1(nc, g):
    with ExitStack() as ctx:
        sem = sem_maker(nc, g, "e1")
        sb, ps = tensor_makers(nc, ctx, "e1")
        w_a, w_z = sb("w_a", [P, MA]), sb("w_z", [MA, NR * ME])
        w = sb("w", [P, MC, P])
        b2 = sb("b2", [ME, D])
        spread = sb("spread", [100, ME, P], BF16)
        lnw = sb("lnw", [P, 4, T])
        xn = sb("xn", [P, GT, D])
        xnT = [sb(f"xnT{p}", [P, TOK]) for p in range(2)]
        xaT = sb("xaT", [MA, TOK])
        rows = GT * NR
        z = sb("z", [P, rows, ME + 8 - TOP1])
        r = {"sorted": sb("sorted", [P, rows, 8]), "taken": sb("taken", [P, rows, 8]),
             "marked": sb("marked", [P, rows, ME + 8 - TOP1]), "sel": sb("sel", [P, rows, ME])[:, :, :]}
        ez, total, weight = sb("ez", [P, rows, ME]), sb("total", [P, rows]), sb("weight", [P, GT, NR, ME])
        part_hi, part_rest = sb("part_hi", [P, GT, 2, ME], BF16), sb("part_rest", [P, GT, 2, ME])
        parts = sb("parts", [P, GT, 2, 64])
        wT = [sb(f"wT{p}", [P, TOK], BF16) for p in range(2)]
        w3T = [sb(f"w3T{p}", [ME, TOK]) for p in range(2)]
        scaled = [sb(f"scaled{p}", [P, TOK]) for p in range(2)]
        hT, yT = sb("hT", [P, TOK]), sb("yT", [P, TOK])

        m_ps, n_ps = ps("m_ps", [P, BANK]), ps("n_ps", [P, BANK])
        w_ps = [ps(f"w_ps{p}", [P, BANK]) for p in range(2)]
        h_ps, y_ps, o_ps = ps("h_ps", [P, BANK]), ps("y_ps", [P, BANK]), ps("o_ps", [P, BANK])

        w_in, ln_step, ready = sem("w_in"), sem("ln_step"), sem("ready")
        xn_ready, xT_psum, xT_sb, xa_psum, xa_sb = (sem(n) for n in ("xn_ready", "xT_psum", "xT_sb", "xa_psum", "xa_sb"))
        z_psum, route, exp_sb, waited = (sem(n) for n in ("z_psum", "route", "exp_sb", "waited"))
        wT_psum, wT_sb = sem("wT_psum"), sem("wT_sb")
        w_psum, scaled_sb, product, h_sb, y_sb = (sem(n) for n in ("w_psum", "scaled_sb", "product", "h_sb", "y_sb"))
        b2_done, o_psum, x_sb, x_out = (sem(n) for n in ("b2_done", "o_psum", "x_sb", "x_out"))
        W_LOADS = 7
        TOP_STEPS = 2 * rows + 3
        ROUTE_STEPS = TOP_STEPS + 1 + 4 + 6
        block = ctx.enter_context(nc.Block())

        @block.sync
        def _(sp):
            sp.dma_start(w_a[:, :], g.dram["L1_ffn_P_w_T"]).then_inc(w_in, 16)
            sp.dma_start(w_z[:, :], g.dram["L1_U_T"]).then_inc(w_in, 16)
            sp.dma_start(spread[0:3 * ME, :, :].rearrange("r e n -> r (e n)"), g.dram["c_spread1"]).then_inc(w_in, 16)
            sp.dma_start(spread[64:64 + 3 * ME, :, :].rearrange("r e n -> r (e n)"), g.dram["c_spread1"]).then_inc(w_in, 16)
            sp.dma_start(w[:, 0:ME, :], g.dram["L1_W1_T"]).then_inc(w_in, 16)
            sp.dma_start(w[:, ME:MC, :], g.dram["L1_W2_T"]).then_inc(w_in, 16)
            sp.dma_start(b2[:, :], g.dram["L1_ffn_b2"]).then_inc(w_in, 16)
            with sp.Fori(0, NG) as n:
                sp.wait_ge(x_sb, n + 1)
                sp.dma_start(g.out[:, bass.ds(n * GT, GT), :], g.x[:, bass.ds(n * GT, GT), :]).then_inc(x_out, 16)
            sp.wait_ge(x_out, 16 * NG)

        @block.tensor
        def _(pe):
            mm, tr = nc.tensor.matmul, nc.tensor.transpose

            def turn_x(n):
                pe.wait_ge(xn_ready, n * GT + GT)
                for k in range(GT):
                    ins = tr(m_ps[:, k * P:(k + 1) * P], xn[:, k, :], g.ident[:, :])
                ins.then_inc(xT_psum, 1)

            def address(n, p):
                pe.wait_ge(xT_sb, n + 1)
                mm(m_ps[0:MA, :], w_a[:, :], xnT[p][:, :], start=True, stop=True).then_inc(xa_psum, 1)

            def rank(n):
                pe.wait_ge(xa_sb, n + 1)
                for k in range(GT):
                    ins = mm(m_ps[:, k * NR * ME:(k + 1) * NR * ME], xaT[:, k * P:(k + 1) * P], w_z[:, :], start=True, stop=True)
                ins.then_inc(z_psum, 1)

            def turn_weights(n):
                pe.wait_ge(route, n * ROUTE_STEPS + ROUTE_STEPS)
                for k in range(GT):
                    tr(m_ps[:, k * P:(k + 1) * P], parts[:, k, :, :], g.ident[:, :])
                for k in range(GT):
                    ins = tr(n_ps[0:ME, k * P:(k + 1) * P], weight[:, k, 2, :], g.ident[:, :])
                ins.then_inc(wT_psum, 1)

            def spread_weight(n, p, j):
                if j == 0:
                    pe.wait_ge(wT_sb, n * 2 + 2)
                wait(pe, scaled_sb, n * MC + j - 1)
                q = 64 * (j // ME)
                mm(w_ps[j % 2][:, :], spread[q:q + 3 * ME, j % ME, :], wT[p][q:q + 3 * ME, :], start=True, stop=True)\
                  .then_inc(w_psum, 1)

            def expert(n, j):
                pe.wait_ge(scaled_sb, n * MC + j + 1)
                if j == 0:
                    wait(pe, h_sb, n)
                mm([h_ps, y_ps][j // ME][:, :], w[:, j, :], scaled[j % 2][:, :], start=(j == 0),
                   stop=(j == ME - 1 or j == MC - 1)).then_inc(product, 1)

            def bias(n, p):
                wait(pe, y_sb, n)
                mm(y_ps[:, :], b2[:, :], w3T[p][:, :], start=True, stop=False).then_inc(b2_done, 1)

            def turn_out(n):
                pe.wait_ge(y_sb, n + 1)
                wait(pe, x_sb, n)
                for k in range(GT):
                    ins = tr(o_ps[:, k * P:(k + 1) * P], yT[:, k * P:(k + 1) * P], g.ident[:, :])
                ins.then_inc(o_psum, 1)

            def group(n, p, prev, nxt):
                for j in range(MC):
                    spread_weight(n, p, j)
                    if j:
                        expert(n, j - 1)
                    elif prev:
                        expert(n - 1, MC - 1)
                    if j == 1:
                        bias(n, p)
                    if prev and j == 2:
                        turn_out(n - 1)
                    if nxt and j == 3:
                        turn_x(n + 1)
                    if nxt and j == 5:
                        address(n + 1, 1 - p)
                    if nxt and j == 7:
                        rank(n + 1)
                    if nxt and j == 20:
                        turn_weights(n + 1)

            pe.wait_ge(w_in, 16 * W_LOADS)
            turn_x(0)
            address(0, 0)
            rank(0)
            turn_weights(0)
            group(0, 0, False, True)
            with pe.Fori(0, NG // 2 - 1) as i:
                group(i * 2 + 1, 1, True, True)
                group(i * 2 + 2, 0, True, True)
            group(NG - 1, 1, True, False)
            expert(NG - 1, MC - 1)
            turn_out(NG - 1)

        @block.scalar
        def _(act):
            def copy_address(n):
                act.wait_ge(xa_psum, n + 1)
                nc.scalar.activation(xaT[:, :], m_ps[0:MA, :], ACT.Copy).then_inc(xa_sb, 1)

            def exps(n):
                act.wait_ge(route, n * ROUTE_STEPS + TOP_STEPS + 1)
                nc.scalar.activation(ez[:, :, :], ez[:, :, :], ACT.Exp).then_inc(exp_sb, 1)

            def group(n, p, prev, nxt):
                if prev:
                    act.wait_ge(product, n * MC)
                    nc.scalar.activation(yT[:, :], y_ps[:, :], ACT.Copy).then_inc(y_sb, 1)
                if nxt:
                    copy_address(n + 1)
                act.wait_ge(product, n * MC + ME)
                nc.scalar.activation(hT[:, :], h_ps[:, :], ACT.Gelu).then_inc(h_sb, 1)
                if nxt:
                    exps(n + 1)

            norm_coefficients(nc, g, act, None, ln_step, lnw)
            copy_address(0)
            exps(0)
            group(0, 0, False, True)
            with act.Fori(1, NG - 1) as n:
                group(n, 0, True, True)
            group(NG - 1, 1, True, False)
            act.wait_ge(product, NG * MC)
            nc.scalar.activation(yT[:, :], y_ps[:, :], ACT.Copy).then_inc(y_sb, 1)

        @block.vector
        def _(dve):
            vec = nc.vector

            def norm(n):
                for k in range(GT):
                    t = n * GT + k
                    vec.tensor_scalar(xn[:, k, :], g.x[:, t, :], g.rstd[:, bass.ds(t, 1)], g.shift[:, bass.ds(t, 1)],
                                      ALU.mult, ALU.add).then_inc(xn_ready, 1)

            def copy_xT(n, p):
                dve.wait_ge(xT_psum, n + 1)
                vec.tensor_copy(xnT[p][:, :], m_ps[:, :]).then_inc(xT_sb, 1)

            def runner(n, start):
                done = [start]

                def run(ins, last=True):
                    ins.then_inc(route, 1)
                    done[0] += 1
                    if last:
                        dve.wait_ge(route, n * ROUTE_STEPS + done[0])
                return run, done

            def routing_top(n):
                run, done = runner(n, 0)
                dve.wait_ge(z_psum, n + 1)
                run(vec.tensor_copy(z[:, :, 0:ME], m_ps[:, 0:rows * ME].rearrange("p (k e) -> p k e", k=rows)))
                take_top(vec, run, lambda: dve.sem_inc(waited, 1), z[:, :, :], ME, TOP1, r)
                assert done[0] == TOP_STEPS
                run(vec.tensor_tensor(ez[:, :, :], z[:, :, 0:ME], r["sorted"][:, :, 0:1].to_broadcast([P, rows, ME]),
                                      ALU.subtract), last=False)

            def routing_weights(n):
                run, done = runner(n, TOP_STEPS + 1)
                dve.wait_ge(exp_sb, n + 1)
                flat = weight[:, :, :, :].rearrange("p k r e -> p (k r) e")
                run(vec.tensor_tensor(flat, r["sel"], ez[:, :, :], ALU.mult))
                run(vec.tensor_reduce(total[:, :], flat, AX.X, ALU.add))
                run(vec.reciprocal(total[:, :], total[:, :]))
                run(vec.tensor_tensor(flat, flat, total[:, :].unsqueeze(2).to_broadcast([P, rows, ME]), ALU.mult))
                split_three(vec, run, weight[:, :, 0:2, :], [parts[:, :, :, j * ME:(j + 1) * ME] for j in range(3)],
                            part_hi[:, :, :, :], part_rest[:, :, :, :])
                assert done[0] == ROUTE_STEPS

            def copy_weights(n, p):
                dve.wait_ge(wT_psum, n + 1)
                vec.tensor_copy(wT[p][:, :], m_ps[:, :]).then_inc(wT_sb, 1)
                vec.tensor_copy(w3T[p][:, :], n_ps[0:ME, :]).then_inc(wT_sb, 1)

            def scale(n, p, j):
                dve.wait_ge(w_psum, n * MC + j + 1)
                if j == ME:
                    dve.wait_ge(h_sb, n + 1)
                wait(dve, product, n * MC + j - 1)
                src = xnT[p] if j < ME else hT
                vec.tensor_tensor(scaled[j % 2][:, :], src[:, :], w_ps[j % 2][:, :], ALU.mult).then_inc(scaled_sb, 1)

            def add_out(n):
                dve.wait_ge(o_psum, n + 1)
                xs = g.x[:, bass.ds(n * GT, GT), :]
                vec.tensor_tensor(xs, xs, o_ps[:, :].rearrange("p (k d) -> p k d", k=GT), ALU.add).then_inc(x_sb, 1)

            def group(n, p, prev, nxt):
                for j in range(MC):
                    scale(n, p, j)
                    if nxt and j == 1:
                        norm(n + 1)
                    if prev and j == 2:
                        add_out(n - 1)
                    if nxt and j == 3:
                        copy_xT(n + 1, 1 - p)
                    if nxt and j == 8:
                        routing_top(n + 1)
                    if nxt and j == 15:
                        routing_weights(n + 1)
                    if nxt and j == 20:
                        copy_weights(n + 1, 1 - p)

            vec.memset(z[:, :, ME:], PAD).then_inc(ready, 1)
            vec.memset(r["taken"][:, :, TOP1:], PAD).then_inc(ready, 1)
            vec.memset(parts[:, :, :, :], 0.0).then_inc(ready, 1)
            norm_coefficients(nc, g, None, dve, ln_step, lnw)
            dve.wait_ge(ready, 3)
            norm(0)
            copy_xT(0, 0)
            routing_top(0)
            routing_weights(0)
            copy_weights(0, 0)
            group(0, 0, False, True)
            with dve.Fori(0, NG // 2 - 1) as i:
                group(i * 2 + 1, 1, True, True)
                group(i * 2 + 2, 0, True, True)
            group(NG - 1, 1, True, False)
            add_out(NG - 1)


STAGES = [stage_cross0, stage_mixer0, stage_experts0, stage_cross1, stage_scan1, stage_experts1]
HALFWAY = stage_scan1


def build(nc, dram, out):
    with ExitStack() as ctx:
        g = Ctx()
        g.dram = dram
        g.out = out
        g.sems = []
        g.x_mid = nc.dram_tensor("x_mid", (NB, S, D), F32).ap()
        sb = tensor_makers(nc, ctx, "all")[0]
        g.x = sb("x", [P, T, D])
        g.bn = sb("bn", [P, T, 6])
        g.rstd = sb("rstd", [P, T])
        g.shift = sb("shift", [P, T])
        g.ident = sb("ident", [P, P])
        stage_load(nc, g)
        for stage in STAGES:
            if stage is HALFWAY:
                clear_semaphores(nc, g)
            stage(nc, g)


PLAIN = ["L0_xattn_bq", "L0_xattn_bk", "L0_xattn_bv", "L0_xattn_bo", "L0_attn_u_w", "L0_attn_u_b", "L0_attn_v_w",
         "L0_attn_v_b", "L0_attn_o_w", "L0_attn_o_b", "L0_attn_pos_w", "L0_attn_pos_b", "L0_attn_lw0", "L0_attn_lw1",
         "L0_attn_lw2", "L0_attn_out_w", "L0_attn_out_b", "L1_xattn_Wk", "L1_xattn_bq", "L1_xattn_bk", "L1_attn_conv_b",
         "L1_attn_b_dt", "L1_attn_A_log", "L1_attn_D_param", "L1_attn_ln_g", "L1_attn_ln_b", "L1_ffn_b2"]
TURNED = ["L0_xattn_Wq", "L0_xattn_Wk", "L0_xattn_Wv", "L0_xattn_Wo", "L0_ffn_gate_weight", "L1_xattn_Wq", "L1_attn_W_in",
          "L1_attn_W_x", "L1_attn_W_dt", "L1_attn_W_out", "L1_ffn_P_w"]


def shape_constants():
    p = np.arange(P)
    r = np.arange(BT * CH)
    tail = np.zeros((BT * CH, 2, CH), np.float32)
    tail[r, 0, r // CH] = 1.0
    tail[r, 1, r % CH] = 1.0
    k, n = np.arange(S)[:, None], np.arange(S)[None, :]
    angle = np.pi * k * n / S
    re, im = np.cos(angle), -np.sin(angle)
    even = (-1.0) ** np.arange(S)

    def three(a, b, c, slot_b):
        m = np.stack([a, b, c])
        m[0, 0], m[1, 0], m[2, 0] = re[0] * (0.5 if slot_b < 0 else 1.0), even * abs(slot_b), 0.0
        return m

    sums = three(re + im, im, re, 1.0)
    mults = three(re, re + im, im - re, 1.0) * GAMMA ** np.arange(S)
    backs = three(re + im, -re, im, -0.5) / S
    eye = np.eye(BT)
    bfloat16 = np.dtype("bfloat16")
    return {
        "c_dft": np.einsum("ab,mkn->anmbk", eye, sums).reshape(P, 3, P).astype(np.float32),
        "c_idft": np.einsum("ab,mkn->akmbn", eye, backs).reshape(P, 3, P).astype(np.float32),
        "c_cdft": np.tile(mults.transpose(2, 0, 1)[:, :, None, :], (1, 1, BT, 1)).reshape(S, 3, P).astype(np.float32),
        "c_pos": np.arange(S, dtype=np.float32)[None, :],
        "c_spread0": np.tile(np.repeat(np.eye(NE), EI, axis=1), (3, 1)).astype(bfloat16),
        "c_spread1": np.tile(np.repeat(np.eye(ME), P, axis=1), (3, 1)).astype(bfloat16),
        "c_rowmask": np.eye(3, dtype=np.float32),
        "c_ident": np.eye(P, dtype=np.float32),
        "c_headmask": (p[:, None] // XD % CH == np.arange(CH)).astype(np.float32),
        "c_tailmask": tail,
        "c_onehot": (p[:, None] % S == p % S).astype(bfloat16),
    }


def kernel(**inputs):
    import concourse.bacc as bacc
    from concourse.bass_utils import run_bass_kernel_spmd

    nc = bacc.Bacc("TRN2", target_bir_lowering=False, num_devices=1)
    a = {k: np.asarray(v) for k, v in inputs.items()}
    arrays = {"x": a["x"], "mask": a["mask_1x1xSxS2_ik0"][0, 0], "ctx": a["ctx_1024"],
              "ctxT": np.transpose(a["ctx_1024"], (0, 2, 1))}
    for k in PLAIN:
        arrays[k] = a[k]
    for k in TURNED:
        arrays[k + "_T"] = a[k].T
    arrays["c_lb"] = np.concatenate([a[f"L0_attn_lb{n}"] for n in range(3)])[None, :]
    rows = {"gate": ("w_gate", "ws_gate"), "up": ("w_up", "ws_up")}
    for k, (routed, shared) in rows.items():
        arrays[f"L0_{k}_T"] = np.concatenate([a[f"L0_ffn_{routed}"].reshape(NE * EI, D), a[f"L0_ffn_{shared}"]]).T
    arrays["L0_down_T"] = np.concatenate([np.transpose(a["L0_ffn_w_down"], (0, 2, 1)).reshape(NE * EI, D),
                                          a["L0_ffn_ws_down"].T])
    arrays["L1_conv_T"] = a["L1_attn_conv_w"][:, 0, :].T.reshape(1, TAPS * DI)
    arrays["L1_U_T"] = np.concatenate([a[f"L1_ffn_U{n + 1}"] for n in range(NR)]).T
    for n in (1, 2):
        arrays[f"L1_W{n}_T"] = np.transpose(a[f"L1_ffn_W{n}"], (2, 0, 1))
    arrays.update(shape_constants())
    arrays = {k: np.ascontiguousarray(v) for k, v in arrays.items()}
    dram = {k: nc.dram_tensor(k, v.shape, mybir.dt.from_np(v.dtype), kind="ExternalInput").ap()
            for k, v in arrays.items()}
    out = nc.dram_tensor("out", (NB, S, D), F32, kind="ExternalOutput").ap()
    build(nc, dram, out)
    return run_bass_kernel_spmd(nc, [arrays], core_ids=[0]).results[0]["out"]
```

```python
import numpy as np
from contextlib import ExitStack

import concourse.bass as bass
import concourse.mybir as mybir

F32 = mybir.dt.float32
BF16 = mybir.dt.bfloat16
I32 = mybir.dt.int32
ALU = mybir.AluOpType
ACT = mybir.ActivationFunctionType
AX = mybir.AxisListType

P = 128
NB, S, D = 128, 32, 128
S2 = 257
BT = P // S
T = NB // BT
BANK = 512
EPS = 1e-5

XH, XD = 16, 8
CH = 4
UN = 2 * BT
MASKED = -3.0e38


class Ctx:
    pass


def sem_maker(nc, g, prefix):
    def sem(name):
        g.sems.append(nc.alloc_semaphore(f"{prefix}_{name}"))
        return g.sems[-1]
    return sem


def clear_semaphores(nc, g):
    nc.clear_and_free_semaphores(g.sems)
    nc.all_engine_barrier()
    g.sems = []


def tensor_makers(nc, ctx, prefix):
    def sb(name, shape, dt=F32):
        return ctx.enter_context(nc.sbuf_tensor(f"{prefix}_{name}", shape, dt))

    def ps(name, shape, dt=F32):
        return ctx.enter_context(nc.psum_tensor(f"{prefix}_{name}", shape, dt))
    return sb, ps


STATS = 8
XQ = 4
QT = T // XQ


def arrived_stats(nc, g, dve, x_in, done):
    for q in range(XQ):
        dve.wait_ge(x_in[q], 16)
        for t in range(q * QT, (q + 1) * QT):
            nc.vector.bn_stats(g.bn[:, t, :], g.x[:, t, :]).then_inc(done, 1)
    dve.wait_ge(done, T)


def norm_coefficients(nc, g, act, dve, step, w, width=D):
    if act is not None:
        act.wait_ge(step, 6)
        nc.scalar.activation(w[:, 1, :], w[:, 0, :], ACT.Sqrt).then_inc(step, 1)
        return
    m0, v0, m1, v1 = (g.bn[:, :, k] for k in (1, 2, 4, 5))
    nc.vector.tensor_tensor(w[:, 0, :], m0, m1, ALU.subtract).then_inc(step, 1)
    nc.vector.tensor_tensor(w[:, 1, :], v0, v1, ALU.add).then_inc(step, 1)
    nc.vector.tensor_tensor(w[:, 2, :], m0, m1, ALU.add).then_inc(step, 1)
    dve.wait_ge(step, 3)
    nc.vector.scalar_tensor_tensor(w[:, 3, :], w[:, 0, :], 0.25, w[:, 0, :], ALU.mult, ALU.mult).then_inc(step, 1)
    nc.vector.tensor_scalar(w[:, 1, :], w[:, 1, :], 1.0 / width, EPS, ALU.mult, ALU.add).then_inc(step, 1)
    dve.wait_ge(step, 5)
    nc.vector.tensor_tensor(w[:, 0, :], w[:, 1, :], w[:, 3, :], ALU.add).then_inc(step, 1)
    dve.wait_ge(step, 7)
    nc.vector.reciprocal(g.rstd[:, :], w[:, 1, :]).then_inc(step, 1)
    dve.wait_ge(step, 8)
    nc.vector.scalar_tensor_tensor(g.shift[:, :], w[:, 2, :], -0.5, g.rstd[:, :], ALU.mult, ALU.mult).then_inc(step, 1)
    dve.wait_ge(step, 9)


def tile_stats(nc, g, dve, x, done):
    with dve.Fori(0, T // STATS) as i:
        for k in range(STATS):
            t = i * STATS + k
            nc.vector.bn_stats(g.bn[:, t, :], x[:, t, :]).then_inc(done, 1)
    dve.wait_ge(done, T)


def stage_cross0(nc, g):
    scale = 1.0 / float(np.sqrt(XD))
    with ExitStack() as ctx:
        sem = sem_maker(nc, g, "x0")
        sb, ps = tensor_makers(nc, ctx, "x0")
        w_qkv = sb("w_qkv", [P, 3, D])
        w_o = sb("w_o", [P, D])
        w_om = sb("w_om", [P, CH, D])
        cols = sb("cols", [P, 3])
        bo_b = sb("bo_b", [P, D])
        bv_b = sb("bv_b", [P, P])
        out_bias = sb("out_bias", [P, D])
        one_col = sb("one_col", [P, 1])
        headmask = sb("headmask", [P, CH])
        headmask_s = sb("headmask_s", [P, XH])
        tailmask = sb("tailmask", [BT * CH, 2, CH])
        onehot = sb("onehot", [P, P], BF16)
        mask_i = sb("mask_i", [S, S2], I32)
        mask_b = sb("mask_b", [P, S2], BF16)
        ctx_t = [sb(f"ctx_t{p}", [P, BT * S2]) for p in range(2)]
        xn = sb("xn", [P, D])
        xnT = sb("xnT", [P, P])
        qT = sb("qT", [P, P])
        qblk = [sb(f"qblk{p}", [P, BT * CH * P]) for p in range(2)]
        kT = [sb(f"kT{p}", [P, BT * S2]) for p in range(2)]
        v = [sb(f"v{p}", [P, BT * 2 * D]) for p in range(2)]
        v_tail = [sb(f"v_tail{p}", [P, D]) for p in range(2)]
        neg_max = [sb(f"neg_max{p}", [P, BT * CH]) for p in range(2)]
        sums = [sb(f"sums{p}", [P, BT * CH]) for p in range(2)]
        probs = [sb(f"probs{p}", [P, BT * CH, S2]) for p in range(2)]
        rsum = sb("rsum", [P, BT * CH])
        pT = [sb(f"pT{p}", [P, BANK]) for p in range(2)]
        p_tail = sb("p_tail", [P, BT, P])
        o_raw = sb("o_raw", [P, BANK])
        o_norm = sb("o_norm", [P, CH, BT, S])
        ctx_last = sb("ctx_last", [P, BT, CH])
        rsum_b = sb("rsum_b", [P, BT * CH, S])
        lnw = sb("lnw", [P, 4, T])

        s_ps = [ps(f"s_ps{p}", [P, 2, BANK]) for p in range(2)]
        pT_ps = [ps(f"pT_ps{p}", [P, BANK]) for p in range(2)]
        o_ps = ps("o_ps", [P, BANK])
        m_ps = ps("m_ps", [P, BANK])

        w_in, mask_in = sem("w_in"), sem("mask_in")
        ctx_in = [sem(f"ctx_in{p}") for p in range(2)]
        one_ready = sem("one_ready")
        prep_dve, prep_pe, ln_step = sem("prep_dve"), sem("prep_pe"), sem("ln_step")
        xn_ready, xnT_psum, xnT_sb = sem("xn_ready"), sem("xnT_psum"), sem("xnT_sb")
        qT_psum, q_sb, qblk_sb = sem("qT_psum"), sem("q_sb"), sem("qblk_sb")
        k_psum, k_sb = sem("k_psum"), sem("k_sb")
        tails_psum, tails_sb = sem("tails_psum"), sem("tails_sb")
        v_psum, v_sb = sem("v_psum"), sem("v_sb")
        scores_psum, max_sb, exp_sb = sem("scores_psum"), sem("max_sb"), sem("exp_sb")
        pT_psum, pT_sb, av_done = sem("pT_psum"), sem("pT_sb"), sem("av_done")
        ptail_psum, ptail_sb = sem("ptail_psum"), sem("ptail_sb")
        rsum_sb, r_psum = sem("rsum_sb"), sem("r_psum")
        ctx_last_sb, rsum_b_sb = sem("ctx_last_sb"), sem("rsum_b_sb")
        o_done, o_sb, on_sb = sem("o_done"), sem("o_sb"), sem("on_sb")
        biased = sem("biased")
        out_psum, x_sb, stats_sb = sem("out_psum"), sem("x_sb"), sem("stats_sb")
        x_in, x_stats = [sem(f"x_in{q}") for q in range(XQ)], sem("x_stats")
        W_LOADS = 13
        block = ctx.enter_context(nc.Block())

        @block.sync
        def _(sp):
            for q in range(XQ):
                src = g.dram["x"][q * QT * BT:(q + 1) * QT * BT].rearrange("(t b) s d -> (b s) t d", b=BT)
                sp.dma_start(g.x[:, q * QT:(q + 1) * QT, :], src).then_inc(x_in[q], 16)

            def load(t, p):
                sp.dma_start(ctx_t[p][:, :].rearrange("d (b k) -> d b k", b=BT),
                             g.dram["ctxT"][bass.ds(t * BT, BT)].rearrange("b d k -> d b k")).then_inc(ctx_in[p], 16)

            load(0, 0)
            load(1, 1)
            with sp.Fori(0, T // 2 - 1) as i:
                for p in range(2):
                    sp.wait_ge(v_psum, i * 4 + 2 * p + 2)
                    load(i * 2 + (2 + p), p)

        @block.gpsimd
        def _(pool):
            def one(a, b):
                return one_col[:, :].unsqueeze(2).to_broadcast([P, a, b])

            def last_rows(t, p):
                pool.wait_ge(ctx_in[p], (t - p) * 8 + 16)
                if not (isinstance(t, int) and t == 0):
                    pool.wait_ge(tails_psum, t)
                rows = ctx_t[p][:, :].rearrange("d (b k) -> d b k", b=BT)[:, :, S2 - 1:S2]
                nc.gpsimd.tensor_tensor(ctx_last[:, :, :], rows.to_broadcast([P, BT, CH]), one(BT, CH), ALU.mult).then_inc(ctx_last_sb, 1)

            def add_bias(t):
                pool.wait_ge(xn_ready, t + 1)
                nc.gpsimd.tensor_tensor(g.x[:, t, :], g.x[:, t, :], out_bias[:, :], ALU.add).then_inc(biased, 1)

            def spread_queries(t, p):
                pool.wait_ge(q_sb, t + 1)
                if not (isinstance(t, int) and t < 2):
                    pool.wait_ge(scores_psum, (t - 1) * UN)
                nc.gpsimd.tensor_tensor(qblk[p][:, :].rearrange("p (b h s) -> p b h s", b=BT, h=XH),
                                        qT[:, :].rearrange("p (b s) -> p b s", b=BT).unsqueeze(2).to_broadcast([P, BT, XH, S]),
                                        headmask_s[:, :].unsqueeze(1).unsqueeze(3).to_broadcast([P, BT, XH, S]),
                                        ALU.mult).then_inc(qblk_sb, 1)

            def spread_sums(t):
                pool.wait_ge(rsum_sb, t + 1)
                nc.gpsimd.tensor_tensor(rsum_b[:, :, :], rsum[:, :].unsqueeze(2).to_broadcast([P, BT * CH, S]),
                                        one(BT * CH, S), ALU.mult)\
                  .then_inc(rsum_b_sb, 1)

            nc.gpsimd.memset(one_col[:, :], 1.0).then_inc(one_ready, 1)
            pool.wait_ge(one_ready, 1)
            last_rows(0, 0)
            pool.wait_ge(prep_dve, 9)
            spread_queries(0, 0)
            last_rows(1, 1)
            add_bias(0)
            spread_queries(1, 1)
            add_bias(1)
            with pool.Fori(0, T // 2 - 1) as i:
                for p in range(2):
                    spread_sums(i * 2 + p)
                    last_rows(i * 2 + (p + 2), p)
                    spread_queries(i * 2 + (p + 2), p)
                    add_bias(i * 2 + (p + 2))
            spread_sums(T - 2)
            spread_sums(T - 1)

        @block.tensor
        def _(pe):
            mm, tr = nc.tensor.matmul, nc.tensor.transpose

            def fill_xnT(t):
                pe.wait_ge(xn_ready, t + 1)
                tr(m_ps[:, 0:P], xn[:, :], g.ident[:, :]).then_inc(xnT_psum, 1)

            def fill_qT(t):
                pe.wait_ge(xnT_sb, t + 1)
                mm(m_ps[:, P:2 * P], w_qkv[:, 0, :], xnT[:, :], start=True, stop=True).then_inc(qT_psum, 1)

            def fill_k(t, p, n):
                if n == 0:
                    pe.wait_ge(tails_sb, t * 2 + 2)
                else:
                    pe.wait_ge(k_sb, t * 2 + n)
                mm(m_ps[:, :], w_qkv[:, 1, :], ctx_t[p][:, n * BANK:(n + 1) * BANK], start=True, stop=True).then_inc(k_psum, 1)

            def fill_tails(t, p):
                pe.wait_ge(ctx_in[p], (t - p) * 8 + 16)
                mm(m_ps[:, 2 * P:2 * P + BT], w_qkv[:, 1, :], ctx_t[p][:, 2 * BANK:BT * S2], start=True, stop=True)
                pe.wait_ge(ctx_last_sb, t + 1)
                mm(m_ps[0:BT * CH, 3 * P:4 * P], ctx_last[:, :, :], w_qkv[:, 2, :], start=True, stop=True).then_inc(tails_psum, 1)

            def fill_v(t, p, n):
                pe.wait_ge(k_sb, t * 2 + 2)
                if n == 1:
                    pe.wait_ge(v_sb, t * 2 + 1)
                for j in range(4):
                    b, k = 2 * n + j // 2, j % 2
                    ins = mm(m_ps[:, j * D:(j + 1) * D], ctx_t[p][:, b * S2 + k * P:b * S2 + k * P + P],
                             w_qkv[:, 2, :], start=True, stop=True)
                ins.then_inc(v_psum, 1)

            def scores(t, p, u):
                if u == 0:
                    pe.wait_ge(qblk_sb, t + 1)
                    pe.wait_ge(tails_sb, t * 2 + 2)
                    pe.wait_ge(k_sb, t * 2 + 2)
                b = u // 2
                for j in range(2):
                    c = b * CH + 2 * (u % 2) + j
                    mm(s_ps[u % 2][:, j, 0:S2], qblk[p][:, c * P:(c + 1) * P], kT[p][:, b * S2:(b + 1) * S2],
                       start=True, stop=False)
                    ins = mm(s_ps[u % 2][:, j, 0:S2], onehot[:, :], mask_b[:, :], start=False, stop=True)
                ins.then_inc(scores_psum, 1)

            def turn(t, p, u):
                pe.wait_ge(exp_sb, t * UN + u + 1)
                if not (isinstance(t, int) and t == 0 and u < 2):
                    pe.wait_ge(pT_sb, t * UN + u - 1)
                for j in range(2):
                    for k in range(2):
                        n = 2 * j + k
                        ins = tr(pT_ps[u % 2][:, n * P:(n + 1) * P], probs[p][:, 2 * u + j, k * P:(k + 1) * P],
                                 g.ident[:, :])
                ins.then_inc(pT_psum, 1)

            def attend(t, p, u):
                pe.wait_ge(pT_sb, t * UN + u + 1)
                b = u // 2
                if u == 0:
                    pe.wait_ge(v_sb, t * 2 + 2)
                if u == 0 and not (isinstance(t, int) and t == 0):
                    pe.wait_ge(o_sb, t)
                for k in range(2):
                    for j in range(2):
                        c = 2 * (u % 2) + j
                        q = slice(S * c, S * c + S)
                        n = 2 * j + k
                        ins = mm(o_ps[q, b * P:(b + 1) * P], v[p][:, (2 * b + k) * D + S * c:(2 * b + k) * D + S * c + S],
                                 pT[u % 2][:, n * P:(n + 1) * P], start=(b == 0 and k == 0), stop=False,
                                 skip_group_check=True)
                ins.then_inc(av_done, 1)

            def attend_tail(t, p):
                pe.wait_ge(ptail_sb, t + 1)
                mm(o_ps[:, :], v_tail[p][:, :], p_tail[:, :, :], start=False, stop=True,
                   skip_group_check=True).then_inc(o_done, 1)

            def fill_ptail(p):
                tr(m_ps[0:BT * CH, P:2 * P], probs[p][:, :, S2 - 1], g.ident[:, :]).then_inc(ptail_psum, 1)

            def fill_r(t):
                pe.wait_ge(rsum_b_sb, t + 1)
                for b in range(BT):
                    ins = tr(m_ps[:, b * P:(b + 1) * P], rsum_b[:, b * CH:(b + 1) * CH, :], g.ident[:, :])
                ins.then_inc(r_psum, 1)

            def fill_out(t):
                pe.wait_ge(on_sb, t + 1)
                for h in range(CH):
                    ins = mm(m_ps[:, 0:D], o_norm[:, h, :, :], w_om[:, h, :], start=(h == 0), stop=(h == CH - 1))
                ins.then_inc(out_psum, 1)

            def tile(t, p, prev, nxt):
                for u in range(UN):
                    scores(t, p, u)
                    if u >= 2:
                        attend(t, p, u - 2)
                    elif prev:
                        attend(t - 1, 1 - p, UN - 2 + u)
                    if u >= 1:
                        turn(t, p, u - 1)
                    elif prev:
                        turn(t - 1, 1 - p, UN - 1)
                    if u == 0:
                        pe.wait_ge(v_sb, t * 2 + 2)
                        if nxt:
                            fill_xnT(t + 1)
                        if prev:
                            fill_ptail(1 - p)
                    if u == 1 and prev:
                        if nxt:
                            pe.wait_ge(xnT_sb, t + 2)
                        pe.wait_ge(ptail_sb, t)
                        fill_r(t - 1)
                        attend_tail(t - 1, 1 - p)
                    if u == 3:
                        if prev:
                            fill_out(t - 1)
                        if nxt:
                            fill_qT(t + 1)
                            fill_tails(t + 1, 1 - p)
                    if u == 4 and nxt:
                        if prev:
                            pe.wait_ge(x_sb, t)
                        pe.wait_ge(q_sb, t + 2)
                        fill_k(t + 1, 1 - p, 0)
                    if u == 5 and nxt:
                        fill_k(t + 1, 1 - p, 1)
                    if u == 6 and nxt:
                        fill_v(t + 1, 1 - p, 0)
                    if u == 7 and nxt:
                        fill_v(t + 1, 1 - p, 1)

            pe.wait_ge(prep_dve, 8)
            mm(m_ps[:, 0:D], bv_b[:, :], w_o[:, :], start=True, stop=True).then_inc(prep_pe, 1)
            pe.wait_ge(prep_dve, 9)
            fill_xnT(0)
            fill_qT(0)
            fill_tails(0, 0)
            pe.wait_ge(q_sb, 1)
            fill_k(0, 0, 0)
            fill_k(0, 0, 1)
            fill_v(0, 0, 0)
            fill_v(0, 0, 1)
            tile(0, 0, False, True)
            with pe.Fori(0, T // 2 - 1) as i:
                tile(i * 2 + 1, 1, True, True)
                tile(i * 2 + 2, 0, True, True)
            tile(T - 1, 1, True, False)
            turn(T - 1, 1, UN - 1)
            attend(T - 1, 1, UN - 2)
            attend(T - 1, 1, UN - 1)
            pe.wait_ge(x_sb, T - 1)
            fill_ptail(1)
            pe.wait_ge(ptail_sb, T)
            fill_r(T - 1)
            attend_tail(T - 1, 1)
            fill_out(T - 1)

        @block.scalar
        def _(act):
            def copy_k(t, p, n):
                act.wait_ge(k_psum, t * 2 + n + 1)
                nc.scalar.activation(kT[p][:, n * BANK:(n + 1) * BANK], m_ps[:, :], ACT.Identity,
                                     bias=cols[:, 1:2]).then_inc(k_sb, 1)

            def copy_v(t, p, n):
                act.wait_ge(v_psum, t * 2 + n + 1)
                nc.scalar.activation(v[p][:, n * BANK:(n + 1) * BANK], m_ps[:, :], ACT.Copy).then_inc(v_sb, 1)

            def exps(t, p, u):
                act.wait_ge(max_sb, t * UN + u + 1)
                for j in range(2):
                    n = 2 * u + j
                    ins = nc.scalar.activation(probs[p][:, n, :], s_ps[u % 2][:, j, 0:S2], ACT.Exp,
                                               bias=neg_max[p][:, n:n + 1], accum_out=sums[p][:, n:n + 1])
                ins.then_inc(exp_sb, 1)

            def copy_o(t):
                act.wait_ge(o_done, t + 1)
                nc.scalar.activation(o_raw[:, :], o_ps[:, :], ACT.Copy).then_inc(o_sb, 1)

            def tile(t, p, prev, nxt):
                for u in range(UN):
                    exps(t, p, u)
                    if u == 1 and prev:
                        copy_o(t - 1)
                    if u in (4, 5) and nxt:
                        copy_k(t + 1, 1 - p, u - 4)
                    if u in (6, 7) and nxt:
                        copy_v(t + 1, 1 - p, u - 6)

            for n, name in enumerate(("Wq", "Wk", "Wv")):
                nc.scalar.dma_start(w_qkv[:, n, :], g.dram[f"L0_xattn_{name}_T"]).then_inc(w_in, 16)
            nc.scalar.dma_start(w_o[:, :], g.dram["L0_xattn_Wo_T"]).then_inc(w_in, 16)
            for n, name in enumerate(("bq", "bk", "bv")):
                nc.scalar.dma_start(cols[:, n:n + 1], g.dram[f"L0_xattn_{name}"].rearrange("(p a) -> p a", a=1)).then_inc(w_in, 16)
            nc.scalar.dma_start(bo_b[:, :], g.dram["L0_xattn_bo"].rearrange("(a n) -> a n", a=1).to_broadcast([P, D])).then_inc(w_in, 16)
            nc.scalar.dma_start(headmask[:, :], g.dram["c_headmask"]).then_inc(w_in, 16)
            nc.scalar.dma_start(tailmask[:, :, :], g.dram["c_tailmask"]).then_inc(w_in, 16)
            nc.scalar.dma_start(onehot[:, :], g.dram["c_onehot"]).then_inc(w_in, 16)
            nc.scalar.dma_start(headmask_s[:, :], g.dram["c_headmask16"]).then_inc(w_in, 16)
            nc.scalar.dma_start(mask_i[:, :], g.dram["mask"]).then_inc(mask_in, 16)
            nc.scalar.dma_start(g.ident[:, :], g.dram["c_ident"]).then_inc(w_in, 16)
            norm_coefficients(nc, g, act, None, ln_step, lnw)
            act.wait_ge(w_in, 16 * W_LOADS)
            copy_k(0, 0, 0)
            copy_k(0, 0, 1)
            copy_v(0, 0, 0)
            copy_v(0, 0, 1)
            tile(0, 0, False, True)
            with act.Fori(0, T // 2 - 1) as i:
                tile(i * 2 + 1, 1, True, True)
                tile(i * 2 + 2, 0, True, True)
            tile(T - 1, 1, True, False)
            copy_o(T - 1)

        @block.vector
        def _(dve):
            vec = nc.vector

            def norm(t):
                vec.tensor_scalar(xn[:, :], g.x[:, t, :], g.rstd[:, bass.ds(t, 1)], g.shift[:, bass.ds(t, 1)],
                                  ALU.mult, ALU.add).then_inc(xn_ready, 1)

            def copy_xnT(t):
                dve.wait_ge(xnT_psum, t + 1)
                vec.tensor_copy(xnT[:, :], m_ps[:, 0:P]).then_inc(xnT_sb, 1)

            def copy_q(t):
                if not (isinstance(t, int) and t == 0):
                    dve.wait_ge(qblk_sb, t)
                dve.wait_ge(qT_psum, t + 1)
                vec.tensor_scalar(qT[:, :], m_ps[:, P:2 * P], cols[:, 0:1], None, ALU.add).then_inc(q_sb, 1)

            def copy_tails(t, p):
                dve.wait_ge(tails_psum, t + 1)
                vec.tensor_scalar(kT[p][:, 2 * BANK:BT * S2], m_ps[:, 2 * P:2 * P + BT], cols[:, 1:2], None, ALU.add).then_inc(tails_sb, 1)
                vec.tensor_tensor(v_tail[p][0:BT * CH, :].rearrange("r (c e) -> r c e", c=CH),
                                  m_ps[0:BT * CH, 3 * P:4 * P].rearrange("r (c e) -> r c e", c=CH),
                                  tailmask[:, 1, :].unsqueeze(2).to_broadcast([BT * CH, CH, S]),
                                  ALU.mult).then_inc(tails_sb, 1)

            def maxes(t, p, u):
                dve.wait_ge(scores_psum, t * UN + u + 1)
                vec.tensor_reduce(neg_max[p][:, 2 * u:2 * u + 2], s_ps[u % 2][:, :, 0:S2], AX.X, ALU.max,
                                  negate=True).then_inc(max_sb, 1)

            def copy_pT(t, u):
                dve.wait_ge(pT_psum, t * UN + u + 1)
                if not (isinstance(t, int) and t == 0 and u < 2):
                    dve.wait_ge(av_done, t * UN + u - 1)
                vec.tensor_copy(pT[u % 2][:, :], pT_ps[u % 2][:, :]).then_inc(pT_sb, 1)

            def copy_ptail(t):
                dve.wait_ge(ptail_psum, t + 1)
                vec.tensor_tensor(p_tail[0:BT * CH, :, :], m_ps[0:BT * CH, P:2 * P].unsqueeze(1).to_broadcast([BT * CH, BT, P]),
                                  tailmask[:, 0, :].unsqueeze(2).to_broadcast([BT * CH, BT, P]),
                                  ALU.mult).then_inc(ptail_sb, 1)

            def recip(t, p):
                dve.wait_ge(exp_sb, t * UN + UN)
                vec.reciprocal(rsum[:, :], sums[p][:, :]).then_inc(rsum_sb, 1)

            def normalise(t):
                dve.wait_ge(r_psum, t + 1)
                dve.wait_ge(o_sb, t + 1)
                four = "p (b h s) -> p h b s"
                vec.tensor_tensor(o_norm[:, :, :, :], o_raw[:, :].rearrange(four, b=BT, h=CH),
                                  m_ps[:, :].rearrange(four, b=BT, h=CH), ALU.mult).then_inc(on_sb, 1)

            def add_out(t):
                dve.wait_ge(out_psum, t + 1)
                dve.wait_ge(biased, t + 1)
                vec.tensor_tensor(g.x[:, t, :], g.x[:, t, :], m_ps[:, 0:D], ALU.add).then_inc(x_sb, 1)

            def moments(t):
                dve.wait_ge(x_sb, t + 1)
                vec.bn_stats(g.bn[:, t, :], g.x[:, t, :]).then_inc(stats_sb, 1)

            def tile(t, p, prev, nxt):
                if nxt:
                    norm(t + 1)
                for u in range(UN):
                    maxes(t, p, u)
                    if u == 0 and prev:
                        copy_pT(t - 1, UN - 1)
                    if u >= 1:
                        copy_pT(t, u - 1)
                    if u == 0:
                        if nxt and prev:
                            dve.wait_ge(ptail_psum, t)
                        if nxt:
                            copy_xnT(t + 1)
                        if prev:
                            copy_ptail(t - 1)
                            recip(t - 1, 1 - p)
                    if u == 2 and prev:
                        normalise(t - 1)
                    if u == 3:
                        if nxt:
                            dve.wait_ge(tails_psum, t + 2)
                        if prev:
                            add_out(t - 1)
                        if nxt:
                            copy_q(t + 1)
                            copy_tails(t + 1, 1 - p)
                    if u == 5 and prev:
                        moments(t - 1)

            arrived_stats(nc, g, dve, x_in, x_stats)
            norm_coefficients(nc, g, None, dve, ln_step, lnw)
            norm(0)
            dve.wait_ge(w_in, 16 * W_LOADS)
            vec.tensor_copy(bv_b[:, :], cols[:, 2:3].to_broadcast([P, P])).then_inc(prep_dve, 1)
            vec.tensor_tensor(w_om[:, :, :], w_o[:, :].unsqueeze(1).to_broadcast([P, CH, D]),
                              headmask[:, :].unsqueeze(2).to_broadcast([P, CH, D]), ALU.mult).then_inc(prep_dve, 1)
            vec.memset(mask_b[:, :], 0.0).then_inc(prep_dve, 1)
            vec.memset(p_tail[:, :, :], 0.0).then_inc(prep_dve, 1)
            for p in range(2):
                vec.memset(v_tail[p][:, :], 0.0).then_inc(prep_dve, 1)
            vec.tensor_scalar(headmask_s[:, :], headmask_s[:, :], scale, None, ALU.mult).then_inc(prep_dve, 1)
            dve.wait_ge(mask_in, 16)
            dve.wait_ge(prep_dve, 7)
            vec.tensor_scalar(mask_b[0:S, :], mask_i[:, :], 0, MASKED, ALU.is_equal, ALU.mult).then_inc(prep_dve, 1)
            dve.wait_ge(prep_pe, 1)
            vec.tensor_tensor(out_bias[:, :], m_ps[:, 0:D], bo_b[:, :], ALU.add).then_inc(prep_dve, 1)
            copy_xnT(0)
            dve.wait_ge(tails_psum, 1)
            copy_q(0)
            copy_tails(0, 0)
            tile(0, 0, False, True)
            with dve.Fori(0, T // 2 - 1) as i:
                tile(i * 2 + 1, 1, True, True)
                tile(i * 2 + 2, 0, True, True)
            tile(T - 1, 1, True, False)
            copy_pT(T - 1, UN - 1)
            copy_ptail(T - 1)
            recip(T - 1, 1)
            normalise(T - 1)
            add_out(T - 1)
            moments(T - 1)
            dve.wait_ge(stats_sb, T)


def split_row(vec, dve, done, base, src, masks, work, out):
    hi, rest, f = work
    n = [base]

    def run(ins):
        ins.then_inc(done, 1)
        n[0] += 1
        dve.wait_ge(done, n[0])

    run(vec.tensor_copy(hi, src))
    run(vec.tensor_tensor(rest, src, hi, ALU.subtract))
    run(vec.tensor_scalar(f, hi, masks[:, 0:1], None, ALU.mult))
    run(vec.tensor_copy(hi, rest))
    run(vec.tensor_tensor(rest, rest, hi, ALU.subtract))
    run(vec.scalar_tensor_tensor(f, hi, masks[:, 1:2], f, ALU.mult, ALU.add))
    run(vec.tensor_copy(hi, rest))
    run(vec.scalar_tensor_tensor(f, hi, masks[:, 2:3], f, ALU.mult, ALU.add))
    run(vec.tensor_copy(out, f))
    return n[0]


E1 = 3 * D
R0 = 64
CB = E1 // P
SRMS_EPS = 1e-8
GAMMA = 0.99


def stage_mixer0(nc, g):
    with ExitStack() as ctx:
        sem = sem_maker(nc, g, "m0")
        sb, ps = tensor_makers(nc, ctx, "m0")
        w_uv = sb("w_uv", [P, 2, E1])
        w_o = sb("w_o", [P, CB, D])
        uvb3 = sb("uvb3", [3, 2 * E1])
        b_hi, b_rest, b_f = sb("b_hi", [3, 2 * E1], BF16), sb("b_rest", [3, 2 * E1]), sb("b_f", [3, 2 * E1])
        uvb = sb("uvb", [P, 2 * E1], BF16)
        ob = sb("ob", [P, D])
        ones, ones1 = sb("ones", [P, P], BF16), sb("ones1", [1, P])
        rowmask = sb("rowmask", [3, 3])
        dft = sb("dft", [P, 3, P])
        idft = sb("idft", [P, 3, P])
        cdft = sb("cdft", [S, 3, P])
        pos = sb("pos", [1, S])
        pos_w = sb("pos_w", [1, 2, R0])
        lw = sb("lw", [R0, 3, R0])
        lb = sb("lb", [1, 3, R0])
        out_w, out_b = sb("out_w", [R0, E1]), sb("out_b", [1, E1])
        sq, ss, rr = sb("sq", [S, R0]), sb("ss", [S, 4]), sb("rr", [S, 4, 2])
        hn, hT = sb("hn", [S, R0]), sb("hT", [R0, S])
        coef = sb("coef", [S, E1])
        mult = sb("mult", [P, 3, E1])
        lnw = sb("lnw", [P, 4, T])
        xn, xnT = sb("xn", [P, D]), sb("xnT", [P, P])
        u = [sb(f"u{p}", [P, E1]) for p in range(2)]
        v = sb("v", [P, E1])
        prod = sb("prod", [P, 3, E1])
        gated, gT = sb("gated", [P, E1]), sb("gT", [P, E1])

        m_ps = ps("m_ps", [P, BANK])
        t_ps = ps("t_ps", [P, BANK])
        uv_ps = [ps(f"uv_ps{n}", [P, BANK]) for n in range(2)]
        f_ps = [ps(f"f_ps{n}", [P, BANK]) for n in range(3)]
        y_ps = ps("y_ps", [P, BANK])

        w_in, line, ln_step, ready, bias_step = sem("w_in"), sem("line"), sem("ln_step"), sem("ready"), sem("bias_step")
        xn_ready, xnT_psum, xnT_sb = sem("xn_ready"), sem("xnT_psum"), sem("xnT_sb")
        uv_psum, v_sb, u_sb = sem("uv_psum"), sem("v_sb"), sem("u_sb")
        sums_psum, prod_sb, y_psum, gated_sb = sem("sums_psum"), sem("prod_sb"), sem("y_psum"), sem("gated_sb")
        gT_psum, gT_sb, out_psum, x_sb, stats_sb = sem("gT_psum"), sem("gT_sb"), sem("out_psum"), sem("x_sb"), sem("stats_sb")
        biased = sem("biased")
        N_LOADS = 19
        block = ctx.enter_context(nc.Block())

        def row(name):
            return g.dram[name].rearrange("(a n) -> a n", a=1)

        @block.sync
        def _(sp):
            def load(dst, src):
                sp.dma_start(dst, src).then_inc(w_in, 16)

            load(w_uv[:, 0, :], g.dram["L0_attn_u_w"])
            load(w_uv[:, 1, :], g.dram["L0_attn_v_w"])
            load(w_o[:, :, :], g.dram["L0_attn_o_w"].rearrange("(c p) n -> p c n", p=P))
            load(uvb3[:, 0:E1], row("L0_attn_u_b").to_broadcast([3, E1]))
            load(uvb3[:, E1:2 * E1], row("L0_attn_v_b").to_broadcast([3, E1]))
            load(ob[:, :], row("L0_attn_o_b").to_broadcast([P, D]))
            load(rowmask[:, :], g.dram["c_rowmask"])
            load(dft[:, :, :], g.dram["c_dft"])
            load(idft[:, :, :], g.dram["c_idft"])
            load(cdft[:, :, :], g.dram["c_cdft"])
            load(pos[:, :], g.dram["c_pos"])
            load(pos_w[:, 0, :], g.dram["L0_attn_pos_w"])
            load(pos_w[:, 1, :], row("L0_attn_pos_b"))
            for n in range(3):
                load(lw[:, n, :], g.dram[f"L0_attn_lw{n}"])
            load(lb[:, :, :].rearrange("a n r -> a (n r)"), g.dram["c_lb"])
            load(out_w[:, :], g.dram["L0_attn_out_w"])
            load(out_b[:, :], row("L0_attn_out_b"))

        ROUND = 8

        @block.tensor
        def _(pe):
            mm, tr = nc.tensor.matmul, nc.tensor.transpose
            pe.wait_ge(w_in, 16 * N_LOADS)
            pe.wait_ge(ready, 3)
            for n in range(5):
                if n:
                    pe.wait_ge(line, n * ROUND)
                width = R0 if n < 4 else E1
                rhs = [pos_w[:, 0, :], lw[:, 0, :], lw[:, 1, :], lw[:, 2, :], out_w[:, :]][n]
                bias = [pos_w[:, 1, :], lb[:, 0, :], lb[:, 1, :], lb[:, 2, :], out_b[:, :]][n]
                mm(m_ps[0:S, 0:width], pos[:, :] if n == 0 else hT[:, :], rhs, start=True, stop=False)
                mm(m_ps[0:S, 0:width], ones1[:, 0:S], bias, start=False, stop=True).then_inc(line, 1)
                if n < 4:
                    pe.wait_ge(line, n * ROUND + 6)
                    tr(t_ps[0:R0, 0:S], hn[:, :], g.ident[0:S, 0:S]).then_inc(line, 1)
            pe.wait_ge(line, 4 * ROUND + 2)
            for n in range(3):
                ins = mm(f_ps[n][:, 0:E1], cdft[:, n, :], coef[:, :], start=True, stop=True)
            ins.then_inc(line, 1)
            pe.wait_ge(bias_step, 9)

            def turn_xn(t):
                pe.wait_ge(xn_ready, t + 1)
                tr(m_ps[:, 0:P], xn[:, :], g.ident[:, :]).then_inc(xnT_psum, 1)

            def uv(t):
                pe.wait_ge(xnT_sb, t + 1)
                for n in range(2):
                    mm(uv_ps[n][:, 0:E1], xnT[:, :], w_uv[:, n, :], start=True, stop=False)
                    ins = mm(uv_ps[n][:, 0:E1], ones[:, :], uvb[:, n * E1:(n + 1) * E1], start=False, stop=True)
                ins.then_inc(uv_psum, 1)

            def transform(t):
                pe.wait_ge(v_sb, t + 1)
                for n in range(3):
                    ins = mm(f_ps[n][:, 0:E1], dft[:, n, :], v[:, :], start=True, stop=True)
                ins.then_inc(sums_psum, 1)

            def back(t):
                pe.wait_ge(prod_sb, t * 3 + 3)
                for n in range(3):
                    ins = mm(y_ps[:, 0:E1], idft[:, n, :], prod[:, n, :], start=(n == 0), stop=(n == 2))
                ins.then_inc(y_psum, 1)

            def turn_gated(t):
                pe.wait_ge(gated_sb, t + 1)
                for c in range(CB):
                    ins = tr(t_ps[:, c * P:(c + 1) * P], gated[:, c * P:(c + 1) * P], g.ident[:, :])
                ins.then_inc(gT_psum, 1)

            def project(t):
                pe.wait_ge(gT_sb, t + 1)
                for c in range(CB):
                    ins = mm(m_ps[:, 0:D], gT[:, c * P:(c + 1) * P], w_o[:, c, :], start=(c == 0), stop=(c == CB - 1))
                ins.then_inc(out_psum, 1)

            def tile(t, prev, nxt):
                if prev and not (isinstance(t, int) and t == 1):
                    pe.wait_ge(x_sb, t - 1)
                if nxt:
                    turn_xn(t + 1)
                transform(t)
                if prev:
                    turn_gated(t - 1)
                if nxt:
                    pe.wait_ge(u_sb, t + 1)
                    uv(t + 1)
                if prev:
                    if nxt:
                        pe.wait_ge(xnT_sb, t + 2)
                    project(t - 1)
                back(t)

            pe.wait_ge(line, 4 * ROUND + 4)
            turn_xn(0)
            uv(0)
            tile(0, False, True)
            tile(1, True, True)
            with pe.Fori(1, T // 2 - 1) as i:
                tile(i * 2, True, True)
                tile(i * 2 + 1, True, True)
            tile(T - 2, True, True)
            tile(T - 1, True, False)
            turn_gated(T - 1)
            pe.wait_ge(x_sb, T - 1)
            project(T - 1)

        @block.scalar
        def _(act):
            norm_coefficients(nc, g, act, None, ln_step, lnw)
            for n in range(4):
                act.wait_ge(line, n * ROUND + 1)
                nc.scalar.activation(sq[:, :], m_ps[0:S, 0:R0], ACT.Square, accum_out=ss[:, n:n + 1]).then_inc(line, 1)
                act.wait_ge(line, n * ROUND + 2)
                nc.scalar.activation(rr[:, n, 0:1], ss[:, n:n + 1], ACT.Sqrt, scale=1.0 / R0).then_inc(line, 1)

            def silus(t, p):
                act.wait_ge(uv_psum, t + 1)
                nc.scalar.activation(v[:, :], uv_ps[1][:, 0:E1], ACT.Silu).then_inc(v_sb, 1)
                nc.scalar.activation(u[p][:, :], uv_ps[0][:, 0:E1], ACT.Silu).then_inc(u_sb, 1)

            def copy_gT(t):
                act.wait_ge(gT_psum, t + 1)
                nc.scalar.activation(gT[:, :], t_ps[:, 0:E1], ACT.Copy).then_inc(gT_sb, 1)

            silus(0, 0)
            act.wait_ge(sums_psum, 1)
            silus(1, 1)
            with act.Fori(0, T // 2 - 1) as i:
                for p in range(2):
                    copy_gT(i * 2 + p)
                    act.wait_ge(sums_psum, i * 2 + (p + 2))
                    silus(i * 2 + (p + 2), p)
            copy_gT(T - 2)
            copy_gT(T - 1)

        @block.gpsimd
        def _(pool):
            pool.wait_ge(w_in, 16 * N_LOADS)
            with pool.Fori(0, T // 2) as i:
                for p in range(2):
                    t = i * 2 + p
                    pool.wait_ge(xn_ready, t + 1)
                    nc.gpsimd.tensor_tensor(g.x[:, t, :], g.x[:, t, :], ob[:, :], ALU.add).then_inc(biased, 1)

        @block.vector
        def _(dve):
            vec = nc.vector
            vec.memset(ones1[:, :], 1.0).then_inc(ready, 1)
            vec.memset(ones[:, :], 1.0).then_inc(ready, 1)
            vec.memset(uvb[:, :], 0.0).then_inc(ready, 1)
            norm_coefficients(nc, g, None, dve, ln_step, lnw)
            for n in range(4):
                k = n * ROUND
                dve.wait_ge(line, k + 3)
                vec.tensor_scalar(rr[:, n, 1:2], rr[:, n, 0:1], SRMS_EPS, None, ALU.add).then_inc(line, 1)
                dve.wait_ge(line, k + 4)
                vec.reciprocal(rr[:, n, 1:2], rr[:, n, 1:2]).then_inc(line, 1)
                dve.wait_ge(line, k + 5)
                vec.tensor_scalar(hn[:, :], m_ps[0:S, 0:R0], rr[:, n, 1:2], 0.0, ALU.mult, ALU.max).then_inc(line, 1)
                dve.wait_ge(line, k + 7)
                vec.tensor_copy(hT[:, :], t_ps[0:R0, 0:S]).then_inc(line, 1)
            dve.wait_ge(line, 4 * ROUND + 1)
            vec.tensor_copy(coef[:, :], m_ps[0:S, 0:E1]).then_inc(line, 1)
            dve.wait_ge(line, 4 * ROUND + 3)
            for n in range(3):
                ins = vec.tensor_copy(mult[:, n, :], f_ps[n][:, 0:E1])
            ins.then_inc(line, 1)
            dve.wait_ge(w_in, 16 * N_LOADS)
            dve.wait_ge(ready, 3)
            split_row(vec, dve, bias_step, 0, uvb3[:, :], rowmask, (b_hi[:, :], b_rest[:, :], b_f[:, :]), uvb[0:3, :])

            def norm(t):
                vec.tensor_scalar(xn[:, :], g.x[:, t, :], g.rstd[:, bass.ds(t, 1)], g.shift[:, bass.ds(t, 1)],
                                  ALU.mult, ALU.add).then_inc(xn_ready, 1)

            def copy_xnT(t):
                dve.wait_ge(xnT_psum, t + 1)
                vec.tensor_copy(xnT[:, :], m_ps[:, 0:P]).then_inc(xnT_sb, 1)

            def products(t):
                dve.wait_ge(sums_psum, t + 1)
                for n in range(3):
                    vec.tensor_tensor(prod[:, n, :], f_ps[n][:, 0:E1], mult[:, n, :], ALU.mult).then_inc(prod_sb, 1)

            def gate(t, p):
                dve.wait_ge(y_psum, t + 1)
                vec.tensor_tensor(gated[:, :], u[p][:, :], y_ps[:, 0:E1], ALU.mult).then_inc(gated_sb, 1)

            def add_out(t):
                dve.wait_ge(out_psum, t + 1)
                dve.wait_ge(biased, t + 1)
                vec.tensor_tensor(g.x[:, t, :], g.x[:, t, :], m_ps[:, 0:D], ALU.add).then_inc(x_sb, 1)
                dve.wait_ge(x_sb, t + 1)
                vec.bn_stats(g.bn[:, t, :], g.x[:, t, :]).then_inc(stats_sb, 1)

            def tile(t, p, prev, nxt):
                if nxt:
                    copy_xnT(t + 1)
                products(t)
                if nxt and not (isinstance(t, int) and t == T - 2):
                    norm(t + 2)
                if prev:
                    add_out(t - 1)
                gate(t, p)

            dve.wait_ge(line, 4 * ROUND + 4)
            norm(0)
            copy_xnT(0)
            norm(1)
            tile(0, 0, False, True)
            tile(1, 1, True, True)
            with dve.Fori(0, T // 2 - 2) as i:
                tile(i * 2 + 2, 0, True, True)
                tile(i * 2 + 3, 1, True, True)
            tile(T - 2, 0, True, True)
            tile(T - 1, 1, True, False)
            add_out(T - 1)
            dve.wait_ge(stats_sb, T)


GT = 4
NG = T // GT
TOK = GT * P
NE, EI = 8, 64
RC = NE * EI // P
HC = RC + 1
TOP0, ROUTE_SCALE = 2, 2.5
PAD = -3.0e38
TAKEN = 3.0e38


def wait(eng, sem, value):
    if not (isinstance(value, int) and value <= 0):
        eng.wait_ge(sem, value)


def top_lists(vec, run, alone, scores, rows, width, r):
    alone()
    for j in rows:
        run(vec.max(r["sorted"][:, j, :], scores[:, j, 0:width]), last=(j == rows[-1]))


def mark_top(vec, run, alone, scores, rows, r):
    alone()
    for j in rows:
        run(vec.match_replace(r["marked"][:, j, :], r["taken"][:, j, :], scores[:, j, :], TAKEN), last=(j == rows[-1]))


def take_top(vec, run, alone, scores, width, top, r):
    rows = range(scores.shape[1])
    top_lists(vec, run, alone, scores, rows, width, r)
    run(vec.tensor_copy(r["taken"][:, :, 0:top], r["sorted"][:, :, 0:top]))
    mark_top(vec, run, alone, scores, rows, r)
    run(vec.tensor_tensor(r["sel"], scores[:, :, 0:width], r["marked"][:, :, 0:width], ALU.not_equal))


def split_three(vec, run, value, parts, hi, rest):
    run(vec.tensor_copy(hi, value))
    run(vec.tensor_copy(parts[0], hi), last=False)
    run(vec.tensor_tensor(rest, value, hi, ALU.subtract))
    run(vec.tensor_copy(hi, rest))
    run(vec.tensor_copy(parts[1], hi), last=False)
    run(vec.tensor_tensor(parts[2], rest, hi, ALU.subtract))


def stage_experts0(nc, g):
    with ExitStack() as ctx:
        sem = sem_maker(nc, g, "e0")
        sb, ps = tensor_makers(nc, ctx, "e0")
        w_g, w_u, w_d = sb("w_g", [P, HC, P]), sb("w_u", [P, HC, P]), sb("w_d", [P, HC, D])
        w_r = sb("w_r", [P, NE])
        spread = sb("spread", [P, RC, P], BF16)
        lnw = sb("lnw", [P, 4, T])
        xn = sb("xn", [P, GT, D])
        xnT = [sb(f"xnT{p}", [P, TOK]) for p in range(2)]
        scores = sb("scores", [P, GT, NE + 8 - TOP0])
        r = {"sorted": sb("sorted", [P, GT, 8]), "taken": sb("taken", [P, GT, 8]),
             "marked": sb("marked", [P, GT, NE + 8 - TOP0]), "sel": sb("sel", [P, GT, NE])[:, :, :]}
        total, weight = sb("total", [P, GT]), sb("weight", [P, GT, NE])
        part_hi, part_rest = sb("part_hi", [P, GT, NE], BF16), sb("part_rest", [P, GT, NE])
        parts = sb("parts", [P, GT, 3 * NE])
        weightT = [sb(f"weightT{p}", [P, TOK], BF16) for p in range(2)]
        gate = [sb(f"gate{p}", [P, TOK]) for p in range(2)]
        hid = [sb(f"hid{p}", [P, TOK]) for p in range(2)]

        m_ps = ps("m_ps", [P, BANK])
        g_ps = [ps(f"g_ps{p}", [P, BANK]) for p in range(2)]
        u_ps = [ps(f"u_ps{p}", [P, BANK]) for p in range(2)]
        w_ps = [ps(f"w_ps{p}", [P, BANK]) for p in range(2)]
        o_ps = ps("o_ps", [P, BANK])

        w_in, ln_step, pads = sem("w_in"), sem("ln_step"), sem("pads")
        xn_ready, xT_psum, xT_sb = sem("xn_ready"), sem("xT_psum"), sem("xT_sb")
        logits_psum, scores_sb, route = sem("logits_psum"), sem("scores_sb"), sem("route")
        wT_psum, wT_sb = sem("wT_psum"), sem("wT_sb")
        up_psum, gate_sb, mid_sb, hid_sb, down = sem("up_psum"), sem("gate_sb"), sem("mid_sb"), sem("hid_sb"), sem("down")
        x_sb, stats_sb = sem("x_sb"), sem("stats_sb")
        waited = sem("waited")
        N_LOADS = 5
        TOP_STEPS = 2 * GT + 3
        ROUTE_STEPS = TOP_STEPS + 10
        block = ctx.enter_context(nc.Block())

        @block.sync
        def _(sp):
            sp.dma_start(w_g[:, :, :].rearrange("p h n -> p (h n)"), g.dram["L0_gate_T"]).then_inc(w_in, 16)
            sp.dma_start(w_u[:, :, :].rearrange("p h n -> p (h n)"), g.dram["L0_up_T"]).then_inc(w_in, 16)
            sp.dma_start(w_d[:, :, :], g.dram["L0_down_T"].rearrange("(h p) n -> p h n", p=P)).then_inc(w_in, 16)
            sp.dma_start(w_r[:, :], g.dram["L0_ffn_gate_weight_T"]).then_inc(w_in, 16)
            sp.dma_start(spread[:, :, :].rearrange("r h n -> r (h n)"), g.dram["c_spread0"]).then_inc(w_in, 16)

        @block.tensor
        def _(pe):
            mm, tr = nc.tensor.matmul, nc.tensor.transpose

            def turn_x(n):
                pe.wait_ge(xn_ready, n * GT + GT)
                for k in range(GT):
                    ins = tr(m_ps[:, k * P:(k + 1) * P], xn[:, k, :], g.ident[:, :])
                ins.then_inc(xT_psum, 1)

            def logits(n, p):
                pe.wait_ge(xT_sb, n + 1)
                for k in range(GT):
                    ins = mm(m_ps[:, k * NE:(k + 1) * NE], xnT[p][:, k * P:(k + 1) * P], w_r[:, :], start=True, stop=True)
                ins.then_inc(logits_psum, 1)

            def turn_weights(n):
                pe.wait_ge(route, n * ROUTE_STEPS + ROUTE_STEPS)
                for k in range(GT):
                    ins = tr(m_ps[0:3 * NE, k * P:(k + 1) * P], parts[:, k, :], g.ident[:, :])
                ins.then_inc(wT_psum, 1)

            def up(n, p, h):
                b = (p + h) % 2
                if h == 0:
                    pe.wait_ge(wT_sb, n + 1)
                wait(pe, hid_sb, n * HC + h - 1)
                mm(g_ps[b][:, :], w_g[:, h, :], xnT[p][:, :], start=True, stop=True)
                ins = mm(u_ps[b][:, :], w_u[:, h, :], xnT[p][:, :], start=True, stop=True)
                if h < RC:
                    ins = mm(w_ps[b][:, :], spread[:, h, :], weightT[p][:, :], start=True, stop=True)
                ins.then_inc(up_psum, 1)

            def project(n, p, h):
                pe.wait_ge(hid_sb, n * HC + h + 1)
                if h == 0:
                    wait(pe, x_sb, n)
                for k in range(GT):
                    ins = mm(o_ps[:, k * D:(k + 1) * D], hid[(p + h) % 2][:, k * P:(k + 1) * P], w_d[:, h, :],
                             start=(h == 0 and k == 0), stop=(h == HC - 1), skip_group_check=True)
                ins.then_inc(down, 1)

            def group(n, p, prev, nxt):
                for h in range(HC):
                    up(n, p, h)
                    if h:
                        project(n, p, h - 1)
                    elif prev:
                        project(n - 1, 1 - p, HC - 1)
                    if nxt and h == 1:
                        turn_x(n + 1)
                    if nxt and h == 2:
                        logits(n + 1, 1 - p)
                    if nxt and h == 4:
                        turn_weights(n + 1)

            pe.wait_ge(w_in, 16 * N_LOADS)
            turn_x(0)
            logits(0, 0)
            turn_weights(0)
            group(0, 0, False, True)
            with pe.Fori(0, NG // 2 - 1) as i:
                group(i * 2 + 1, 1, True, True)
                group(i * 2 + 2, 0, True, True)
            group(NG - 1, 1, True, False)
            project(NG - 1, 1, HC - 1)

        @block.scalar
        def _(act):
            def sigmoids(n):
                act.wait_ge(logits_psum, n + 1)
                nc.scalar.activation(scores[:, :, 0:NE], m_ps[:, 0:GT * NE].rearrange("p (k e) -> p k e", k=GT),
                                     ACT.Sigmoid).then_inc(scores_sb, 1)

            def silu(n, p, h):
                act.wait_ge(up_psum, n * HC + h + 1)
                nc.scalar.activation(gate[(p + h) % 2][:, :], g_ps[(p + h) % 2][:, :], ACT.Silu).then_inc(gate_sb, 1)

            def group(n, p, nxt):
                for h in range(HC):
                    silu(n, p, h)
                    if nxt and h == 2:
                        sigmoids(n + 1)

            norm_coefficients(nc, g, act, None, ln_step, lnw)
            sigmoids(0)
            with act.Fori(0, NG // 2 - 1) as i:
                group(i * 2, 0, True)
                group(i * 2 + 1, 1, True)
            group(NG - 2, 0, True)
            group(NG - 1, 1, False)

        @block.vector
        def _(dve):
            vec = nc.vector

            def norm(n):
                for k in range(GT):
                    t = n * GT + k
                    vec.tensor_scalar(xn[:, k, :], g.x[:, t, :], g.rstd[:, bass.ds(t, 1)], g.shift[:, bass.ds(t, 1)],
                                      ALU.mult, ALU.add).then_inc(xn_ready, 1)

            def copy_xT(n, p):
                dve.wait_ge(xT_psum, n + 1)
                vec.tensor_copy(xnT[p][:, :], m_ps[:, :]).then_inc(xT_sb, 1)

            def runner(n, start):
                done = [start]

                def run(ins, last=True):
                    ins.then_inc(route, 1)
                    done[0] += 1
                    if last:
                        dve.wait_ge(route, n * ROUTE_STEPS + done[0])
                return run, done

            def routing_top(n):
                run, done = runner(n, 0)
                dve.wait_ge(scores_sb, n + 1)
                take_top(vec, run, lambda: dve.sem_inc(waited, 1), scores[:, :, :], NE, TOP0, r)
                run(vec.tensor_tensor(weight[:, :, :], r["sel"], scores[:, :, 0:NE], ALU.mult))
                assert done[0] == TOP_STEPS

            def routing_weights(n):
                run, done = runner(n, TOP_STEPS)
                run(vec.tensor_reduce(total[:, :], weight[:, :, :], AX.X, ALU.add))
                run(vec.tensor_scalar(total[:, :], total[:, :], 1e-20, None, ALU.add))
                run(vec.reciprocal(total[:, :], total[:, :]))
                run(vec.scalar_tensor_tensor(weight[:, :, :], weight[:, :, :], ROUTE_SCALE,
                                             total[:, :].unsqueeze(2).to_broadcast([P, GT, NE]), ALU.mult, ALU.mult))
                split_three(vec, run, weight[:, :, :], [parts[:, :, j * NE:(j + 1) * NE] for j in range(3)],
                            part_hi[:, :, :], part_rest[:, :, :])
                assert done[0] == ROUTE_STEPS

            def copy_weights(n, p):
                dve.wait_ge(wT_psum, n + 1)
                vec.tensor_copy(weightT[p][0:3 * NE, :], m_ps[0:3 * NE, :]).then_inc(wT_sb, 1)

            def hidden(n, p, h):
                b = (p + h) % 2
                dve.wait_ge(gate_sb, n * HC + h + 1)
                wait(dve, down, n * HC + h - 1)
                first = vec.tensor_tensor(hid[b][:, :], gate[b][:, :], u_ps[b][:, :], ALU.mult)
                if h < RC:
                    first.then_inc(mid_sb, 1)
                    dve.wait_ge(mid_sb, n * RC + h + 1)
                    vec.tensor_tensor(hid[b][:, :], hid[b][:, :], w_ps[b][:, :], ALU.mult).then_inc(hid_sb, 1)
                else:
                    first.then_inc(hid_sb, 1)

            def add_out(n):
                dve.wait_ge(down, n * HC + HC)
                xs = g.x[:, bass.ds(n * GT, GT), :]
                vec.tensor_tensor(xs, xs, o_ps[:, :].rearrange("p (k d) -> p k d", k=GT), ALU.add).then_inc(x_sb, 1)
                dve.wait_ge(x_sb, n + 1)
                for k in range(GT):
                    vec.bn_stats(g.bn[:, n * GT + k, :], g.x[:, n * GT + k, :]).then_inc(stats_sb, 1)

            def group(n, p, prev, nxt):
                for h in range(HC):
                    hidden(n, p, h)
                    if h == 0:
                        if prev:
                            add_out(n - 1)
                        if nxt:
                            norm(n + 1)
                    if nxt and h == 1:
                        copy_xT(n + 1, 1 - p)
                    if nxt and h == 2:
                        routing_top(n + 1)
                    if nxt and h == 3:
                        routing_weights(n + 1)
                    if nxt and h == 4:
                        copy_weights(n + 1, 1 - p)

            vec.memset(scores[:, :, NE:], PAD).then_inc(pads, 1)
            vec.memset(r["taken"][:, :, TOP0:], PAD).then_inc(pads, 1)
            for p in range(2):
                vec.memset(weightT[p][:, :], 0.0).then_inc(pads, 1)
            norm_coefficients(nc, g, None, dve, ln_step, lnw)
            dve.wait_ge(pads, 4)
            norm(0)
            copy_xT(0, 0)
            routing_top(0)
            routing_weights(0)
            copy_weights(0, 0)
            group(0, 0, False, True)
            with dve.Fori(0, NG // 2 - 1) as i:
                group(i * 2 + 1, 1, True, True)
                group(i * 2 + 2, 0, True, True)
            group(NG - 1, 1, True, False)
            add_out(NG - 1)
            dve.wait_ge(stats_sb, T)


def pipeline(eng, step, ahead, behind, unroll=2):
    first = -(-behind // unroll) * unroll
    last = T - -(-ahead // unroll) * unroll
    for t in range(-ahead, first):
        step(t, t % unroll)
    with eng.Fori(0, (last - first) // unroll) as i:
        for p in range(unroll):
            step(i * unroll + (first + p), p)
    for t in range(last, T + behind):
        step(t, t % unroll)


def inside(t):
    return not isinstance(t, int) or 0 <= t < T


def stage_cross1(nc, g):
    inv = 1.0 / 32.0
    with ExitStack() as ctx:
        sem = sem_maker(nc, g, "x1")
        sb, ps = tensor_makers(nc, ctx, "x1")
        w_q, w_k = sb("w_q", [P, D]), sb("w_k", [P, D])
        cols = sb("cols", [P, 2])
        lnw = sb("lnw", [P, 4, T])
        ctx_t = [sb(f"ctx_t{p}", [P, BT, S2]) for p in range(2)]
        ctx_n = [sb(f"ctx_n{p}", [P, 2, BT, D]) for p in range(2)]
        ctx_l = [sb(f"ctx_l{p}", [1, BT, D]) for p in range(2)]
        xn = [sb(f"xn{p}", [P, D]) for p in range(2)]
        xnT, qT, qkT = ([sb(f"{n}{p}", [P, P]) for p in range(2)] for n in ("xnT", "qT", "qkT"))
        c = [sb(f"c{p}", [P, 1]) for p in range(2)]
        neg, bias = sb("neg", [P, 2, 2]), sb("bias", [P, 2])
        sums, rsum = sb("sums", [P, 2]), sb("rsum", [P, 2])
        probs = [sb(f"probs{p}", [P, S2]) for p in range(2)]
        pT = [sb(f"pT{p}", [P, 2, P]) for p in range(2)]
        pT_l = [sb(f"pT_l{p}", [1, P]) for p in range(2)]

        x_ps, q_ps, k_ps, p_ps, o_ps = (ps(n, [P, BANK]) for n in ("x_ps", "q_ps", "k_ps", "p_ps", "o_ps"))
        s_ps = [ps(f"s_ps{p}", [P, BANK]) for p in range(2)]

        w_in, ln_step = sem("w_in"), sem("ln_step")
        ctxT_in, ctx_in = ([sem(f"{n}{p}") for p in range(2)] for n in ("ctxT_in", "ctx_in"))
        xn_ready, xT_psum, xT_sb, q_psum, q_sb = (sem(n) for n in ("xn_ready", "xT_psum", "xT_sb", "q_psum", "q_sb"))
        qk_psum, qk_sb, scores_psum, max_sb = (sem(n) for n in ("qk_psum", "qk_sb", "scores_psum", "max_sb"))
        neg_sb, bias_sb, exp_sb, pT_psum, pT_sb = (sem(n) for n in ("neg_sb", "bias_sb", "exp_sb", "pT_psum", "pT_sb"))
        rsum_sb, o_psum, x_sb, x_out = (sem(n) for n in ("rsum_sb", "o_psum", "x_sb", "x_out"))
        block = ctx.enter_context(nc.Block())
        W_LOADS = 4

        @block.sync
        def _(sp):
            def load_T(t, p):
                sp.dma_start(ctx_t[p][:, :, :], g.dram["ctxT"][bass.ds(t * BT, BT)].rearrange("b d k -> d b k"))\
                  .then_inc(ctxT_in[p], 16)

            def load_n(t, p):
                src = g.dram["ctx"][bass.ds(t * BT, BT)]
                for k in range(2):
                    sp.dma_start(ctx_n[p][:, k, :, :], src[:, k * P:(k + 1) * P, :].rearrange("b p d -> p b d"))\
                      .then_inc(ctx_in[p], 16)
                sp.dma_start(ctx_l[p][:, :, :], src[:, 2 * P:S2, :].rearrange("b k d -> k b d")).then_inc(ctx_in[p], 16)

            sp.dma_start(w_q[:, :], g.dram["L1_xattn_Wq_T"]).then_inc(w_in, 16)
            sp.dma_start(w_k[:, :], g.dram["L1_xattn_Wk"]).then_inc(w_in, 16)
            sp.dma_start(cols[:, 0:1], g.dram["L1_xattn_bq"].rearrange("(p a) -> p a", a=1)).then_inc(w_in, 16)
            sp.dma_start(cols[:, 1:2], g.dram["L1_xattn_bk"].rearrange("(p a) -> p a", a=1)).then_inc(w_in, 16)
            load_T(0, 0)
            load_T(1, 1)

            def step(t, p):
                if inside(t):
                    wait(sp, o_psum, t - 1)
                    load_n(t, p)
                if inside(t + 2) and inside(t):
                    sp.wait_ge(scores_psum, t + 1)
                    load_T(t + 2, p)
                if inside(t - 3):
                    sp.wait_ge(x_sb, t - 2)
                    dst = g.x_mid[bass.ds((t - 3) * BT, BT)].rearrange("b s d -> (b s) d")
                    sp.dma_start(dst, g.x[:, t - 3, :]).then_inc(x_out, 16)

            pipeline(sp, step, 2, 3)
            sp.wait_ge(x_out, 16 * T)

        @block.tensor
        def _(pe):
            mm, tr = nc.tensor.matmul, nc.tensor.transpose

            def step(t, p):
                o = 1 - p
                if inside(t + 3):
                    pe.wait_ge(xn_ready, t + 4)
                    wait(pe, xT_sb, t + 3)
                    tr(x_ps[:, 0:P], xn[o][:, :], g.ident[:, :]).then_inc(xT_psum, 1)
                if inside(t + 2):
                    pe.wait_ge(xT_sb, t + 3)
                    wait(pe, q_sb, t + 2)
                    mm(q_ps[:, 0:P], w_q[:, :], xnT[p][:, :], start=True, stop=True).then_inc(q_psum, 1)
                if inside(t + 1):
                    pe.wait_ge(q_sb, t + 2)
                    wait(pe, qk_sb, (t + 1) * 2)
                    mm(k_ps[:, 0:P], w_k[:, :], qT[o][:, :], start=True, stop=True)
                    mm(k_ps[:, P:P + 1], qT[o][:, :], cols[:, 1:2], start=True, stop=True).then_inc(qk_psum, 1)
                if inside(t):
                    pe.wait_ge(qk_sb, (t + 1) * 2)
                    pe.wait_ge(ctxT_in[p], (t - p) * 8 + 16)
                    wait(pe, exp_sb, t - 1)
                    for b in range(BT):
                        q = slice(b * S, b * S + S)
                        ins = mm(s_ps[p][q, 0:S2], qkT[p][:, q], ctx_t[p][:, b, :], start=True, stop=True)
                    ins.then_inc(scores_psum, 1)
                if inside(t - 1):
                    pe.wait_ge(exp_sb, t)
                    wait(pe, pT_sb, (t - 1) * 2)
                    for k in range(2):
                        tr(p_ps[:, k * P:(k + 1) * P], probs[o][:, k * P:(k + 1) * P], g.ident[:, :])
                    tr(p_ps[0:1, 2 * P:3 * P], probs[o][:, 2 * P:S2], g.ident[:, :]).then_inc(pT_psum, 1)
                if inside(t - 2):
                    pe.wait_ge(pT_sb, (t - 1) * 2)
                    pe.wait_ge(ctx_in[p], (t - 2 - p) * 24 + 48)
                    wait(pe, x_sb, t - 2)
                    for k in range(3):
                        for b in range(BT):
                            q = slice(b * S, b * S + S)
                            lhs, rhs = (pT[p][:, k, q], ctx_n[p][:, k, b, :]) if k < 2 else (pT_l[p][:, q], ctx_l[p][:, b, :])
                            ins = mm(o_ps[q, 0:D], lhs, rhs, start=(k == 0), stop=(k == 2), skip_group_check=True)
                    ins.then_inc(o_psum, 1)

            pe.wait_ge(w_in, 16 * W_LOADS)
            pipeline(pe, step, 3, 3)

        @block.scalar
        def _(act):
            def step(t, p):
                o = 1 - p
                if inside(t + 2):
                    act.wait_ge(q_psum, t + 3)
                    nc.scalar.activation(qT[p][:, :], q_ps[:, 0:P], ACT.Identity, bias=cols[:, 0:1]).then_inc(q_sb, 1)
                if inside(t + 3):
                    act.wait_ge(xT_psum, t + 4)
                    nc.scalar.activation(xnT[o][:, :], x_ps[:, 0:P], ACT.Copy).then_inc(xT_sb, 1)
                if inside(t):
                    act.wait_ge(bias_sb, t + 1)
                    nc.scalar.activation(probs[p][:, :], s_ps[p][:, 0:S2], ACT.Exp, scale=inv, bias=bias[:, p:p + 1],
                                         accum_out=sums[:, p:p + 1]).then_inc(exp_sb, 1)

            norm_coefficients(nc, g, act, None, ln_step, lnw)
            act.wait_ge(w_in, 16 * W_LOADS)
            pipeline(act, step, 3, 0)

        @block.vector
        def _(dve):
            vec = nc.vector

            def norm(t, p):
                vec.tensor_scalar(xn[p][:, :], g.x[:, t, :], g.rstd[:, bass.ds(t, 1)], g.shift[:, bass.ds(t, 1)],
                                  ALU.mult, ALU.add).then_inc(xn_ready, 1)

            def step(t, p):
                o = 1 - p
                if inside(t + 4):
                    wait(dve, xT_psum, t + 3)
                    norm(t + 4, p)
                if inside(t + 1):
                    wait(dve, bias_sb, t)
                    dve.wait_ge(qk_psum, t + 2)
                    vec.tensor_copy(qkT[o][:, :], k_ps[:, 0:P]).then_inc(qk_sb, 1)
                    vec.tensor_copy(c[o][:, :], k_ps[:, P:P + 1]).then_inc(qk_sb, 1)
                if inside(t):
                    dve.wait_ge(scores_psum, t + 1)
                    vec.tensor_reduce(neg[:, p, 0:1], s_ps[p][:, 0:S2], AX.X, ALU.max, negate=True).then_inc(max_sb, 1)
                    dve.wait_ge(max_sb, t + 1)
                    vec.tensor_scalar(neg[:, p, 1:2], neg[:, p, 0:1], c[p][:, :], inv, ALU.subtract, ALU.mult).then_inc(neg_sb, 1)
                    dve.wait_ge(neg_sb, t + 1)
                    vec.scalar_tensor_tensor(bias[:, p:p + 1], c[p][:, :], inv, neg[:, p, 1:2], ALU.mult, ALU.add)\
                       .then_inc(bias_sb, 1)
                if inside(t - 1):
                    dve.wait_ge(pT_psum, t)
                    vec.tensor_copy(pT[o][:, :, :], p_ps[:, 0:2 * P].rearrange("p (k q) -> p k q", k=2)).then_inc(pT_sb, 1)
                    vec.tensor_copy(pT_l[o][:, :], p_ps[0:1, 2 * P:3 * P]).then_inc(pT_sb, 1)
                    wait(dve, x_sb, t - 2)
                    vec.reciprocal(rsum[:, o:o + 1], sums[:, o:o + 1]).then_inc(rsum_sb, 1)
                if inside(t - 2):
                    dve.wait_ge(o_psum, t - 1)
                    dve.wait_ge(rsum_sb, t - 1)
                    vec.scalar_tensor_tensor(g.x[:, t - 2, :], o_ps[:, 0:D], rsum[:, p:p + 1], g.x[:, t - 2, :],
                                             ALU.mult, ALU.add).then_inc(x_sb, 1)

            norm_coefficients(nc, g, None, dve, ln_step, lnw)
            pipeline(dve, step, 4, 3)
            dve.wait_ge(x_sb, T)


DI, NS, TAPS = 256, 16, 4
DB = DI // P
XW = 1 + 2 * NS
NH = 4
NQ = NS // NH
NQP = NQ - 1
TINY = float(np.exp(-20.0))
LN_Q = 4


def stage_scan1(nc, g):
    with ExitStack() as ctx:
        sb = tensor_makers(nc, ctx, "sc")[0]
        uz = sb("uz", [P, T, 2 * DI])
        dt = sb("dt", [P, T, DI])
        xd = sb("xd", [P, T, XW])
        a = sb("a", [P, NS])
        scan_inputs(nc, g, uz, dt, xd, a)
        scan_states(nc, g, uz, dt, xd, a)
        scan_output(nc, g, uz, dt)


def scan_inputs(nc, g, uz, dt, xd, a):
    with ExitStack() as ctx:
        sem = sem_maker(nc, g, "si")
        sb, ps = tensor_makers(nc, ctx, "si")
        w_in_T = sb("w_in_T", [P, 2 * DI])
        taps = sb("taps", [P, TAPS, DI])
        w_c = sb("w_c", [P, TAPS, DI])
        w_x = sb("w_x", [P, DB, XW])
        w_dt, b_dt = sb("w_dt", [P, DI]), sb("b_dt", [P, DI])
        cb3, c_rest, c_f = sb("cb3", [3, DI]), sb("c_rest", [3, DI]), sb("c_f", [3, DI])
        c_hi, cb = sb("c_hi", [3, DI], BF16), sb("cb", [P, DI], BF16)
        ones, rowmask = sb("ones", [P, P], BF16), sb("rowmask", [3, 3])
        lnw = sb("lnw", [P, 4, T])
        xn = [sb(f"xn{p}", [P, D]) for p in range(2)]
        xnT = [sb(f"xnT{p}", [P, P]) for p in range(TAPS)]
        u = [sb(f"u{p}", [P, 2 * DI]) for p in range(2)]
        uT = [sb(f"uT{p}", [P, DI]) for p in range(2)]
        soft = sb("soft", [P, T, DI])

        x_ps, c_ps, u_ps, d_ps = (ps(n, [P, BANK]) for n in ("x_ps", "c_ps", "u_ps", "d_ps"))
        c_ps = [c_ps, ps("c_ps1", [P, BANK])]

        x_in = [sem(f"x_in{q}") for q in range(XQ)]
        w_in, stats, ln_step, prep = (sem(n) for n in ("w_in", "stats", "ln_step", "prep"))
        xn_ready, xT_psum, xT_sb, conv_psum, u_sb = (sem(n) for n in ("xn_ready", "xT_psum", "xT_sb", "conv_psum", "u_sb"))
        uz_sb, uT_psum, uT_sb, xd_psum, xd_sb, dt_sb = (sem(n) for n in ("uz_sb", "uT_psum", "uT_sb", "xd_psum", "xd_sb", "dt_sb"))
        waited_pool = sem("waited_pool")
        waited, abs_sb, exp_sb, ln_sb, soft_sb, clip_sb = (sem(n) for n in ("waited", "abs_sb", "exp_sb", "ln_sb", "soft_sb", "clip_sb"))
        block = ctx.enter_context(nc.Block())
        a_step = sem("a_step")
        W_LOADS = 8
        LT = T // LN_Q

        @block.sync
        def _(sp):
            for q in range(XQ):
                t = slice(q * QT, (q + 1) * QT)
                sp.dma_start(g.x[:, t, :], g.x_mid[:, t, :]).then_inc(x_in[q], 16)

        @block.tensor
        def _(pe):
            mm, tr = nc.tensor.matmul, nc.tensor.transpose

            def step(t, p):
                if inside(t + 2):
                    pe.wait_ge(xn_ready, t + 3)
                    wait(pe, xT_sb, t + 2)
                    tr(x_ps[:, 0:P], xn[p % 2][:, :], g.ident[:, :]).then_inc(xT_psum, 1)
                if inside(t + 1):
                    pe.wait_ge(xT_sb, t + 2)
                    wait(pe, u_sb, t)
                    out = c_ps[(p + 1) % 2]
                    for j in range(TAPS):
                        if inside(t + 1 - j):
                            mm(out[:, 0:DI], xnT[(p + 1 - j) % TAPS][:, :], w_c[:, TAPS - 1 - j, :], start=(j == 0), stop=False)
                    mm(out[:, 0:DI], ones[:, :], cb[:, :], start=False, stop=True)
                    mm(out[:, DI:2 * DI], xnT[(p + 1) % TAPS][:, :], w_in_T[:, DI:2 * DI], start=True, stop=True)\
                      .then_inc(conv_psum, 1)
                if inside(t):
                    pe.wait_ge(u_sb, t + 1)
                    wait(pe, uT_sb, t)
                    for c in range(DB):
                        ins = tr(u_ps[:, c * P:(c + 1) * P], u[p % 2][:, c * P:(c + 1) * P], g.ident[:, :])
                    ins.then_inc(uT_psum, 1)
                if inside(t - 1):
                    pe.wait_ge(uT_sb, t)
                    wait(pe, xd_sb, t - 1)
                    for c in range(DB):
                        ins = mm(d_ps[:, 0:XW], uT[(p + 1) % 2][:, c * P:(c + 1) * P], w_x[:, c, :], start=(c == 0), stop=(c == DB - 1))
                    ins.then_inc(xd_psum, 1)

            pe.wait_ge(prep, TAPS + 2 + 9)
            pipeline(pe, step, 2, 1, TAPS)

        @block.scalar
        def _(act):
            def step(t, p):
                if inside(t + 1):
                    act.wait_ge(conv_psum, t + 2)
                    wait(act, uz_sb, t)
                    nc.scalar.activation(u[(p + 1) % 2][:, :], c_ps[(p + 1) % 2][:, :], ACT.Silu).then_inc(u_sb, 1)
                if inside(t + 2):
                    act.wait_ge(xT_psum, t + 3)
                    nc.scalar.activation(xnT[(p + 2) % TAPS][:, :], x_ps[:, 0:P], ACT.Copy).then_inc(xT_sb, 1)
                if inside(t - 2):
                    act.wait_ge(dt_sb, t - 1)
                    act.sem_inc(waited, 1)
                    nc.scalar.activation(soft[:, t - 2, :], dt[:, t - 2, :], ACT.Abs).then_inc(abs_sb, 1)

            nc.scalar.dma_start(w_in_T[:, :], g.dram["L1_attn_W_in_T"]).then_inc(w_in, 16)
            nc.scalar.dma_start(taps[:, :, :].rearrange("p k e -> p (k e)"),
                         g.dram["L1_conv_T"].to_broadcast([P, TAPS * DI])).then_inc(w_in, 16)
            nc.scalar.dma_start(w_x[:, :, :], g.dram["L1_attn_W_x_T"].rearrange("(c p) n -> p c n", p=P)).then_inc(w_in, 16)
            nc.scalar.dma_start(w_dt[:, :], g.dram["L1_attn_W_dt_T"].to_broadcast([P, DI])).then_inc(w_in, 16)
            nc.scalar.dma_start(b_dt[:, :], g.dram["L1_attn_b_dt"].rearrange("(a n) -> a n", a=1).to_broadcast([P, DI])).then_inc(w_in, 16)
            nc.scalar.dma_start(cb3[:, :], g.dram["L1_attn_conv_b"].rearrange("(a n) -> a n", a=1).to_broadcast([3, DI])).then_inc(w_in, 16)
            nc.scalar.dma_start(a[:, :], g.dram["L1_attn_A_log"].rearrange("(a n) -> a n", a=1).to_broadcast([P, NS])).then_inc(w_in, 16)
            nc.scalar.dma_start(rowmask[:, :], g.dram["c_rowmask"]).then_inc(w_in, 16)
            norm_coefficients(nc, g, act, None, ln_step, lnw)
            pipeline(act, step, 2, 2, TAPS)
            act.wait_ge(abs_sb, T)
            act.wait_ge(a_step, 1)
            nc.scalar.activation(a[:, :], a[:, :], ACT.Exp).then_inc(a_step, 1)
            for half in range(2):
                quarters = range(half * LN_Q // 2, (half + 1) * LN_Q // 2)
                for q in quarters:
                    s = slice(q * LT, (q + 1) * LT)
                    nc.scalar.activation(soft[:, s, :], soft[:, s, :], ACT.Exp, scale=-1.0).then_inc(exp_sb, 1)
                for q in quarters:
                    s = slice(q * LT, (q + 1) * LT)
                    act.wait_ge(exp_sb, q + 1)
                    nc.scalar.activation(soft[:, s, :], soft[:, s, :], ACT.Ln, bias=1.0).then_inc(ln_sb, 1)

        @block.gpsimd
        def _(pool):
            def keep(t, p):
                pool.wait_ge(u_sb, t + 1)
                pool.sem_inc(waited_pool, 1)
                nc.gpsimd.tensor_copy(uz[:, t, :], u[p][:, :]).then_inc(uz_sb, 1)

            with pool.Fori(0, T // 2) as i:
                keep(i * 2, 0)
                keep(i * 2 + 1, 1)
            pool.wait_ge(uz_sb, T)

        @block.vector
        def _(dve):
            vec = nc.vector

            def step(t, p):
                if inside(t + 3):
                    wait(dve, xT_psum, t + 2)
                    vec.tensor_scalar(xn[(p + 1) % 2][:, :], g.x[:, t + 3, :], g.rstd[:, bass.ds(t + 3, 1)],
                                      g.shift[:, bass.ds(t + 3, 1)], ALU.mult, ALU.add).then_inc(xn_ready, 1)
                if inside(t):
                    dve.wait_ge(uT_psum, t + 1)
                    vec.tensor_copy(uT[p % 2][:, :], u_ps[:, 0:DI]).then_inc(uT_sb, 1)
                if inside(t - 1):
                    dve.wait_ge(xd_psum, t)
                    vec.tensor_copy(xd[:, t - 1, :], d_ps[:, 0:XW]).then_inc(xd_sb, 1)
                    dve.wait_ge(xd_sb, t)
                    vec.scalar_tensor_tensor(dt[:, t - 1, :], w_dt[:, :], xd[:, t - 1, 0:1], b_dt[:, :],
                                             ALU.mult, ALU.add).then_inc(dt_sb, 1)

            arrived_stats(nc, g, dve, x_in, stats)
            norm_coefficients(nc, g, None, dve, ln_step, lnw)
            vec.memset(ones[:, :], 1.0).then_inc(prep, 1)
            vec.memset(cb[:, :], 0.0).then_inc(prep, 1)
            dve.wait_ge(w_in, 16 * W_LOADS)
            for k in range(TAPS):
                vec.tensor_tensor(w_c[:, k, :], w_in_T[:, 0:DI], taps[:, k, :], ALU.mult).then_inc(prep, 1)
            vec.tensor_scalar(a[:, :], a[:, :], 5.0, None, ALU.min).then_inc(a_step, 1)
            dve.wait_ge(prep, 2)
            split_row(vec, dve, prep, TAPS + 2, cb3[:, :], rowmask, (c_hi[:, :], c_rest[:, :], c_f[:, :]), cb[0:3, :])
            pipeline(dve, step, 3, 1, TAPS)
            for q in range(LN_Q):
                s = slice(q * LT, (q + 1) * LT)
                dve.wait_ge(ln_sb, q + 1)
                vec.scalar_tensor_tensor(dt[:, s, :], dt[:, s, :], 0.0, soft[:, s, :], ALU.max, ALU.add).then_inc(soft_sb, 1)
                dve.wait_ge(soft_sb, q + 1)
                vec.tensor_scalar(dt[:, s, :], dt[:, s, :], 1e-4, 10.0, ALU.max, ALU.min).then_inc(clip_sb, 1)
            dve.wait_ge(a_step, 2)
            vec.tensor_scalar(a[:, :], a[:, :], -1.0, None, ALU.mult).then_inc(a_step, 1)
            dve.wait_ge(clip_sb, LN_Q)


def scan_states(nc, g, uz, dt, xd, a):
    with ExitStack() as ctx:
        sem = sem_maker(nc, g, "ss")
        sb, ps = tensor_makers(nc, ctx, "ss")
        dtu = [sb(f"dtu{p}", [P, DI]) for p in range(2)]
        decay = [sb(f"decay{q}", [P, NH, DI]) for q in range(NQ)]
        come = [[sb(f"come{q}{p}", [P, NH, DI]) for p in range(2)] for q in range(NQ)]
        h = [sb(f"h{q}", [P, NH, DI]) for q in range(NQ)]
        diag = [sb(f"diag{q}", [P, NH, P]) for q in range(NQ)]
        y_ps = [ps(f"y_ps{p}", [P, BANK]) for p in range(2)]

        dtu_sb, raw_sb, come_sb, diag_sb = (sem(n) for n in ("dtu_sb", "raw_sb", "come_sb", "diag_sb"))
        decay_sb, kept_sb, h_sb, y_psum, y_sb = (sem(n) for n in ("decay_sb", "kept_sb", "h_sb", "y_psum", "y_sb"))
        sum_sb, last_sum_sb = sem("sum_sb"), sem("last_sum_sb")
        waited_act = sem("waited_act")
        block = ctx.enter_context(nc.Block())

        @block.gpsimd
        def _(pool):
            def dt_u(t, p):
                if not (isinstance(t, int) and t < 2):
                    pool.wait_ge(raw_sb, (t - 1) * NQP)
                    pool.wait_ge(come_sb, (t - 1) * NQ)
                nc.gpsimd.tensor_tensor(dtu[p][:, :], dt[:, t, :], uz[:, t, 0:DI], ALU.mult).then_inc(dtu_sb, 1)

            def add(t, p, q):
                n = t * NQ + q
                pool.wait_ge(kept_sb, n - NQ + 1)
                pool.wait_ge(come_sb, n + 1)
                nc.gpsimd.tensor_tensor(come[q][p][:, :, :], come[q][p][:, :, :], decay[q][:, :, :], ALU.add).then_inc(sum_sb, 1)

            def diagonals(t, q):
                c = xd[:, t, 1 + NS + q * NH:1 + NS + (q + 1) * NH]
                wait(pool, y_psum, t * NQ + q - NQ + 1)
                nc.gpsimd.tensor_tensor(diag[q][:, :, :], g.ident[:, :].unsqueeze(1).to_broadcast([P, NH, P]),
                                        c.unsqueeze(2).to_broadcast([P, NH, P]), ALU.mult).then_inc(diag_sb, 1)

            def position(t, p, adds=True, more=True):
                for q in range(NQ):
                    if q < NQP and adds:
                        add(t, p, q)
                    diagonals(t, q)
                    if q == 1 and more:
                        dt_u(t + 2, p)

            dt_u(0, 0)
            dt_u(1, 1)
            position(0, 0, adds=False)
            position(1, 1)
            with pool.Fori(1, T // 2 - 1) as i:
                position(i * 2, 0)
                position(i * 2 + 1, 1)
            position(T - 2, 0, more=False)
            position(T - 1, 1, more=False)

        @block.scalar
        def _(act):
            def decays(t, q):
                if not (isinstance(t, int) and t == 1):
                    if q < NQP:
                        act.wait_ge(sum_sb, (t - 2) * NQP + q + 1)
                    else:
                        act.wait_ge(last_sum_sb, t - 1)
                    act.sem_inc(waited_act, 1)
                for m in range(NH):
                    s = q * NH + m
                    ins = nc.scalar.activation(decay[q][:, m, :], dt[:, t, :], ACT.Exp, scale=a[:, s:s + 1])
                ins.then_inc(decay_sb, 1)

            def raw(t, p, q):
                act.wait_ge(dtu_sb, t + 1)
                if not (isinstance(t, int) and t < 2):
                    act.wait_ge(h_sb, (t - 2) * NQ + q + 1)
                act.sem_inc(waited_act, 1)
                for m in range(NH):
                    s = 1 + q * NH + m
                    ins = nc.scalar.activation(come[q][p][:, m, :], dtu[p][:, :], ACT.Copy, scale=xd[:, t, s:s + 1])
                ins.then_inc(raw_sb, 1)

            def keep_y(t, p):
                act.wait_ge(y_psum, t * NQ + NQ)
                act.sem_inc(waited_act, 1)
                nc.scalar.activation(dt[:, t, :], y_ps[p][:, 0:DI], ACT.Copy).then_inc(y_sb, 1)

            def position(t, p, keep=True, more=True):
                for q in range(NQ):
                    decays(t, q)
                    if q < NQP and more:
                        raw(t + 1, 1 - p, q)
                    if q == NQ - 1 and keep:
                        keep_y(t - 2, p)

            for q in range(NQP):
                raw(0, 0, q)
            for q in range(NQP):
                raw(1, 1, q)
            position(1, 1, keep=False)
            with act.Fori(1, T // 2 - 1) as i:
                position(i * 2, 0)
                position(i * 2 + 1, 1)
            position(T - 2, 0)
            position(T - 1, 1, more=False)
            keep_y(T - 2, 0)
            keep_y(T - 1, 1)

        @block.vector
        def _(dve):
            vec = nc.vector

            def bound(t, p, q):
                c = come[q][p]
                if q < NQP:
                    dve.wait_ge(raw_sb, t * NQP + q + 1)
                    vec.tensor_scalar(c[:, :, :], c[:, :, :], 10.0, -10.0, ALU.min, ALU.max).then_inc(come_sb, 1)
                    return
                dve.wait_ge(dtu_sb, t + 1)
                if not (isinstance(t, int) and t < 2):
                    dve.wait_ge(h_sb, (t - 2) * NQ + q + 1)
                for m in range(NH):
                    s = 1 + q * NH + m
                    ins = vec.tensor_scalar(c[:, m, :], dtu[p][:, :], xd[:, t, s:s + 1], 10.0, ALU.mult, ALU.min)
                ins.then_inc(come_sb, 1)

            def kept(t, q):
                n = t * NQ + q
                dve.wait_ge(decay_sb, n - NQ + 1)
                dve.wait_ge(h_sb, n - NQ + 1)
                vec.scalar_tensor_tensor(decay[q][:, :, :], decay[q][:, :, :], TINY, h[q][:, :, :],
                                         ALU.max, ALU.mult).then_inc(kept_sb, 1)

            def add_last(t, p):
                q = NQ - 1
                dve.wait_ge(come_sb, t * NQ + q + 1)
                dve.wait_ge(kept_sb, t * NQ + q - NQ + 1)
                vec.scalar_tensor_tensor(come[q][p][:, :, :], come[q][p][:, :, :], -10.0, decay[q][:, :, :],
                                         ALU.max, ALU.add).then_inc(last_sum_sb, 1)

            def clip(t, p, q):
                if q < NQP:
                    dve.wait_ge(sum_sb, (t - 1) * NQP + q + 1)
                else:
                    dve.wait_ge(last_sum_sb, t)
                dve.wait_ge(y_psum, t * NQ + q - NQ + 1)
                vec.tensor_scalar(h[q][:, :, :], come[q][p][:, :, :], 100.0, -100.0, ALU.min, ALU.max).then_inc(h_sb, 1)

            def position(t, p, first=False, more=True):
                for q in range(NQ):
                    if q < 2:
                        bound(t, p, q + 2)
                    elif more:
                        bound(t + 1, 1 - p, q - 2)
                    kept(t, q)
                    if q == 0 and not first:
                        add_last(t - 1, 1 - p)
                    if q >= 2:
                        clip(t, p, q - 2)
                    elif not first:
                        clip(t - 1, 1 - p, q + 2)

            for q in range(NQ):
                bound(0, 0, q)
            for q in range(NQ):
                dve.wait_ge(come_sb, q + 1)
                vec.tensor_scalar(h[q][:, :, :], come[q][0][:, :, :], -10.0, 100.0, ALU.max, ALU.min).then_inc(h_sb, 1)
            bound(1, 1, 0)
            bound(1, 1, 1)
            position(1, 1, first=True)
            position(2, 0)
            with dve.Fori(1, T // 2 - 1) as i:
                position(i * 2 + 1, 1)
                position(i * 2 + 2, 0)
            position(T - 1, 1, more=False)
            clip(T - 1, 1, NQ - 2)
            add_last(T - 1, 1)
            clip(T - 1, 1, NQ - 1)

        @block.tensor
        def _(pe):
            def unit(t, p, q):
                pe.wait_ge(h_sb, t * NQ + q + 1)
                pe.wait_ge(diag_sb, t * NQ + q + 1)
                if q == 0:
                    wait(pe, y_sb, t - 1)
                for m in range(NH):
                    ins = nc.tensor.matmul(y_ps[p][:, 0:DI], diag[q][:, m, :], h[q][:, m, :],
                                           start=(q == 0 and m == 0), stop=(q == NQ - 1 and m == NH - 1))
                ins.then_inc(y_psum, 1)

            for t in range(2):
                for q in range(NQ):
                    unit(t, t, q)
            with pe.Fori(1, T // 2) as i:
                for p in range(2):
                    for q in range(NQ):
                        unit(i * 2 + p, p, q)


def scan_output(nc, g, uz, y):
    NGS = T // LN_Q
    with ExitStack() as ctx:
        sem = sem_maker(nc, g, "so")
        sb, ps = tensor_makers(nc, ctx, "so")
        ln_g, ln_b, d_p = sb("ln_g", [P, DI]), sb("ln_b", [P, DI]), sb("d_p", [P, DI])
        w_o = sb("w_o", [P, DB, D])
        lnw = sb("lnw", [P, 4, T])
        skip = [sb(f"skip{p}", [P, LN_Q, DI]) for p in range(2)]
        v = [sb(f"v{p}", [P, LN_Q, DI]) for p in range(2)]
        vT = [sb(f"vT{p}", [P, 2, BANK]) for p in range(2)]
        t_ps = ps("t_ps", [P, 2, BANK])
        o_ps = ps("o_ps", [P, BANK])
        w_in, stats, ln_step = sem("w_in"), sem("stats"), sem("ln_step")
        du_sb, skip_sb, yn_sb, mul_sb, add_sb, v_sb = (sem(n) for n in ("du_sb", "skip_sb", "yn_sb", "mul_sb", "add_sb", "v_sb"))
        vT_psum, vT_sb, o_psum, x_sb, moments = (sem(n) for n in ("vT_psum", "vT_sb", "o_psum", "x_sb", "moments"))
        block = ctx.enter_context(nc.Block())
        W_LOADS = 4

        def every(row):
            return row[:, :].unsqueeze(1).to_broadcast([P, LN_Q, DI])

        @block.sync
        def _(sp):
            for dst, name in ((ln_g, "ln_g"), (ln_b, "ln_b"), (d_p, "D_param")):
                row = g.dram[f"L1_attn_{name}"].rearrange("(a n) -> a n", a=1)
                sp.dma_start(dst[:, :], row.to_broadcast([P, DI])).then_inc(w_in, 16)
            sp.dma_start(w_o[:, :, :], g.dram["L1_attn_W_out_T"].rearrange("(c p) n -> p c n", p=P)).then_inc(w_in, 16)

        @block.gpsimd
        def _(pool):
            def skips(n, p):
                wait(pool, add_sb, n - 1)
                nc.gpsimd.tensor_tensor(skip[p][:, :, :], uz[:, bass.ds(n * LN_Q, LN_Q), 0:DI], every(d_p), ALU.mult).then_inc(du_sb, 1)
                pool.wait_ge(du_sb, n + 1)
                nc.gpsimd.tensor_tensor(skip[p][:, :, :], skip[p][:, :, :], every(ln_b), ALU.add).then_inc(skip_sb, 1)

            pool.wait_ge(w_in, 16 * W_LOADS)
            skips(0, 0)
            skips(1, 1)
            with pool.Fori(1, NGS // 2) as i:
                skips(i * 2, 0)
                skips(i * 2 + 1, 1)

        @block.vector
        def _(dve):
            vec = nc.vector

            def gated(n, p):
                wait(dve, vT_psum, n - 1)
                for j in range(LN_Q):
                    t = n * LN_Q + j
                    vec.tensor_scalar(v[p][:, j, :], y[:, t, :], g.rstd[:, bass.ds(t, 1)], g.shift[:, bass.ds(t, 1)],
                                      ALU.mult, ALU.add).then_inc(yn_sb, 1)
                dve.wait_ge(yn_sb, n * LN_Q + LN_Q)
                vec.tensor_tensor(v[p][:, :, :], v[p][:, :, :], every(ln_g), ALU.mult).then_inc(mul_sb, 1)
                dve.wait_ge(mul_sb, n + 1)
                dve.wait_ge(skip_sb, n + 1)
                vec.tensor_tensor(v[p][:, :, :], v[p][:, :, :], skip[p][:, :, :], ALU.add).then_inc(add_sb, 1)
                dve.wait_ge(add_sb, n + 1)
                vec.tensor_tensor(v[p][:, :, :], v[p][:, :, :], uz[:, bass.ds(n * LN_Q, LN_Q), DI:2 * DI], ALU.mult)\
                   .then_inc(v_sb, 1)

            def add_out(n):
                dve.wait_ge(o_psum, n + 1)
                xs = g.x[:, bass.ds(n * LN_Q, LN_Q), :]
                vec.tensor_tensor(xs, xs, o_ps[:, :].rearrange("p (k d) -> p k d", k=LN_Q), ALU.add).then_inc(x_sb, 1)
                dve.wait_ge(x_sb, n + 1)
                for j in range(LN_Q):
                    vec.bn_stats(g.bn[:, n * LN_Q + j, :], g.x[:, n * LN_Q + j, :]).then_inc(moments, 1)

            tile_stats(nc, g, dve, y, stats)
            norm_coefficients(nc, g, None, dve, ln_step, lnw, DI)
            dve.wait_ge(w_in, 16 * W_LOADS)
            gated(0, 0)
            gated(1, 1)
            add_out(0)
            with dve.Fori(1, NGS // 2) as i:
                gated(i * 2, 0)
                add_out(i * 2 - 1)
                gated(i * 2 + 1, 1)
                add_out(i * 2)
            add_out(NGS - 1)
            dve.wait_ge(moments, T)

        @block.scalar
        def _(act):
            norm_coefficients(nc, g, act, None, ln_step, lnw, DI)

            def copy(n, p):
                act.wait_ge(vT_psum, n + 1)
                for b in range(2):
                    nc.scalar.activation(vT[p][:, b, :], t_ps[:, b, :], ACT.Copy).then_inc(vT_sb, 1)

            with act.Fori(0, NGS // 2) as i:
                copy(i * 2, 0)
                copy(i * 2 + 1, 1)

        @block.tensor
        def _(pe):
            mm, tr = nc.tensor.matmul, nc.tensor.transpose

            def turn(n, p):
                pe.wait_ge(v_sb, n + 1)
                wait(pe, vT_sb, n * 2)
                for j in range(LN_Q):
                    for c in range(DB):
                        ins = tr(t_ps[:, j // 2, (j % 2 * DB + c) * P:(j % 2 * DB + c + 1) * P],
                                 v[p][:, j, c * P:(c + 1) * P], g.ident[:, :])
                ins.then_inc(vT_psum, 1)

            def project(n, p):
                pe.wait_ge(vT_sb, n * 2 + 2)
                wait(pe, x_sb, n)
                for j in range(LN_Q):
                    for c in range(DB):
                        k = j % 2 * DB + c
                        ins = mm(o_ps[:, j * D:(j + 1) * D], vT[p][:, j // 2, k * P:(k + 1) * P], w_o[:, c, :],
                                 start=(c == 0), stop=(c == DB - 1))
                ins.then_inc(o_psum, 1)

            pe.wait_ge(w_in, 16 * W_LOADS)
            turn(0, 0)
            turn(1, 1)
            project(0, 0)
            with pe.Fori(1, NGS // 2) as i:
                turn(i * 2, 0)
                project(i * 2 - 1, 1)
                turn(i * 2 + 1, 1)
                project(i * 2, 0)
            project(NGS - 1, 1)


ME, MA = 12, 64
NR, TOP1 = 3, 3
MC = 2 * ME


def stage_experts1(nc, g):
    with ExitStack() as ctx:
        sem = sem_maker(nc, g, "e1")
        sb, ps = tensor_makers(nc, ctx, "e1")
        w_a, w_z = sb("w_a", [P, MA]), sb("w_z", [MA, NR * ME])
        w = sb("w", [P, MC, P])
        b2 = sb("b2", [P, D])
        spread = sb("spread", [P, MC, P], BF16)
        lnw = sb("lnw", [P, 4, T])
        xn = sb("xn", [P, GT, D])
        xnT = [sb(f"xnT{p}", [P, TOK]) for p in range(2)]
        xaT = sb("xaT", [MA, TOK])
        rows = GT * NR
        z = sb("z", [P, rows, ME + 8 - TOP1])
        r = {"sorted": sb("sorted", [P, rows, 8]), "taken": sb("taken", [P, rows, 8]),
             "marked": sb("marked", [P, rows, ME + 8 - TOP1]), "sel": sb("sel", [P, rows, ME])[:, :, :]}
        ez, total, weight = sb("ez", [P, rows, ME]), sb("total", [P, rows]), sb("weight", [P, GT, NR, ME])
        part_hi, part_rest = sb("part_hi", [P, GT, 2, ME], BF16), sb("part_rest", [P, GT, 2, ME])
        parts = sb("parts", [P, GT, 2, 64])
        wT = [sb(f"wT{p}", [P, TOK], BF16) for p in range(2)]
        w3T = [sb(f"w3T{p}", [P, TOK]) for p in range(2)]
        scaled = [sb(f"scaled{k}", [P, TOK]) for k in range(3)]
        hT, yT = sb("hT", [P, TOK]), sb("yT", [P, TOK])

        m_ps, n_ps = ps("m_ps", [P, BANK]), ps("n_ps", [P, BANK])
        w_ps = [ps(f"w_ps{k}", [P, BANK]) for k in range(3)]
        h_ps, y_ps, o_ps = ps("h_ps", [P, BANK]), ps("y_ps", [P, BANK]), ps("o_ps", [P, BANK])

        w_in, ln_step, ready = sem("w_in"), sem("ln_step"), sem("ready")
        xn_ready, xT_psum, xT_sb, xa_psum, xa_sb = (sem(n) for n in ("xn_ready", "xT_psum", "xT_sb", "xa_psum", "xa_sb"))
        z_psum, route, exp_sb, waited = (sem(n) for n in ("z_psum", "route", "exp_sb", "waited"))
        wT_psum, wT_sb = sem("wT_psum"), sem("wT_sb")
        w_psum, scaled_sb, product, h_sb, y_sb = (sem(n) for n in ("w_psum", "scaled_sb", "product", "h_sb", "y_sb"))
        b2_done, o_psum, x_sb, x_out = (sem(n) for n in ("b2_done", "o_psum", "x_sb", "x_out"))
        W_LOADS = 6
        TOP_STEPS = 2 * rows + 3
        ROUTE_STEPS = TOP_STEPS + 1 + 4 + 6
        block = ctx.enter_context(nc.Block())

        @block.sync
        def _(sp):
            sp.dma_start(w_a[:, :], g.dram["L1_ffn_P_w_T"]).then_inc(w_in, 16)
            sp.dma_start(w_z[:, :], g.dram["L1_U_T"]).then_inc(w_in, 16)
            sp.dma_start(spread[:, :, :].rearrange("r e n -> r (e n)"), g.dram["c_spread1"]).then_inc(w_in, 16)
            sp.dma_start(w[:, 0:ME, :], g.dram["L1_W1_T"]).then_inc(w_in, 16)
            sp.dma_start(w[:, ME:MC, :], g.dram["L1_W2_T"]).then_inc(w_in, 16)
            sp.wait_ge(ready, 1)
            sp.dma_start(b2[0:ME, :], g.dram["L1_ffn_b2"]).then_inc(w_in, 16)
            with sp.Fori(0, NG) as n:
                sp.wait_ge(x_sb, n + 1)
                sp.dma_start(g.out[:, bass.ds(n * GT, GT), :], g.x[:, bass.ds(n * GT, GT), :]).then_inc(x_out, 16)
            sp.wait_ge(x_out, 16 * NG)

        @block.tensor
        def _(pe):
            mm, tr = nc.tensor.matmul, nc.tensor.transpose

            def turn_x(n):
                pe.wait_ge(xn_ready, n * GT + GT)
                for k in range(GT):
                    ins = tr(m_ps[:, k * P:(k + 1) * P], xn[:, k, :], g.ident[:, :])
                ins.then_inc(xT_psum, 1)

            def address(n, p):
                pe.wait_ge(xT_sb, n + 1)
                mm(m_ps[0:MA, :], w_a[:, :], xnT[p][:, :], start=True, stop=True).then_inc(xa_psum, 1)

            def rank(n):
                pe.wait_ge(xa_sb, n + 1)
                for k in range(GT):
                    ins = mm(m_ps[:, k * NR * ME:(k + 1) * NR * ME], xaT[:, k * P:(k + 1) * P], w_z[:, :], start=True, stop=True)
                ins.then_inc(z_psum, 1)

            def turn_weights(n):
                pe.wait_ge(route, n * ROUTE_STEPS + ROUTE_STEPS)
                for k in range(GT):
                    tr(m_ps[:, k * P:(k + 1) * P], parts[:, k, :, :], g.ident[:, :])
                for k in range(GT):
                    ins = tr(n_ps[0:ME, k * P:(k + 1) * P], weight[:, k, 2, :], g.ident[:, :])
                ins.then_inc(wT_psum, 1)

            def spread_weight(n, p, j):
                if j == 0:
                    pe.wait_ge(wT_sb, n * 2 + 2)
                wait(pe, scaled_sb, n * MC + j - 2)
                mm(w_ps[j % 3][:, :], spread[:, j, :], wT[p][:, :], start=True, stop=True)\
                  .then_inc(w_psum, 1)

            def expert(n, j):
                pe.wait_ge(scaled_sb, n * MC + j + 1)
                if j == 0:
                    wait(pe, h_sb, n)
                mm([h_ps, y_ps][j // ME][:, :], w[:, j, :], scaled[j % 3][:, :], start=(j == 0),
                   stop=(j == ME - 1 or j == MC - 1)).then_inc(product, 1)

            def bias(n, p):
                wait(pe, y_sb, n)
                mm(y_ps[:, :], b2[:, :], w3T[p][:, :], start=True, stop=False).then_inc(b2_done, 1)

            def turn_out(n):
                pe.wait_ge(y_sb, n + 1)
                wait(pe, x_sb, n)
                for k in range(GT):
                    ins = tr(o_ps[:, k * P:(k + 1) * P], yT[:, k * P:(k + 1) * P], g.ident[:, :])
                ins.then_inc(o_psum, 1)

            def group(n, p, prev, nxt):
                for j in range(MC):
                    spread_weight(n, p, j)
                    if j >= 2:
                        expert(n, j - 2)
                    elif prev:
                        expert(n - 1, MC - 2 + j)
                    if j == ME + 1:
                        bias(n, p)
                        if prev:
                            turn_out(n - 1)
                    if nxt and j == 3:
                        turn_x(n + 1)
                    if nxt and j == 5:
                        address(n + 1, 1 - p)
                    if nxt and j == 7:
                        rank(n + 1)
                    if nxt and j == 20:
                        turn_weights(n + 1)

            pe.wait_ge(w_in, 16 * W_LOADS)
            turn_x(0)
            address(0, 0)
            rank(0)
            turn_weights(0)
            group(0, 0, False, True)
            with pe.Fori(0, NG // 2 - 1) as i:
                group(i * 2 + 1, 1, True, True)
                group(i * 2 + 2, 0, True, True)
            group(NG - 1, 1, True, False)
            expert(NG - 1, MC - 2)
            expert(NG - 1, MC - 1)
            turn_out(NG - 1)

        @block.scalar
        def _(act):
            def copy_address(n):
                act.wait_ge(xa_psum, n + 1)
                nc.scalar.activation(xaT[:, :], m_ps[0:MA, :], ACT.Copy).then_inc(xa_sb, 1)

            def exps(n):
                act.wait_ge(route, n * ROUTE_STEPS + TOP_STEPS + 1)
                nc.scalar.activation(ez[:, :, :], ez[:, :, :], ACT.Exp).then_inc(exp_sb, 1)

            def group(n, p, prev, nxt):
                if prev:
                    act.wait_ge(product, n * MC)
                    nc.scalar.activation(yT[:, :], y_ps[:, :], ACT.Copy).then_inc(y_sb, 1)
                if nxt:
                    copy_address(n + 1)
                act.wait_ge(product, n * MC + ME)
                nc.scalar.activation(hT[:, :], h_ps[:, :], ACT.Gelu).then_inc(h_sb, 1)
                if nxt:
                    exps(n + 1)

            norm_coefficients(nc, g, act, None, ln_step, lnw)
            copy_address(0)
            exps(0)
            group(0, 0, False, True)
            with act.Fori(1, NG - 1) as n:
                group(n, 0, True, True)
            group(NG - 1, 1, True, False)
            act.wait_ge(product, NG * MC)
            nc.scalar.activation(yT[:, :], y_ps[:, :], ACT.Copy).then_inc(y_sb, 1)

        @block.vector
        def _(dve):
            vec = nc.vector

            def norm(n):
                for k in range(GT):
                    t = n * GT + k
                    vec.tensor_scalar(xn[:, k, :], g.x[:, t, :], g.rstd[:, bass.ds(t, 1)], g.shift[:, bass.ds(t, 1)],
                                      ALU.mult, ALU.add).then_inc(xn_ready, 1)

            def copy_xT(n, p):
                dve.wait_ge(xT_psum, n + 1)
                vec.tensor_copy(xnT[p][:, :], m_ps[:, :]).then_inc(xT_sb, 1)

            def runner(n, start):
                done = [start]

                def run(ins, last=True):
                    ins.then_inc(route, 1)
                    done[0] += 1
                    if last:
                        dve.wait_ge(route, n * ROUTE_STEPS + done[0])
                return run, done

            half = rows // 2
            flat = weight[:, :, :, :].rearrange("p k r e -> p (k r) e")

            def alone():
                dve.sem_inc(waited, 1)

            def lists(n, k):
                run, done = runner(n, 0 if k == 0 else 1 + half)
                if k == 0:
                    dve.wait_ge(z_psum, n + 1)
                    run(vec.tensor_copy(z[:, :, 0:ME], m_ps[:, 0:rows * ME].rearrange("p (k e) -> p k e", k=rows)))
                top_lists(vec, run, alone, z[:, :, :], range(k * half, k * half + half), ME, r)

            def marks(n, k):
                run, done = runner(n, 1 + rows if k == 0 else 2 + rows + half)
                if k == 0:
                    run(vec.tensor_copy(r["taken"][:, :, 0:TOP1], r["sorted"][:, :, 0:TOP1]))
                mark_top(vec, run, alone, z[:, :, :], range(k * half, k * half + half), r)

            def exponents(n):
                run, done = runner(n, 2 + 2 * rows)
                run(vec.tensor_tensor(r["sel"], z[:, :, 0:ME], r["marked"][:, :, 0:ME], ALU.not_equal))
                assert done[0] == TOP_STEPS
                run(vec.tensor_tensor(ez[:, :, :], z[:, :, 0:ME], r["sorted"][:, :, 0:1].to_broadcast([P, rows, ME]),
                                      ALU.subtract), last=False)

            def totals(n):
                run, done = runner(n, TOP_STEPS + 1)
                dve.wait_ge(exp_sb, n + 1)
                run(vec.tensor_tensor(flat, r["sel"], ez[:, :, :], ALU.mult))
                run(vec.tensor_reduce(total[:, :], flat, AX.X, ALU.add))

            def weights(n):
                run, done = runner(n, TOP_STEPS + 3)
                run(vec.reciprocal(total[:, :], total[:, :]))
                run(vec.tensor_tensor(flat, flat, total[:, :].unsqueeze(2).to_broadcast([P, rows, ME]), ALU.mult))

            def split(n):
                run, done = runner(n, TOP_STEPS + 5)
                split_three(vec, run, weight[:, :, 0:2, :], [parts[:, :, :, j * ME:(j + 1) * ME] for j in range(3)],
                            part_hi[:, :, :, :], part_rest[:, :, :, :])
                assert done[0] == ROUTE_STEPS

            def routing(n):
                for k in range(2):
                    lists(n, k)
                for k in range(2):
                    marks(n, k)
                exponents(n)
                totals(n)
                weights(n)
                split(n)

            def copy_weights(n, p, k):
                dve.wait_ge(wT_psum, n + 1)
                if k == 0:
                    vec.tensor_copy(wT[p][:, :], m_ps[:, :]).then_inc(wT_sb, 1)
                else:
                    vec.tensor_copy(w3T[p][0:ME, :], n_ps[0:ME, :]).then_inc(wT_sb, 1)

            def scale(n, p, j):
                dve.wait_ge(w_psum, n * MC + j + 1)
                if j == ME:
                    dve.wait_ge(h_sb, n + 1)
                wait(dve, product, n * MC + j - 2)
                src = xnT[p] if j < ME else hT
                vec.tensor_tensor(scaled[j % 3][:, :], src[:, :], w_ps[j % 3][:, :], ALU.mult).then_inc(scaled_sb, 1)

            def add_out(n):
                dve.wait_ge(o_psum, n + 1)
                xs = g.x[:, bass.ds(n * GT, GT), :]
                vec.tensor_tensor(xs, xs, o_ps[:, :].rearrange("p (k d) -> p k d", k=GT), ALU.add).then_inc(x_sb, 1)

            def group(n, p, prev, nxt):
                for j in range(MC):
                    if prev and j == ME:
                        add_out(n - 1)
                    scale(n, p, j)
                    if nxt:
                        if j == 1:
                            norm(n + 1)
                        if j == 3:
                            copy_xT(n + 1, 1 - p)
                        if j in (8, 9):
                            lists(n + 1, j - 8)
                        if j in (10, 11):
                            marks(n + 1, j - 10)
                        if j == 12:
                            exponents(n + 1)
                        if j == 15:
                            totals(n + 1)
                        if j == 16:
                            weights(n + 1)
                        if j == 17:
                            split(n + 1)
                        if j in (20, 21):
                            copy_weights(n + 1, 1 - p, j - 20)

            for rows128 in (b2, w3T[0], w3T[1]):
                vec.memset(rows128[:, :], 0.0).then_inc(ready, 1)
            vec.memset(z[:, :, ME:], PAD).then_inc(ready, 1)
            vec.memset(r["taken"][:, :, TOP1:], PAD).then_inc(ready, 1)
            vec.memset(parts[:, :, :, :], 0.0).then_inc(ready, 1)
            norm_coefficients(nc, g, None, dve, ln_step, lnw)
            dve.wait_ge(ready, 6)
            norm(0)
            copy_xT(0, 0)
            routing(0)
            copy_weights(0, 0, 0)
            copy_weights(0, 0, 1)
            group(0, 0, False, True)
            with dve.Fori(0, NG // 2 - 1) as i:
                group(i * 2 + 1, 1, True, True)
                group(i * 2 + 2, 0, True, True)
            group(NG - 1, 1, True, False)
            add_out(NG - 1)


STAGES = [stage_cross0, stage_mixer0, stage_experts0, stage_cross1, stage_scan1, stage_experts1]
HALFWAY = stage_scan1


def build(nc, dram, out):
    with ExitStack() as ctx:
        g = Ctx()
        g.dram = dram
        g.out = out
        g.sems = []
        g.x_mid = nc.dram_tensor("x_mid", (NB, S, D), F32).ap()
        sb = tensor_makers(nc, ctx, "all")[0]
        g.x = sb("x", [P, T, D])
        g.bn = sb("bn", [P, T, 6])
        g.rstd = sb("rstd", [P, T])
        g.shift = sb("shift", [P, T])
        g.ident = sb("ident", [P, P])
        for stage in STAGES:
            if stage is HALFWAY:
                clear_semaphores(nc, g)
            stage(nc, g)


PLAIN = ["L0_xattn_bq", "L0_xattn_bk", "L0_xattn_bv", "L0_xattn_bo", "L0_attn_u_w", "L0_attn_u_b", "L0_attn_v_w",
         "L0_attn_v_b", "L0_attn_o_w", "L0_attn_o_b", "L0_attn_pos_w", "L0_attn_pos_b", "L0_attn_lw0", "L0_attn_lw1",
         "L0_attn_lw2", "L0_attn_out_w", "L0_attn_out_b", "L1_xattn_Wk", "L1_xattn_bq", "L1_xattn_bk", "L1_attn_conv_b",
         "L1_attn_b_dt", "L1_attn_A_log", "L1_attn_D_param", "L1_attn_ln_g", "L1_attn_ln_b", "L1_ffn_b2"]
TURNED = ["L0_xattn_Wq", "L0_xattn_Wk", "L0_xattn_Wv", "L0_xattn_Wo", "L0_ffn_gate_weight", "L1_xattn_Wq", "L1_attn_W_in",
          "L1_attn_W_x", "L1_attn_W_dt", "L1_attn_W_out", "L1_ffn_P_w"]


def shape_constants():
    p = np.arange(P)
    r = np.arange(BT * CH)
    tail = np.zeros((BT * CH, 2, CH), np.float32)
    tail[r, 0, r // CH] = 1.0
    tail[r, 1, r % CH] = 1.0
    k, n = np.arange(S)[:, None], np.arange(S)[None, :]
    angle = np.pi * k * n / S
    re, im = np.cos(angle), -np.sin(angle)
    even = (-1.0) ** np.arange(S)

    def three(a, b, c, slot_b):
        m = np.stack([a, b, c])
        m[0, 0], m[1, 0], m[2, 0] = re[0] * (0.5 if slot_b < 0 else 1.0), even * abs(slot_b), 0.0
        return m

    sums = three(re + im, im, re, 1.0)
    mults = three(re, re + im, im - re, 1.0) * GAMMA ** np.arange(S)
    backs = three(re + im, -re, im, -0.5) / S
    eye = np.eye(BT)
    bfloat16 = np.dtype("bfloat16")
    spread0, spread1 = np.zeros((P, RC * P)), np.zeros((P, MC * P))
    spread0[0:3 * NE] = np.tile(np.repeat(np.eye(NE), EI, axis=1), (3, 1))
    for n in range(2):
        spread1[64 * n:64 * n + 3 * ME, n * ME * P:(n + 1) * ME * P] = np.tile(np.repeat(np.eye(ME), P, axis=1), (3, 1))
    return {
        "c_dft": np.einsum("ab,mkn->anmbk", eye, sums).reshape(P, 3, P).astype(np.float32),
        "c_idft": np.einsum("ab,mkn->akmbn", eye, backs).reshape(P, 3, P).astype(np.float32),
        "c_cdft": np.tile(mults.transpose(2, 0, 1)[:, :, None, :], (1, 1, BT, 1)).reshape(S, 3, P).astype(np.float32),
        "c_pos": np.arange(S, dtype=np.float32)[None, :],
        "c_spread0": spread0.astype(bfloat16),
        "c_spread1": spread1.astype(bfloat16),
        "c_rowmask": np.eye(3, dtype=np.float32),
        "c_ident": np.eye(P, dtype=np.float32),
        "c_headmask": (p[:, None] // XD % CH == np.arange(CH)).astype(np.float32),
        "c_headmask16": (p[:, None] // XD == np.arange(XH)).astype(np.float32),
        "c_tailmask": tail,
        "c_onehot": (p[:, None] % S == p % S).astype(bfloat16),
    }


def kernel(**inputs):
    import concourse.bacc as bacc
    from concourse.bass_utils import run_bass_kernel_spmd

    nc = bacc.Bacc("TRN2", target_bir_lowering=False, num_devices=1)
    a = {k: np.asarray(v) for k, v in inputs.items()}
    arrays = {"x": a["x"], "mask": a["mask_1x1xSxS2_ik0"][0, 0], "ctx": a["ctx_1024"],
              "ctxT": np.transpose(a["ctx_1024"], (0, 2, 1))}
    for k in PLAIN:
        arrays[k] = a[k]
    for k in TURNED:
        arrays[k + "_T"] = a[k].T
    arrays["c_lb"] = np.concatenate([a[f"L0_attn_lb{n}"] for n in range(3)])[None, :]
    rows = {"gate": ("w_gate", "ws_gate"), "up": ("w_up", "ws_up")}
    for k, (routed, shared) in rows.items():
        arrays[f"L0_{k}_T"] = np.concatenate([a[f"L0_ffn_{routed}"].reshape(NE * EI, D), a[f"L0_ffn_{shared}"]]).T
    arrays["L0_down_T"] = np.concatenate([np.transpose(a["L0_ffn_w_down"], (0, 2, 1)).reshape(NE * EI, D),
                                          a["L0_ffn_ws_down"].T])
    arrays["L1_conv_T"] = a["L1_attn_conv_w"][:, 0, :].T.reshape(1, TAPS * DI)
    arrays["L1_U_T"] = np.concatenate([a[f"L1_ffn_U{n + 1}"] for n in range(NR)]).T
    for n in (1, 2):
        arrays[f"L1_W{n}_T"] = np.transpose(a[f"L1_ffn_W{n}"], (2, 0, 1))
    arrays.update(shape_constants())
    arrays = {k: np.ascontiguousarray(v) for k, v in arrays.items()}
    dram = {k: nc.dram_tensor(k, v.shape, mybir.dt.from_np(v.dtype), kind="ExternalInput").ap()
            for k, v in arrays.items()}
    out = nc.dram_tensor("out", (NB, S, D), F32, kind="ExternalOutput").ap()
    build(nc, dram, out)
    return run_bass_kernel_spmd(nc, [arrays], core_ids=[0]).results[0]["out"]
```
